# Optimizing a Trainium2 kernel written in Bass

```python
import numpy as np
import jax
import jax.numpy as jnp

def _softmax(x, axis=-1):
    return jax.nn.softmax(x, axis=axis)

def _gelu(x):
    return jax.nn.gelu(x, approximate=True)

def _silu(x):
    return jax.nn.silu(x)

def _sigmoid(x):
    return jax.nn.sigmoid(x)

def _layernorm(x, axis=-1, eps=1e-05):
    m = jnp.mean(x, axis=axis, keepdims=True)
    v = jnp.var(x, axis=axis, keepdims=True)
    return (x - m) / jnp.sqrt(v + eps)

def _scatter_add(tgt, idx, src, axis=0):
    return tgt.at[idx].add(src)

def _segment_sum(src, seg, n):
    return jax.ops.segment_sum(src, seg, n)
kernel_name = 'mk_gnn_resnorm_d2_gnn_r8_5178b4'

def setup_inputs(seed: int=0):
    np.random.seed(seed)
    _w = jnp.asarray

    def _rec_inputs():
        import jax
        import jax.numpy as jnp
        _gk = jax.random.key(seed)
        x = -0.000364 + 1 * jax.random.normal(jax.random.fold_in(_gk, 1), (1250, 768), jnp.float32)
        _s = jax.random.randint(jax.random.fold_in(_gk, 2), (10000,), 0, 1250, jnp.int32)
        _d = jax.random.randint(jax.random.fold_in(_gk, 3), (10000,), 0, 1250, jnp.int32)
        _loop = jnp.arange(1250, dtype=jnp.int32)
        src = jnp.concatenate([_s, _d, _loop])
        dst = jnp.concatenate([_d, _s, _loop])
        _o = jnp.argsort(dst, stable=True)
        src = src[_o]
        dst = dst[_o]
        return (x, src, dst)
    x, src, dst = _rec_inputs()

    def _L0_gnn_setup():
        import jax, jax.numpy as jnp
        import numpy as np
        N = 2500
        DEG = 16
        E = N * DEG
        H = 12
        DIN = 64
        DOUT = 64
        NEG_SLOPE = 0.2
        key = jax.random.key(seed)
        k_h, k_src, k_w, k_al, k_ar, k_wr = jax.random.split(key, 6)
        std = 1.414 * np.sqrt(2.0 / (DIN + DOUT))
        h = jax.random.normal(k_h, (N, H * DIN), dtype=jnp.float32)
        src = jax.random.randint(k_src, (E,), 0, N, dtype=jnp.int64)
        dst = jnp.repeat(jnp.arange(N, dtype=jnp.int64), DEG)
        W = jax.random.normal(k_w, (DOUT, DIN), dtype=jnp.float32) * std
        attn_l = jax.random.normal(k_al, (1, H, DOUT), dtype=jnp.float32) * std
        attn_r = jax.random.normal(k_ar, (1, H, DOUT), dtype=jnp.float32) * std
        W_res = jax.random.normal(k_wr, (DOUT, DIN), dtype=jnp.float32) * std
        return {'h': h, 'src': src, 'dst': dst, 'W': W, 'attn_l': attn_l, 'attn_r': attn_r, 'W_res': W_res}
    _L0_gnn_all = _L0_gnn_setup()
    _L0_gnn_in = {k: v for k, v in _L0_gnn_all.items() if k in ('W', 'attn_l', 'attn_r', 'W_res')}
    del _L0_gnn_all

    def _L1_gnn_setup():
        import jax, jax.numpy as jnp
        import numpy as np
        N_NODES = 2500
        N_EDGES = 20000
        IN_DIM = 768
        HID = 256
        HEADS = 4
        OUT_DIM = 768
        LN_EPS = 1e-05

        def _add_self_loops(edge_index, n):
            loop = jnp.arange(n, dtype=edge_index.dtype)
            return jnp.concatenate([edge_index, jnp.stack([loop, loop])], axis=1)

        def gat_conv(x, edge_index, W, a_src, a_dst, bias, heads, out_ch, concat):
            n = x.shape[0]
            ei = _add_self_loops(edge_index, n)
            src, dst = (ei[0], ei[1])
            xl = (x @ W).reshape(n, heads, out_ch)
            alpha_src = jnp.einsum('nhc,hc->nh', xl, a_src)
            alpha_dst = jnp.einsum('nhc,hc->nh', xl, a_dst)
            e = jax.nn.leaky_relu(alpha_src[src] + alpha_dst[dst], 0.2)
            m = jax.ops.segment_max(e, dst, num_segments=n)
            e = jnp.exp(e - m[dst])
            s = jax.ops.segment_sum(e, dst, num_segments=n)
            alpha = e / (s[dst] + 1e-16)
            msg = xl[src] * alpha[:, :, None]
            out = jax.ops.segment_sum(msg, dst, num_segments=n)
            out = out.reshape(n, heads * out_ch) if concat else out.mean(axis=1)
            return out + bias

        def layer_norm(x, g, b):
            mu = jnp.mean(x, axis=-1, keepdims=True)
            var = jnp.var(x, axis=-1, keepdims=True)
            return (x - mu) * jax.lax.rsqrt(var + LN_EPS) * g + b
        key = jax.random.key(seed)
        ks = jax.random.split(key, 16)
        s = 0.02
        HC = HID * HEADS
        return {'x': jax.random.normal(ks[0], (N_NODES, IN_DIM), jnp.float32), 'edge_index': jax.random.randint(ks[1], (2, N_EDGES), 0, N_NODES, jnp.int64 if jax.config.jax_enable_x64 else jnp.int32), 'W1': jax.random.normal(ks[2], (IN_DIM, HC), jnp.float32) * s, 'a_src1': jax.random.normal(ks[3], (HEADS, HID), jnp.float32) * s, 'a_dst1': jax.random.normal(ks[4], (HEADS, HID), jnp.float32) * s, 'b1': jnp.zeros((HC,), jnp.float32), 'g1': jnp.ones((HC,), jnp.float32), 'be1': jnp.zeros((HC,), jnp.float32), 'Wr1': jax.random.normal(ks[5], (IN_DIM, HC), jnp.float32) * s, 'br1': jnp.zeros((HC,), jnp.float32), 'W2': jax.random.normal(ks[6], (HC, OUT_DIM), jnp.float32) * s, 'a_src2': jax.random.normal(ks[7], (1, OUT_DIM), jnp.float32) * s, 'a_dst2': jax.random.normal(ks[8], (1, OUT_DIM), jnp.float32) * s, 'b2': jnp.zeros((OUT_DIM,), jnp.float32), 'g2': jnp.ones((OUT_DIM,), jnp.float32), 'be2': jnp.zeros((OUT_DIM,), jnp.float32), 'Wr2': jax.random.normal(ks[9], (HC, OUT_DIM), jnp.float32) * s, 'br2': jnp.zeros((OUT_DIM,), jnp.float32)}
    _L1_gnn_all = _L1_gnn_setup()
    _L1_gnn_in = {k: v for k, v in _L1_gnn_all.items() if k in ('W1', 'a_src1', 'a_dst1', 'b1', 'g1', 'be1', 'Wr1', 'br1', 'W2', 'a_src2', 'a_dst2', 'b2', 'g2', 'be2', 'Wr2', 'br2')}
    del _L1_gnn_all
    return {'x': x, 'src': src, 'dst': dst, 'L0_gnn_W': _L0_gnn_in['W'], 'L0_gnn_attn_l': _L0_gnn_in['attn_l'], 'L0_gnn_attn_r': _L0_gnn_in['attn_r'], 'L0_gnn_W_res': _L0_gnn_in['W_res'], 'L1_gnn_W1': _L1_gnn_in['W1'], 'L1_gnn_a_src1': _L1_gnn_in['a_src1'], 'L1_gnn_a_dst1': _L1_gnn_in['a_dst1'], 'L1_gnn_b1': _L1_gnn_in['b1'], 'L1_gnn_g1': _L1_gnn_in['g1'], 'L1_gnn_be1': _L1_gnn_in['be1'], 'L1_gnn_Wr1': _L1_gnn_in['Wr1'], 'L1_gnn_br1': _L1_gnn_in['br1'], 'L1_gnn_W2': _L1_gnn_in['W2'], 'L1_gnn_a_src2': _L1_gnn_in['a_src2'], 'L1_gnn_a_dst2': _L1_gnn_in['a_dst2'], 'L1_gnn_b2': _L1_gnn_in['b2'], 'L1_gnn_g2': _L1_gnn_in['g2'], 'L1_gnn_be2': _L1_gnn_in['be2'], 'L1_gnn_Wr2': _L1_gnn_in['Wr2'], 'L1_gnn_br2': _L1_gnn_in['br2']}

def reference(x, src, dst, L0_gnn_W, L0_gnn_attn_l, L0_gnn_attn_r, L0_gnn_W_res, L1_gnn_W1, L1_gnn_a_src1, L1_gnn_a_dst1, L1_gnn_b1, L1_gnn_g1, L1_gnn_be1, L1_gnn_Wr1, L1_gnn_br1, L1_gnn_W2, L1_gnn_a_src2, L1_gnn_a_dst2, L1_gnn_b2, L1_gnn_g2, L1_gnn_be2, L1_gnn_Wr2, L1_gnn_br2):
    import jax
    import jax.numpy as jnp

    def _L0_gnn_ref(h, src, dst, W, attn_l, attn_r, W_res):
        import jax, jax.numpy as jnp
        import numpy as np
        N = 2500
        DEG = 16
        E = N * DEG
        H = 12
        DIN = 64
        DOUT = 64
        NEG_SLOPE = 0.2
        n = h.shape[0]
        hv = h.reshape(n, H, DIN)
        ft = jnp.einsum('nhd,od->nho', hv, W)
        a1 = jnp.sum(ft * attn_l, axis=-1)
        a2 = jnp.sum(ft * attn_r, axis=-1)
        e = jax.nn.leaky_relu(a1[src] + a2[dst], negative_slope=NEG_SLOPE)
        m = jax.ops.segment_max(e, dst, num_segments=n)
        m = jnp.where(jnp.isfinite(m), m, 0.0)
        w = jnp.exp(e - m[dst])
        denom = jax.ops.segment_sum(w, dst, num_segments=n)
        alpha = w / jnp.maximum(denom[dst], 1e-16)
        msg = alpha[:, :, None] * ft[src]
        agg = jax.ops.segment_sum(msg, dst, num_segments=n)
        res = jnp.einsum('nhd,od->nho', hv, W_res)
        out = jax.nn.relu((agg + res).reshape(n, H * DOUT))
        return out

    def _L1_gnn_ref(x, edge_index, W1, a_src1, a_dst1, b1, g1, be1, Wr1, br1, W2, a_src2, a_dst2, b2, g2, be2, Wr2, br2):
        import jax, jax.numpy as jnp
        import numpy as np
        N_NODES = 2500
        N_EDGES = 20000
        IN_DIM = 768
        HID = 256
        HEADS = 4
        OUT_DIM = 768
        LN_EPS = 1e-05

        def _add_self_loops(edge_index, n):
            loop = jnp.arange(n, dtype=edge_index.dtype)
            return jnp.concatenate([edge_index, jnp.stack([loop, loop])], axis=1)

        def gat_conv(x, edge_index, W, a_src, a_dst, bias, heads, out_ch, concat):
            n = x.shape[0]
            ei = _add_self_loops(edge_index, n)
            src, dst = (ei[0], ei[1])
            xl = (x @ W).reshape(n, heads, out_ch)
            alpha_src = jnp.einsum('nhc,hc->nh', xl, a_src)
            alpha_dst = jnp.einsum('nhc,hc->nh', xl, a_dst)
            e = jax.nn.leaky_relu(alpha_src[src] + alpha_dst[dst], 0.2)
            m = jax.ops.segment_max(e, dst, num_segments=n)
            e = jnp.exp(e - m[dst])
            s = jax.ops.segment_sum(e, dst, num_segments=n)
            alpha = e / (s[dst] + 1e-16)
            msg = xl[src] * alpha[:, :, None]
            out = jax.ops.segment_sum(msg, dst, num_segments=n)
            out = out.reshape(n, heads * out_ch) if concat else out.mean(axis=1)
            return out + bias

        def layer_norm(x, g, b):
            mu = jnp.mean(x, axis=-1, keepdims=True)
            var = jnp.var(x, axis=-1, keepdims=True)
            return (x - mu) * jax.lax.rsqrt(var + LN_EPS) * g + b
        h0 = x
        h = gat_conv(x, edge_index, W1, a_src1, a_dst1, b1, HEADS, HID, True)
        h = layer_norm(h, g1, be1)
        h = jax.nn.relu(h)
        h = h + (h0 @ Wr1 + br1)
        h1 = h
        h = gat_conv(h, edge_index, W2, a_src2, a_dst2, b2, 1, OUT_DIM, False)
        h = layer_norm(h, g2, be2)
        h = h + (h1 @ Wr2 + br2)
        return h
    edge_index = jnp.stack([src, dst])
    x = _layernorm(x + _L0_gnn_ref(x, src, dst, L0_gnn_W, L0_gnn_attn_l, L0_gnn_attn_r, L0_gnn_W_res), axis=-1)
    x = _layernorm(x + _L1_gnn_ref(x, edge_index, L1_gnn_W1, L1_gnn_a_src1, L1_gnn_a_dst1, L1_gnn_b1, L1_gnn_g1, L1_gnn_be1, L1_gnn_Wr1, L1_gnn_br1, L1_gnn_W2, L1_gnn_a_src2, L1_gnn_a_dst2, L1_gnn_b2, L1_gnn_g2, L1_gnn_be2, L1_gnn_Wr2, L1_gnn_br2), axis=-1)
    return x

_drawn_inputs = setup_inputs


def setup_inputs(seed=0):
    import zlib

    import numpy as np

    out = dict(_drawn_inputs(seed))
    spreads = {'L1_gnn_b1': (0.0, 0.1),
     'L1_gnn_g1': (1.0, 0.2),
     'L1_gnn_be1': (0.0, 0.1),
     'L1_gnn_br1': (0.0, 0.1),
     'L1_gnn_b2': (0.0, 0.1),
     'L1_gnn_g2': (1.0, 0.2),
     'L1_gnn_be2': (0.0, 0.1),
     'L1_gnn_br2': (0.0, 0.1)}
    factors = {}
    for name, (base, spread) in spreads.items():
        noise = np.random.default_rng([zlib.crc32(name.encode()), seed]).standard_normal(out[name].shape)
        drawn = base * np.exp(spread * noise) if base else spread * noise
        out[name] = jnp.asarray(drawn.astype(out[name].dtype))
    for name, factor in factors.items():
        out[name] = (out[name] * factor).astype(out[name].dtype)
    return out
```

```python
from contextlib import ExitStack

import concourse.bass as bass
from concourse import mybir

F32 = mybir.dt.float32
BF16 = mybir.dt.bfloat16
F16 = mybir.dt.float16
I32 = mybir.dt.int32
ALU = mybir.AluOpType
ACT = mybir.ActivationFunctionType

P = 128
BANK = 512
NO_EDGE = -1.0e30
MAX_FLOOR = -1.0e29
SLOPE = 0.2
LN_EPS = 1e-5
LN_TINY = 2.0 ** -60


class Counter:

    def __init__(self, handle):
        self.handle = handle
        self.value = 0

    def now(self):
        return self, self.value


class Queue:

    def __init__(self):
        self.steps = []
        self.reached = {}

    def after(self, *events):
        for event in events:
            if event is None:
                continue
            counter, value = event
            if self.reached.get(counter, 0) < value:
                self.reached[counter] = value
                self.steps.append(lambda e, c=counter, v=value: e.wait_ge(c.handle, v))
        return self

    def run(self, step, counter=None, by=1):
        if counter is None:
            self.steps.append(step)
            return None
        counter.value += by
        self.steps.append(lambda e: step(e).then_inc(counter.handle, by))
        return counter.now()

    def play(self, engine):
        for step in self.steps:
            step(engine)


def gnn_kernel(nc, x, src, dst, W0, attn_l, attn_r, Wres, W1, a_src1, a_dst1, b1, g1, be1, Wr1, br1,
               W2, a_src2, a_dst2, b2, g2, be2, Wr2, br2, out):
    N, D = x.shape
    E = src.shape[0]
    C0 = W0.shape[0]
    H0 = D // C0
    H1, C1 = a_src1.shape
    HC = H1 * C1
    NT = (N + P - 1) // P
    KT = D // P
    KH = HC // P
    EP = 125
    ET = E // EP
    assert EP * ET == E and ET % 2 == 0 and 2 * C0 == P and HC == 2 * BANK
    rows = [min(P, N - i * P) for i in range(NT)]
    pieces = [(c, min(BANK, N - c)) for c in range(0, N, BANK)]
    units = [range(0, 4), range(4, 7), range(7, 10)]
    RING = 8

    x1_dram = nc.dram_tensor("x1_spill", (N, D), F32, kind="Internal").ap()
    base_dram = nc.dram_tensor("base_spill", (N, D), F32, kind="Internal").ap()

    with ExitStack() as ctx:
        def sbuf(name, free, dt=F32, parts=P):
            return ctx.enter_context(nc.sbuf_tensor(name, [parts] + list(free), dt))

        def counter(name):
            return Counter(ctx.enter_context(nc.semaphore(name)))

        LC = sbuf("LC", [NT, N])
        R1 = sbuf("R1", [10240])
        R2 = sbuf("R2", [10240])
        R3 = sbuf("R3", [2 * NT * D])
        rowbuf = sbuf("rowbuf", [2, N])
        colbuf = sbuf("colbuf", [3, BANK])
        ident = sbuf("ident", [P])
        off_diag = sbuf("off_diag", [P])
        att = sbuf("att", [NT, 2 * H0])
        diag_count = sbuf("diag_count", [NT])
        diag_ln = sbuf("diag_ln", [NT])
        row_max = sbuf("row_max", [RING])
        stats = sbuf("stats", [2, 12])
        moments = sbuf("moments", [NT, 2])
        rstd = sbuf("rstd", [NT])
        minus_half = sbuf("minus_half", [1])
        tiny = sbuf("tiny", [1])
        recip = sbuf("recip", [8])

        banks = [ctx.enter_context(nc.psum_tensor(f"bank{b}", [P, BANK], F32)) for b in range(8)]
        turn_banks, misc_banks, acc_banks = banks[0:2], banks[2:4], banks[4:8]

        def view(region, start, shape, dt=F32, parts=P):
            n = 1
            for s in shape:
                n *= s
            words = n if dt == F32 or dt == I32 else n // 2
            ap = region[0:parts, start:start + words]
            if dt != F32:
                ap = ap.bitcast(dt)
            if len(shape) == 2:
                ap = ap.rearrange("p (a b) -> p a b", a=shape[0])
            if len(shape) == 3:
                ap = ap.rearrange("p (a b c) -> p a b c", a=shape[0], b=shape[1])
            return ap

        src_i = view(R1, 0, [ET], I32, EP)
        dst_i = view(R1, ET, [ET], I32, EP)
        src_f = view(R1, 2 * ET, [ET], F32, EP)
        dst_f = view(R1, 3 * ET, [ET], F32, EP)
        iota_i = view(R1, 4 * ET, [N], I32)
        iota_h = view(R1, 4 * ET + N, [N], F16)
        NW = N // 2
        hot_src = [view(R1, 4 * ET + N + NW * (1 + b), [N], BF16, EP) for b in range(2)]
        at = 4 * ET + N + NW * 3
        hot_dst = [view(R1, at + P * b, [2 * P], BF16, EP) for b in range(2)]
        zeros = view(R1, at + 2 * P, [BANK], BF16, EP)
        x_in = view(R2, 0, [NT, D])
        xT = view(R3, 0, [KT, N])
        ft = view(R2, 0, [NT, H0, C0 + 1])
        acc0 = view(R3, NT * D, [NT, D])
        W0_twice = view(R2, NT * D, [2, C0], F32, C0)
        Wres_twice = view(R2, NT * D + P, [2, C0], F32, C0)
        attn_in = view(R2, NT * D + 2 * P, [C0], F32, 2 * H0)
        attnT = view(R2, NT * D + 3 * P, [2 * H0], F32, C0)
        ring = view(R1, 0, [RING, N])
        x0 = view(R3, 0, [NT, D])
        aggT = [view(R3, b * BANK, [BANK], F32, C0 + 1) for b in range(2)]

        q = {n: Queue() for n in ("sync", "pe", "act", "dve", "pool")}
        sync, pe, act, dve, pool = (q[n] for n in ("sync", "pe", "act", "dve", "pool"))

        def load(name, dst_ap, src_ap, *waits):
            c = counter("dma_" + name)
            sync.after(*waits)
            return sync.run(lambda e: e.dma_start(dst_ap, src_ap), c, 16)

        def rows_in(name, tile_ap, dram, *waits):
            full = (NT - 1) * P
            a = load(name + "_full", tile_ap[:, 0:NT - 1, :],
                     dram[0:full, :].rearrange("(t p) d -> p t d", p=P), *waits)
            b = load(name + "_last", tile_ap[0:rows[-1], NT - 1, :], dram[full:N, :])
            return a, b

        def spread(vec, parts=P):
            return vec.partition_broadcast(parts)

        ev_dst = load("dst", dst_i, dst.rearrange("(p t) -> p t", p=EP))
        ev_src = load("src", src_i, src.rearrange("(p t) -> p t", p=EP))
        ev_w = [load("w0a", W0_twice[:, 0, :], W0), load("w0b", W0_twice[:, 1, :], W0),
                load("wra", Wres_twice[:, 0, :], Wres), load("wrb", Wres_twice[:, 1, :], Wres),
                load("al", attn_in[0:H0, :], attn_l[0]), load("ar", attn_in[H0:2 * H0, :], attn_r[0])]
        ev_x = rows_in("x", x_in, x)

        c_const = counter("const")
        c_pool = counter("pool_done")
        pool.run(lambda e: e.iota(iota_i, [[1, N]], base=0, channel_multiplier=0), c_const)
        pool.run(lambda e: e.memset(ident[:, :], 0.0), c_const)
        pool.run(lambda e: e.memset(off_diag[:, :], 1.0), c_const)
        ev = pool.run(lambda e: e.memset(zeros, 0.0), c_const)
        pool.after(ev)
        pool.run(lambda e: e.affine_select(out=ident[:, :], in_=ident[:, :], compare_op=ALU.not_equal, fill=1.0,
                                           base=0, pattern=[[-1, P]], channel_multiplier=1), c_const)
        pool.run(lambda e: e.affine_select(out=off_diag[:, :], in_=off_diag[:, :], compare_op=ALU.not_equal,
                                           fill=0.0, base=0, pattern=[[-1, P]], channel_multiplier=1), c_const)
        pool.run(lambda e: e.memset(minus_half[:, :], -0.5), c_const)
        pool.run(lambda e: e.memset(att[:, :, :], 0.0), c_const)
        pool.run(lambda e: e.memset(row_max[:, :], 0.0), c_const)
        ev_const = pool.run(lambda e: e.memset(tiny[:, :], LN_TINY), c_const)

        c_dve = counter("dve_done")
        c_act = counter("act_done")
        c_pe = counter("pe_done")
        c_hot = counter("hot_ready")
        c_hot_free = counter("hot_free")
        dve.after(ev_const, ev_src, ev_dst)
        dve.run(lambda e: e.tensor_copy(iota_h, iota_i))
        dve.run(lambda e: e.tensor_copy(src_f, src_i))
        ev = dve.run(lambda e: e.tensor_copy(dst_f, dst_i), c_dve)
        dve.after(ev)

        side_free = {3: None, 7: None}
        side = [0]

        def side_bank():
            side[0] ^= 1
            return (3, 7)[side[0]]

        rhs = view(rowbuf[:, :, :].rearrange("p a b -> p (a b)"), 0, [KT, 2 * P + 4])
        pe.after(ev_const, *ev_w)
        b_w = side_bank()
        pe.run(lambda e: e.transpose(banks[b_w][0:C0, 0:2 * H0], attn_in, ident[0:2 * H0, 0:2 * H0]))
        pe.run(lambda e: e.transpose(banks[b_w][:, P:P + C0], W0_twice.rearrange("p a b -> p (a b)"), ident[0:C0, 0:C0]))
        ev = pe.run(lambda e: e.transpose(banks[b_w][:, 2 * P:2 * P + C0], Wres_twice.rearrange("p a b -> p (a b)"),
                                          ident[0:C0, 0:C0]), c_pe)
        c_rhs0 = counter("rhs0_zero")
        ev_zero = pool.run(lambda e: e.memset(rhs[:, :, :], 0.0), c_rhs0)
        act.after(ev, ev_zero)
        ev_at = act.run(lambda e: e.copy(attnT, banks[b_w][0:C0, 0:2 * H0]), c_act)
        for k in range(KT):
            for half in range(2):
                ps = slice(half * C0, half * C0 + C0)
                act.run(lambda e, k=k, ps=ps: e.copy(rhs[ps, k, ps.start:ps.stop], banks[b_w][ps, P:P + C0]))
                last = act.run(lambda e, k=k, ps=ps: e.copy(rhs[ps, k, P + ps.start:P + ps.stop],
                                                            banks[b_w][ps, 2 * P:2 * P + C0]), c_act)
        side_free[b_w] = last
        b2_ = side_bank()
        pe.after(ev_at)
        ev = pe.run(lambda e: e.matmul(banks[b2_][:, 0:2 * H0], W0_twice.rearrange("p a b -> p (a b)"), attnT,
                                       start=True, stop=True), c_pe)
        act.after(ev)
        for half in range(2):
            ps = slice(half * C0, half * C0 + C0)
            for side_ in range(2):
                ev_rhs = act.run(lambda e, half=half, ps=ps, s=side_: e.copy(
                    rhs[ps, :, 2 * P + 2 * s + half],
                    banks[b2_][ps, s * H0 + half:(s + 1) * H0:2]), c_act)
        side_free[b2_] = ev_rhs
        pe.after(*ev_x)
        for k in range(KT):
            for c, w in pieces:
                b = side_bank()
                pe.after(side_free[b])
                for i in range(c // P, (c + w + P - 1) // P):
                    ev = pe.run(lambda e, b=b, c=c, i=i, k=k: e.transpose(
                        banks[b][:, i * P - c:i * P - c + rows[i]], x_in[0:rows[i], i, k * P:(k + 1) * P],
                        ident[0:rows[i], 0:rows[i]]), c_pe)
                act.after(ev)
                ev_xT = side_free[b] = act.run(lambda e, b=b, c=c, w=w, k=k: e.copy(xT[:, k, c:c + w],
                                                                                    banks[b][:, 0:w]), c_act)
        pool.after(ev_xT)
        ev_ones = pool.run(lambda e: e.memset(ft, 1.0), counter("ft_ones"))
        pe.after(ev_xT, ev_rhs)
        for i in range(NT):
            m = rows[i]
            for k in range(KT):
                b = side_bank()
                pe.after(side_free[b])
                ev = pe.run(lambda e, b=b, m=m, i=i, k=k: e.matmul(
                    banks[b][0:m, 0:2 * P + 4], xT[:, k, i * P:i * P + m], rhs[:, k, :], start=True, stop=True), c_pe)
                act.after(ev, ev_ones, ev_const)
                act.run(lambda e, b=b, m=m, i=i, k=k: e.copy(
                    ft[0:m, i, 2 * k:2 * k + 2, 0:C0],
                    banks[b][0:m, 0:P].rearrange("p (a b) -> p a b", a=2)))
                act.run(lambda e, b=b, m=m, i=i, k=k: e.copy(acc0[0:m, i, k * P:(k + 1) * P], banks[b][0:m, P:2 * P]))
                ev_ft = side_free[b] = act.run(lambda e, b=b, m=m, i=i, k=k: e.copy(
                    att[0:m, i, :].rearrange("p (s h) -> p s h", s=2)[:, :, 2 * k:2 * k + 2],
                    banks[b][0:m, 2 * P:2 * P + 4].rearrange("p (s h) -> p s h", s=2)), c_act)

        count_banks = [[banks[0], banks[1], banks[2]], [banks[4], banks[5], banks[6]]]
        pe.steps.append(lambda e: e.sem_inc(c_hot_free.handle, 2))
        ev_counts = []
        free = None
        for g in range(NT // 2):
            tiles = (2 * g, 2 * g + 1)
            hot0 = c_hot.value
            c_hot.value += ET
            c_hot_free.value += ET

            def dve_loop(e, g=g, hot0=hot0):
                with e.Fori(0, ET // 2) as r:
                    for buf in range(2):
                        e.wait_ge(c_hot_free.handle, r * 2 + (hot0 + buf + 1))
                        t = r * 2 + buf
                        e.tensor_scalar(hot_src[buf], iota_h[0:EP, :], src_f[:, bass.ds(t, 1)], None, ALU.is_equal)
                        e.tensor_scalar(hot_dst[buf], iota_h[0:EP, 0:2 * P], dst_f[:, bass.ds(t, 1)],
                                        None, ALU.is_equal).then_inc(c_hot.handle, 1)

            def pe_loop(e, g=g, hot0=hot0, tiles=tiles):
                def product(buf, lhs, start, stop):
                    last = None
                    for a, k in enumerate(tiles):
                        for (c, w), bank in zip(pieces, count_banks[a]):
                            l = lhs[:, 0:rows[k]] if lhs is zeros else lhs[:, a * P:a * P + rows[k]]
                            r_ = zeros[:, 0:w] if lhs is zeros else hot_src[buf][:, c:c + w]
                            last = e.matmul(bank[0:rows[k], 0:w], l, r_, start=start, stop=stop)
                    return last
                product(0, zeros, True, False)
                with e.Fori(0, ET // 2) as r:
                    for buf in range(2):
                        e.wait_ge(c_hot.handle, r * 2 + (hot0 + buf + 1))
                        product(buf, hot_dst[buf], False, False).then_inc(c_hot_free.handle, 1)
                product(0, zeros, False, True).then_inc(c_pe.handle, 1)

            dve.steps.append(dve_loop)
            if g + 1 < NT // 2:
                dve.after(c_hot.now())
                ev = dve.run(lambda e: e.tensor_scalar(dst_f, dst_f, float(-2 * P), None, ALU.add), c_dve)
                dve.after(ev)
            pe.after(free)
            pe.steps.append(pe_loop)
            c_pe.value += 1
            act.after(c_pe.now())
            for a, k in enumerate(tiles):
                for (c, w), bank in zip(pieces, count_banks[a]):
                    free = act.run(lambda e, k=k, c=c, w=w, bank=bank: e.copy(
                        LC[0:rows[k], k, c:c + w], bank[0:rows[k], 0:w]), c_act)
            ev_counts += [free, free]
        ev_counting_over = free

        ln_free = [None] * 2
        ln_buf = [view(R1, 7000, [N]), view(R1, 7000 + N, [N])]
        for i in range(NT):
            m = rows[i]
            k = i % 2
            act.after(ev_counts[i], ln_free[k])
            ev_ln = act.run(lambda e, m=m, i=i, k=k: e.activation(ln_buf[k][0:m, :], LC[0:m, i, :], ACT.Ln,
                                                                  bias=tiny[0:m, :]), c_act)
            dve.after(ev_counts[i])
            ev = dve.run(lambda e, m=m, i=i: e.tensor_tensor_reduce(
                colbuf[0:m, 0, 0:m], LC[0:m, i, i * P:i * P + m], ident[0:m, 0:m], 1.0, 0.0, ALU.mult, ALU.add,
                diag_count[0:m, i:i + 1]), c_dve)
            dve.after(ev_ln, ev)
            ev = dve.run(lambda e, m=m, i=i: e.tensor_scalar(LC[0:m, i, :], LC[0:m, i, :], 0.0, NO_EDGE,
                                                             ALU.is_equal, ALU.mult), c_dve)
            dve.after(ev)
            ev_LC = ln_free[k] = dve.run(lambda e, m=m, i=i, k=k: e.tensor_tensor(
                LC[0:m, i, :], LC[0:m, i, :], ln_buf[k][0:m, :], ALU.add), c_dve)

        ring_free = [None] * RING
        ring_at = [0]
        turn_at = [0]
        turn_free = [ev_counting_over] * 2
        col_at = [0]
        acc_free = [ev_counting_over] * 4
        misc_at = [0]
        misc_free = [ev_counting_over] * 2

        def row_of(col, buf, waits, free_ev):
            ev = None
            for c, w in pieces:
                b = misc_at[0] % 2
                misc_at[0] += 1
                pe.after(misc_free[b], *waits)
                for i in range(c // P, (c + w + P - 1) // P):
                    m = rows[i]
                    ev = pe.run(lambda e, b=b, i=i, m=m, c=c: e.matmul(
                        misc_banks[b][:, i * P - c:i * P - c + m], att[0:m, i, col:col + 1].to_broadcast([m, P]),
                        ident[0:m, 0:m], start=True, stop=True), c_pe)
                dve.after(ev, *free_ev)
                misc_free[b] = ev = dve.run(lambda e, b=b, c=c, w=w: e.tensor_copy(rowbuf[:, buf, c:c + w],
                                                                                   misc_banks[b][:, 0:w]), c_dve)
            return ev

        def edge_maximum(i, row_buf, row_ev, slot, junk):
            m = rows[i]
            dve.after(row_ev, junk_written[0])
            junk_written[0] = dve.run(lambda e: e.tensor_tensor_reduce(
                junk[0:m, :], rowbuf[0:m, row_buf, :], LC[0:m, i, :], 1.0, MAX_FLOOR, ALU.add, ALU.max,
                row_max[0:m, slot:slot + 1]), c_dve)

        def unit_maxima(tiles, slot, dst_col, net):
            t = row_max[:, slot:slot + len(tiles)]
            a = att[:, tiles[0]:tiles[-1] + 1, dst_col]
            dve.after(junk_written[0])
            ev = dve.run(lambda e: e.tensor_tensor(t, t, a, ALU.add), c_dve)
            dve.after(ev)
            ev = dve.run(lambda e: e.scalar_tensor_tensor(out=t, in0=t, scalar=SLOPE, in1=t, op0=ALU.mult,
                                                          op1=ALU.max), c_dve)
            dve.after(ev)
            return dve.run(lambda e: e.tensor_tensor(t, t, net.att_slope[:, tiles[0]:tiles[-1] + 1, dst_col],
                                                     ALU.subtract), c_dve)

        def scores(i, row_buf, row_ev, dst_col, slot, max_slot, max_ev, net):
            m = rows[i]
            act.after(row_ev, ring_free[slot])
            ev_r = act.run(lambda e: e.activation(ring[0:m, slot, :], rowbuf[0:m, row_buf, :], ACT.Relu,
                                                  bias=net.att_rest[0:m, i, dst_col:dst_col + 1],
                                                  scale=1.0 - SLOPE), c_act)
            dve.after(ev_r, max_ev)
            ev = dve.run(lambda e: e.scalar_tensor_tensor(
                out=ring[0:m, slot, :], in0=ring[0:m, slot, :], scalar=row_max[0:m, max_slot:max_slot + 1],
                in1=LC[0:m, i, :], op0=ALU.subtract, op1=ALU.add), c_dve)
            return ev_r, ev

        def columns(s, tiles, slots, col_ap, col_free, bias):
            m = rows[s]
            b = turn_at[0] % 2
            turn_at[0] += 1
            pe.after(turn_free[b])
            w = 0
            for (slot, ev_s), i in zip(slots, tiles):
                pe.after(ev_s)
                n = rows[i]
                ev = pe.run(lambda e, slot=slot, n=n, w=w: e.transpose(
                    turn_banks[b][0:m, w:w + n], ring[0:n, slot, s * P:s * P + m], ident[0:n, 0:n]), c_pe)
                w += n
            if s == NT - 1:
                for slot, _ in slots:
                    ring_free[slot] = ev
            act.after(ev, col_free)
            turn_free[b] = act.run(lambda e: e.activation(col_ap[0:m, 0:w], turn_banks[b][0:m, 0:w], ACT.Exp,
                                                          bias=bias), c_act)
            return turn_free[b], w

        class Net:

            def __init__(self, att_slope, att_rest, junk, ring_slots, ready):
                self.att_slope, self.att_rest, self.junk, self.ring_slots = att_slope, att_rest, junk, ring_slots
                self.n = att_slope.shape[2]
                dve.after(*ready)
                self.scaled = None
                self.junk_ready = ready

            def scale_terms(self, ev):
                dve.after(ev)
                dve.run(lambda e: e.tensor_scalar(self.att_slope, att[:, :, 0:self.n], SLOPE, None, ALU.mult), c_dve)
                return dve.run(lambda e: e.tensor_scalar(self.att_rest, att[:, :, 0:self.n], 1.0 - SLOPE, None,
                                                         ALU.mult), c_dve)

        junk_written = [None]
        max_free = [None, None]

        def attention(net, heads, row_col, dst_col, begin_head, use, finish):
            todo = [(h, u) for h in heads for u in range(len(units))]
            made = {}
            row_evs = {}
            row_readers = {}
            for n in range(len(todo) + 1):
                new = todo[n] if n < len(todo) else None
                old = todo[n - 1] if n else None
                plan = []
                if new:
                    h, u = new
                    if u == 0:
                        ready = begin_head(h)
                        row_evs[h] = row_of(row_col(h), h % 2, ready, row_readers.get(h - 2, []))
                        row_readers[h] = []
                    made[new] = []
                    tiles = units[u]
                    half = 4 * (n % 2)
                    state = {}

                    def maximum(j, h=h, tiles=tiles, half=half):
                        if j == 0:
                            dve.after(max_free[half // 4])
                        edge_maximum(tiles[j], h % 2, row_evs[h], half + j, net.junk)
                        row_readers[h].append(junk_written[0])

                    def all_maxima(h=h, tiles=tiles, half=half, state=state):
                        state["ev"] = unit_maxima(tiles, half, dst_col(h), net)

                    def score(j, h=h, tiles=tiles, half=half, state=state, new=new):
                        slot = ring_at[0] % net.ring_slots
                        ring_at[0] += 1
                        ev_r, ev = scores(tiles[j], h % 2, row_evs[h], dst_col(h), slot, half + j, state["ev"], net)
                        made[new].append((slot, ev))
                        row_readers[h].append(ev_r)
                        max_free[half // 4] = ev

                    plan = [lambda j=j: maximum(j) for j in range(len(tiles))] + [all_maxima]
                    plan += [lambda j=j: score(j) for j in range(len(tiles))]
                if not old:
                    for step in plan:
                        step()
                    continue
                for s in range(NT):
                    if s < len(plan):
                        plan[s]()
                    use(old, s, units[old[1]], made[old])
                finish(old, units[old[1]])

        c_fin = counter("network0_units")
        col_free = [None] * 3
        agg_free = [None] * 2
        recip_read = [None]
        acc_of = {}

        def ring_ready(ev):
            for s in range(RING):
                ring_free[s] = ev

        ring_ready(ev_LC)
        dve_last0 = {}

        def use0(unit, s, tiles, slots):
            h, u = unit
            c = col_at[0] % 3
            col_at[0] += 1
            ev, w = columns(s, tiles, slots, colbuf[:, c, :], col_free[c], net0.att_slope[0:rows[s], s, h:h + 1])
            if s == 0:
                acc_of[unit] = len(acc_of) % 2
                pe.after(acc_free[acc_of[unit]])
            b = acc_of[unit]
            m = rows[s]
            pe.after(ev)
            col_free[c] = pe.run(lambda e: e.matmul(acc_banks[b][0:C0 + 1, 0:w], ft[0:m, s, h, :],
                                                    colbuf[0:m, c, 0:w], start=(s == 0), stop=(s == NT - 1)), c_pe)

        def finish0(unit, tiles):
            h, u = unit
            b = acc_of[unit]
            w = sum(rows[i] for i in tiles)
            dve.after(c_pe.now(), agg_free[b])
            ev = dve.run(lambda e: e.tensor_copy(aggT[b][:, 0:w], acc_banks[b][0:C0 + 1, 0:w]), c_dve)
            acc_free[b] = ev
            ob = acc_banks[2 + b]
            pe.after(ev, acc_free[2 + b])
            at = 0
            for j, i in enumerate(tiles):
                n = rows[i]
                ev = pe.run(lambda e, j=j, n=n, at=at: e.transpose(
                    ob[0:n, j * (C0 + 1):(j + 1) * (C0 + 1)], aggT[b][:, at:at + n], ident[0:C0 + 1, 0:C0 + 1]), c_pe)
                at += n
            agg_free[b] = ev
            dve.after(ev)
            k = len(tiles)
            full = k if rows[tiles[-1]] == P else k - 1
            sums = ob[:, C0:C0 + (k - 1) * (C0 + 1) + 1:C0 + 1]
            dve.after(recip_read[0])
            groups = [(0, full, P)] + ([(full, k, rows[tiles[-1]])] if full < k else [])
            for lo, hi, m in groups:
                ev = dve.run(lambda e, lo=lo, hi=hi, m=m: e.tensor_scalar(recip[0:m, lo:hi], sums[0:m, lo:hi],
                                                                          1e-16, None, ALU.max), c_dve)
            dve.after(ev)
            for lo, hi, m in groups:
                ev = dve.run(lambda e, lo=lo, hi=hi, m=m: e.reciprocal(recip[0:m, lo:hi], recip[0:m, lo:hi]), c_dve)
            dve.after(ev)
            for j, i in enumerate(tiles):
                n = rows[i]
                dst_ap = acc0[0:n, i, h * C0:(h + 1) * C0]
                ev = dve.run(lambda e, j=j, n=n, dst_ap=dst_ap: e.scalar_tensor_tensor(
                    out=dst_ap, in0=ob[0:n, j * (C0 + 1):j * (C0 + 1) + C0], scalar=recip[0:n, j:j + 1],
                    in1=dst_ap, op0=ALU.mult, op1=ALU.add), c_dve)
            acc_free[2 + b] = recip_read[0] = ev

        def begin0(h):
            return [ev_ft]

        net0 = Net(view(R3, 2 * BANK, [NT, 2 * H0]), view(R1, RING * N, [NT, 2 * H0]),
                   view(R3, 4 * BANK, [N], BF16), RING, [ev_ft])
        act.after(net0.scale_terms(ev_LC))
        attention(net0, range(H0), lambda h: h, lambda h: H0 + h, begin0, use0, finish0)
        ev_attn0 = c_dve.now()

        ev_x0 = rows_in("x0", x0, x, ev_attn0, c_pe.now())
        dve.after(*ev_x0)
        ev = act.run(lambda e: e.activation(diag_ln[:, 0:NT - 1], diag_count[:, 0:NT - 1], ACT.Ln, bias=1.0), c_act)
        ev = act.run(lambda e: e.activation(diag_ln[0:rows[-1], NT - 1:NT], diag_count[0:rows[-1], NT - 1:NT],
                                            ACT.Ln, bias=1.0), c_act)
        for i in range(NT):
            m = rows[i]
            dve.run(lambda e, m=m, i=i: e.scalar_tensor_tensor(
                out=acc0[0:m, i, :], in0=acc0[0:m, i, :], scalar=0.0, in1=x0[0:m, i, :], op0=ALU.max, op1=ALU.add),
                c_dve)
        ev_sum = c_dve.now()
        dve.after(ev)
        for i in range(NT):
            m = rows[i]
            block = LC[0:m, i, i * P:i * P + m]
            ev = dve.run(lambda e, m=m, b=block: e.tensor_tensor(b, b, off_diag[0:m, 0:m], ALU.mult), c_dve)
            dve.after(ev)
            ev_LC1 = dve.run(lambda e, m=m, i=i, b=block: e.scalar_tensor_tensor(
                out=b, in0=ident[0:m, 0:m], scalar=diag_ln[0:m, i:i + 1], in1=b, op0=ALU.mult, op1=ALU.add), c_dve)

        c_pool_rstd = counter("rstd")

        def norm_stats(i, ap, width, waits=()):
            m = rows[i]
            half = width // 2
            dve.after(*waits)
            dve.run(lambda e: e.bn_stats(stats[0:m, 0, 0:6], ap[:, 0:half]))
            ev = dve.run(lambda e: e.bn_stats(stats[0:m, 0, 6:12], ap[:, half:width]), c_dve)
            dve.after(ev)
            ev = dve.run(lambda e: e.bn_aggr(moments[0:m, i, :], stats[0:m, 0, :]), c_dve)
            dve.after(ev)
            ev = dve.run(lambda e: e.tensor_scalar(rstd[0:m, i:i + 1], moments[0:m, i, 1:2], LN_EPS, None, ALU.add),
                         c_dve)
            pool.after(ev)
            return pool.run(lambda e: e.tensor_tensor(rstd[0:m, i:i + 1], rstd[0:m, i:i + 1], minus_half[0:m, :],
                                                      ALU.pow), c_pool_rstd)

        x1T = view(R3, 0, [KT, N])
        dve.after(ev_sum)
        evs = [norm_stats(i, acc0[0:rows[i], i, :], D) for i in range(NT)]
        ev_x1 = []
        for i in range(NT):
            m = rows[i]
            dve.after(evs[i])
            ev_x1.append(dve.run(lambda e, m=m, i=i: e.tensor_scalar(
                acc0[0:m, i, :], acc0[0:m, i, :], moments[0:m, i, 0:1], rstd[0:m, i:i + 1],
                ALU.subtract, ALU.mult), c_dve))
        full = (NT - 1) * P
        ev_spill = [load("x1_out_full", x1_dram[0:full, :].rearrange("(t p) d -> p t d", p=P), acc0[:, 0:NT - 1, :],
                         ev_x1[-1]),
                    load("x1_out_last", x1_dram[full:N, :], acc0[0:rows[-1], NT - 1, :])]

        def transpose_rows(src_ap, dst_ap, n_k, tile_evs, free_ev):
            last = None
            for c, w in pieces:
                for k in range(n_k):
                    b = turn_at[0] % 2
                    turn_at[0] += 1
                    pe.after(turn_free[b])
                    for i in range(c // P, (c + w + P - 1) // P):
                        pe.after(tile_evs[i])
                        ev = pe.run(lambda e, b=b, c=c, i=i, k=k: e.transpose(
                            turn_banks[b][:, i * P - c:i * P - c + rows[i]],
                            src_ap[0:rows[i], i, k * P:(k + 1) * P], ident[0:rows[i], 0:rows[i]]), c_pe)
                    act.after(ev, free_ev)
                    last = turn_free[b] = act.run(lambda e, b=b, c=c, w=w, k=k: e.copy(
                        dst_ap[:, k, c:c + w], turn_banks[b][:, 0:w]), c_act)
            return last

        ev_x1T = transpose_rows(acc0, x1T, KT, ev_x1, ev_sum)

        XL = NT * (C1 + 1)
        base = NT * D
        xl = [view(R3, base + b * XL, [NT, C1 + 1]) for b in range(2)]
        W1h = view(R3, base + 2 * XL, [KT, C1])
        h_buf = view(R2, 0, [NT, HC])
        vec_at = base + 2 * XL + KT * C1
        a1_b = [view(R3, vec_at + s * C1, [C1]) for s in range(2)]
        b1_b = view(R3, vec_at + 2 * C1, [C1])
        assert vec_at + 3 * C1 + NT * 2 * H1 <= 2 * NT * D
        ring_junk = view(R1, (RING - 1) * N, [N])
        pool.after(*ev_spill, ev_x1T)
        ev_ones1 = pool.run(lambda e: e.memset(view(R3, base, [2 * XL]), 1.0), counter("xl_ones"))
        lin_free = [None, None]
        w1_free = [None]
        xl_free = [None] * 4
        vec_free = [None]
        b1_free = [None]
        ev_b1 = {}
        unit_last = {}

        def begin1(h):
            ev_w1 = load(f"w1_{h}", W1h, W1[:, h * C1:(h + 1) * C1].rearrange("(k p) c -> p k c", p=P),
                         ev_ones1, *ev_spill, ev_x1T, w1_free[0])
            ev_a = [load(f"a1s_{h}", a1_b[0], spread(a_src1[h]), ev_ones1, ev_x1T, *ev_spill, vec_free[0]),
                    load(f"a1d_{h}", a1_b[1], spread(a_dst1[h]))]
            k = h % 2
            for i in range(NT):
                m = rows[i]
                b = misc_at[0] % 2
                misc_at[0] += 1
                pe.after(ev_x1T, ev_w1, misc_free[b])
                for kk in range(KT):
                    ev = pe.run(lambda e, b=b, i=i, m=m, kk=kk: e.matmul(
                        misc_banks[b][0:m, 0:C1], x1T[:, kk, i * P:i * P + m], W1h[:, kk, :],
                        start=(kk == 0), stop=(kk == KT - 1)), c_pe)
                dve.after(ev, xl_free[h - 2] if h >= 2 else None, ev_ones1)
                ev = dve.run(lambda e, b=b, i=i, m=m, k=k: e.tensor_copy(xl[k][0:m, i, 0:C1],
                                                                         misc_banks[b][0:m, 0:C1]), c_dve)
                dve.after(ev, *ev_a)
                for s in range(2):
                    dve.after(ev)
                    ev = dve.run(lambda e, b=b, i=i, m=m, k=k, s=s: e.tensor_tensor_reduce(
                        misc_banks[b][0:m, C1:2 * C1], xl[k][0:m, i, 0:C1], a1_b[s][0:m, :], 1.0, 0.0, ALU.mult, ALU.add,
                        att[0:m, i, 2 * h + s:2 * h + s + 1]), c_dve)
                misc_free[b] = ev
            w1_free[0] = c_pe.now()
            vec_free[0] = ev
            dve.after(ev)
            for part, factor in ((net1.att_slope, SLOPE), (net1.att_rest, 1.0 - SLOPE)):
                ev = dve.run(lambda e, p=part, f=factor: e.tensor_scalar(
                    p[:, :, 2 * h:2 * h + 2], att[:, :, 2 * h:2 * h + 2], f, None, ALU.mult), c_dve)
            act.after(ev)
            return [ev]

        def use1(unit, s, tiles, slots):
            h, u = unit
            c = col_at[0] % 3
            col_at[0] += 1
            ev, w = columns(s, tiles, slots, colbuf[:, c, :], col_free[c],
                             net1.att_slope[0:rows[s], s, 2 * h:2 * h + 1])
            m = rows[s]
            at = 0
            for j, i in enumerate(tiles):
                if s == 0:
                    pe.after(acc_free[j])
                pe.after(ev)
                n = rows[i]
                col_free[c] = pe.run(lambda e, j=j, n=n, at=at: e.matmul(
                    acc_banks[j][0:n, 0:C1 + 1], colbuf[0:m, c, at:at + n], xl[h % 2][0:m, s, :],
                    start=(s == 0), stop=(s == NT - 1)), c_pe)
                at += n
            if s == NT - 1:
                xl_free[h] = col_free[c]

        def finish1(unit, tiles):
            h, u = unit
            if u == 0:
                ev_b1[h] = load(f"b1_{h}", b1_b, spread(b1[h * C1:(h + 1) * C1]), b1_free[0])
            dve.after(c_pe.now(), ev_b1[h], recip_read[0])
            for j, i in enumerate(tiles):
                n = rows[i]
                ev = dve.run(lambda e, j=j, n=n: e.tensor_scalar(recip[0:n, j:j + 1], acc_banks[j][0:n, C1:C1 + 1],
                                                                 1e-16, None, ALU.add), c_dve)
            dve.after(ev)
            for j, i in enumerate(tiles):
                n = rows[i]
                ev = dve.run(lambda e, j=j, n=n: e.reciprocal(recip[0:n, j:j + 1], recip[0:n, j:j + 1]), c_dve)
            dve.after(ev)
            for j, i in enumerate(tiles):
                n = rows[i]
                acc_free[j] = dve.run(lambda e, j=j, n=n, i=i: e.scalar_tensor_tensor(
                    out=h_buf[0:n, i, h * C1:(h + 1) * C1], in0=acc_banks[j][0:n, 0:C1], scalar=recip[0:n, j:j + 1],
                    in1=b1_b[0:n, :], op0=ALU.mult, op1=ALU.add), c_dve)
            b1_free[0] = recip_read[0] = acc_free[len(tiles) - 1]

        dve.after(ev_LC1)
        ring_ready(None)
        net1 = Net(view(R3, vec_at + 3 * C1, [NT, 2 * H1]), view(R1, RING * N, [NT, 2 * H1]),
                   ring_junk, RING - 1, [])
        attention(net1, range(H1), lambda h: 2 * h, lambda h: 2 * h + 1, begin1, use1, finish1)
        ev_attn1 = c_dve.now()
        ev_attn1_pe = c_pe.now()

        Wr1_sb = view(R1, 0, [KT, HC])
        vecs1 = view(R3, base, [4, HC])
        ev_wr1 = load("wr1", Wr1_sb, Wr1.rearrange("(k p) c -> p k c", p=P), ev_attn1_pe, ev_attn1)
        ev_v = [load(f"vec1_{n}", vecs1[:, n, :], spread(v)) for n, v in enumerate((g1, be1, br1))]
        ones_row = view(R3, base + 4 * HC, [P])
        ev_or = pool.after(ev_attn1_pe).run(lambda e: e.memset(ones_row, 1.0), counter("ones_row"))
        evs = [norm_stats(i, h_buf[0:rows[i], i, :], HC) for i in range(NT)]
        ev_h1 = []
        for i in range(NT):
            m = rows[i]
            pair = (i % 2) * 2
            pe.after(ev_wr1, ev_v[2], ev_or, acc_free[pair], acc_free[pair + 1])
            for half in range(2):
                cols = slice(half * BANK, (half + 1) * BANK)
                for k in range(KT):
                    pe.run(lambda e, k=k, m=m, i=i, cols=cols, b=pair + half: e.matmul(
                        acc_banks[b][0:m, :], x1T[:, k, i * P:i * P + m], Wr1_sb[:, k, cols],
                        start=(k == 0), stop=False))
                ev = pe.run(lambda e, m=m, cols=cols, b=pair + half: e.matmul(
                    acc_banks[b][0:m, :], ones_row[0:1, 0:m], vecs1[0:1, 2, cols], start=False, stop=True), c_pe)
            hi = h_buf[0:m, i, :]
            dve.after(evs[i], *ev_v)
            e1 = dve.run(lambda e, m=m, i=i, hi=hi: e.scalar_tensor_tensor(
                out=hi, in0=hi, scalar=moments[0:m, i, 0:1], in1=vecs1[0:m, 0, :], op0=ALU.subtract, op1=ALU.mult),
                c_dve)
            dve.after(e1)
            e1 = dve.run(lambda e, m=m, i=i, hi=hi: e.scalar_tensor_tensor(
                out=hi, in0=hi, scalar=rstd[0:m, i:i + 1], in1=vecs1[0:m, 1, :], op0=ALU.mult, op1=ALU.add), c_dve)
            dve.after(e1, ev)
            for half in range(2):
                cols = slice(half * BANK, (half + 1) * BANK)
                e1 = dve.run(lambda e, m=m, hi=hi, cols=cols, b=pair + half: e.scalar_tensor_tensor(
                    out=hi[:, cols], in0=hi[:, cols], scalar=0.0, in1=acc_banks[b][0:m, :], op0=ALU.max,
                    op1=ALU.add), c_dve)
            acc_free[pair] = acc_free[pair + 1] = e1
            ev_h1.append(e1)
        ev_wr1_done = c_pe.now()

        h1T = view(R3, 0, [KH, N])
        tail = KH * N
        a2_b = [view(R3, tail + s * D, [D]) for s in range(2)]
        stage = [view(R3, tail + (2 + s) * D, [D]) for s in range(2)]
        x1_back = [view(R3, tail + (4 + s) * D, [D]) for s in range(2)]
        br2_row = rowbuf[:, 0, 0:D]
        W2_sb = view(R1, 0, [KH, D])
        xl2 = view(R2, 0, [NT, D + 1])
        ev_w2 = load("w2", W2_sb, W2.rearrange("(k p) c -> p k c", p=P), ev_wr1_done)
        ev_a2 = [load("a2s", a2_b[0], spread(a_src2[0]), ev_h1[-1], ev_wr1_done),
                 load("a2d", a2_b[1], spread(a_dst2[0])), load("br2", br2_row, spread(br2))]
        ev_h1T = transpose_rows(h_buf, h1T, KH, ev_h1, ev_h1[-1])
        assert tail + 6 * D <= 2 * NT * D
        ones2 = rowbuf[:, 0, D:D + P]
        ev_or2 = pool.after(ev_h1[-1], ev_wr1_done).run(lambda e: e.memset(ones2, 1.0), counter("ones_row2"))
        ev_ones2 = pool.after(ev_h1T).run(lambda e: e.memset(xl2, 1.0), counter("xl2_ones"))
        halves = [(0, BANK), (BANK, D - BANK)]
        ev_att2 = None
        for i in range(NT):
            m = rows[i]
            pair = (i % 2) * 2
            pe.after(ev_w2, ev_h1T, acc_free[pair], acc_free[pair + 1])
            for half, (c, w) in enumerate(halves):
                for k in range(KH):
                    ev = pe.run(lambda e, k=k, m=m, i=i, c=c, w=w, b=pair + half: e.matmul(
                        acc_banks[b][0:m, 0:w], h1T[:, k, i * P:i * P + m], W2_sb[:, k, c:c + w],
                        start=(k == 0), stop=(k == KH - 1)), c_pe)
            act.after(ev, ev_ones2)
            for half, (c, w) in enumerate(halves):
                ev = act.run(lambda e, m=m, i=i, c=c, w=w, b=pair + half: e.copy(
                    xl2[0:m, i, c:c + w], acc_banks[b][0:m, 0:w]), c_act)
            acc_free[pair] = acc_free[pair + 1] = ev
            dve.after(ev, *ev_a2)
            for s in range(2):
                dve.after(ev_att2)
                ev_att2 = dve.run(lambda e, i=i, m=m, s=s: e.tensor_tensor_reduce(
                    rowbuf[0:m, 1, 0:D], xl2[0:m, i, 0:D], a2_b[s][0:m, :], 1.0, 0.0, ALU.mult, ALU.add,
                    att[0:m, i, s:s + 1]), c_dve)
        ev_w2_done = c_pe.now()
        Wr2_sb = view(R1, 0, [KH, D])
        ev_wr2 = load("wr2", Wr2_sb, Wr2.rearrange("(k p) c -> p k c", p=P), ev_w2_done)
        x1b_free = [None, None]
        stage_free = [None, None]
        ev_base = []
        for i in range(NT):
            m = rows[i]
            pair = (i % 2) * 2
            s = i % 2
            ev_xb = load(f"x1b_{i}", x1_back[s][0:m, :], x1_dram[i * P:i * P + m, :], *ev_spill, x1b_free[s],
                         ev_h1[-1])
            pe.after(ev_wr2, *ev_a2, ev_or2, acc_free[pair], acc_free[pair + 1])
            for half, (c, w) in enumerate(halves):
                for k in range(KH):
                    pe.run(lambda e, k=k, m=m, i=i, c=c, w=w, b=pair + half: e.matmul(
                        acc_banks[b][0:m, 0:w], h1T[:, k, i * P:i * P + m], Wr2_sb[:, k, c:c + w],
                        start=(k == 0), stop=False))
                ev = pe.run(lambda e, m=m, c=c, w=w, b=pair + half: e.matmul(
                    acc_banks[b][0:m, 0:w], ones2[0:1, 0:m], br2_row[0:1, c:c + w], start=False, stop=True), c_pe)
            dve.after(ev, ev_xb, stage_free[s])
            for half, (c, w) in enumerate(halves):
                ev = dve.run(lambda e, m=m, s=s, c=c, w=w, b=pair + half: e.tensor_tensor(
                    stage[s][0:m, c:c + w], acc_banks[b][0:m, 0:w], x1_back[s][0:m, c:c + w], ALU.add), c_dve)
            acc_free[pair] = acc_free[pair + 1] = ev
            x1b_free[s] = ev
            stage_free[s] = load(f"base_{i}", base_dram[i * P:i * P + m, :], stage[s][0:m, :], ev)
            ev_base.append(stage_free[s])
        ev_wr2_done = c_pe.now()

        cols2 = view(R3, NT * D + 2 * NT, [NT, BANK])
        base_sb = view(R3, 0, [NT, D])
        ev_bl = rows_in("base", base_sb, base_dram, *ev_base, ev_wr2_done)
        vec2_at = NT * (D + 1)
        vecs2 = view(R2, vec2_at, [3, D])
        assert vec2_at + 3 * D <= 10240
        ev_v2 = [load(f"vec2_{n}", vecs2[:, n, :], spread(v), ev_h1T) for n, v in enumerate((b2, g2, be2))]
        for b in range(RING):
            ring_free[b] = ev_wr2_done
        ring_at[0] = 0
        y_bufs = [view_ap for view_ap in (colbuf[:, :, :].rearrange("p a b -> p (a b)")[:, 0:D],
                                          colbuf[:, :, :].rearrange("p a b -> p (a b)")[:, D:2 * D])]
        cols2_free = [None] * NT
        y_free = [col_free[2], col_free[2]]
        c_out = []

        def use2(unit, s, tiles, slots):
            ev, w = columns(s, tiles, slots, cols2[:, s, :], cols2_free[s], net2.att_slope[0:rows[s], s, 0:1])
            col_ready[s] = ev

        col_ready = [None] * NT
        out_n = [0]

        def finish2(unit, tiles):
            at = 0
            for j, i in enumerate(tiles):
                n = rows[i]
                pair = (out_n[0] % 2) * 2
                yb = out_n[0] % 2
                out_n[0] += 1
                pe.after(acc_free[pair], acc_free[pair + 1])
                for s in range(NT):
                    m = rows[s]
                    pe.after(col_ready[s])
                    for half, (c, w) in enumerate([(0, BANK), (BANK, D + 1 - BANK)]):
                        ev = pe.run(lambda e, s=s, m=m, n=n, at=at, c=c, w=w, b=pair + half: e.matmul(
                            acc_banks[b][0:n, 0:w], cols2[0:m, s, at:at + n], xl2[0:m, s, c:c + w],
                            start=(s == 0), stop=(s == NT - 1)), c_pe)
                    cols2_free[s] = ev
                at += n
                y = y_bufs[yb][0:n, :]
                dve.after(ev, y_free[yb], *ev_v2, *ev_bl)
                r = recip[0:n, yb:yb + 1]
                ev = dve.run(lambda e, n=n, r=r, b=pair + 1: e.tensor_scalar(
                    r, acc_banks[b][0:n, D - BANK:D - BANK + 1], 1e-16, None, ALU.add), c_dve)
                dve.after(ev)
                ev = dve.run(lambda e, r=r: e.reciprocal(r, r), c_dve)
                dve.after(ev)
                for half, (c, w) in enumerate(halves):
                    ev = dve.run(lambda e, n=n, r=r, y=y, c=c, w=w, b=pair + half: e.scalar_tensor_tensor(
                        out=y[:, c:c + w], in0=acc_banks[b][0:n, 0:w], scalar=r, in1=vecs2[0:n, 0, c:c + w],
                        op0=ALU.mult, op1=ALU.add), c_dve)
                acc_free[pair] = acc_free[pair + 1] = ev
                ev = norm_stats(i, y, D, [ev])
                dve.after(ev)
                ev = dve.run(lambda e, n=n, i=i, y=y: e.scalar_tensor_tensor(
                    out=y, in0=y, scalar=moments[0:n, i, 0:1], in1=vecs2[0:n, 1, :], op0=ALU.subtract,
                    op1=ALU.mult), c_dve)
                dve.after(ev)
                ev = dve.run(lambda e, n=n, i=i, y=y: e.scalar_tensor_tensor(
                    out=y, in0=y, scalar=rstd[0:n, i:i + 1], in1=vecs2[0:n, 2, :], op0=ALU.mult, op1=ALU.add), c_dve)
                dve.after(ev)
                ev = dve.run(lambda e, n=n, i=i, y=y: e.tensor_tensor(y, y, base_sb[0:n, i, :], ALU.add), c_dve)
                ev = norm_stats(i, y, D, [ev])
                dve.after(ev)
                ev = dve.run(lambda e, n=n, i=i, y=y: e.tensor_scalar(
                    y, y, moments[0:n, i, 0:1], rstd[0:n, i:i + 1], ALU.subtract, ALU.mult), c_dve)
                y_free[yb] = load(f"out_{i}", out[i * P:i * P + n, :], y, ev)
                c_out.append(y_free[yb])

        net2 = Net(view(R3, NT * D, [NT, 2]), view(R1, RING * N, [NT, 2]), ring_junk, RING - 1, [ev_att2])
        dve.after(ev_wr2_done, *ev_base)
        act.after(*ev_base)
        act.after(net2.scale_terms(ev_att2))
        attention(net2, [0], lambda h: 0, lambda h: 1, lambda h: [ev_att2], use2, finish2)
        sync.after(*c_out)

        block = ctx.enter_context(nc.Block())

        @block.sync
        def _(e):
            sync.play(e)

        @block.tensor
        def _(e):
            pe.play(e)

        @block.scalar
        def _(e):
            act.play(e)

        @block.vector
        def _(e):
            dve.play(e)

        @block.gpsimd
        def _(e):
            pool.play(e)


_INS = ['x', 'src', 'dst', 'L0_gnn_W', 'L0_gnn_attn_l', 'L0_gnn_attn_r', 'L0_gnn_W_res', 'L1_gnn_W1',
        'L1_gnn_a_src1', 'L1_gnn_a_dst1', 'L1_gnn_b1', 'L1_gnn_g1', 'L1_gnn_be1', 'L1_gnn_Wr1', 'L1_gnn_br1',
        'L1_gnn_W2', 'L1_gnn_a_src2', 'L1_gnn_a_dst2', 'L1_gnn_b2', 'L1_gnn_g2', 'L1_gnn_be2', 'L1_gnn_Wr2',
        'L1_gnn_br2']


def kernel(**inputs):
    import numpy as _np
    import concourse.bacc as _bacc
    from concourse import mybir as _mybir
    from concourse.bass_utils import run_bass_kernel_spmd as _run

    nc = _bacc.Bacc("TRN2", target_bir_lowering=False, num_devices=1)
    arrays, args = {}, []
    for name in _INS:
        a = _np.ascontiguousarray(inputs[name])
        arrays[f"in_{name}_dram"] = a
        args.append(nc.dram_tensor(f"in_{name}_dram", a.shape, _mybir.dt.from_np(a.dtype), kind="ExternalInput").ap())
    out = nc.dram_tensor("out_dram", inputs['x'].shape, _mybir.dt.float32, kind="ExternalOutput").ap()
    gnn_kernel(nc, *args, out)
    r = _run(nc, [arrays], core_ids=[0])
    return r.results[0]["out_dram"]
```

```python
from contextlib import ExitStack

import concourse.bass as bass
from concourse import mybir

F32 = mybir.dt.float32
BF16 = mybir.dt.bfloat16
F16 = mybir.dt.float16
I32 = mybir.dt.int32
U16 = mybir.dt.uint16
ALU = mybir.AluOpType
ACT = mybir.ActivationFunctionType
AX = mybir.AxisListType.X

P = 128
BANK = 512
NO_EDGE_FACTOR = 1.0e29
MAX_FLOOR = -1.0e29
SLOPE = 0.2
LN_EPS = 1e-5
LN_TINY = 2.0 ** -60


class Counter:

    def __init__(self, handle):
        self.handle = handle
        self.value = 0

    def now(self):
        return self, self.value


class Queue:

    def __init__(self):
        self.steps = []
        self.reached = {}

    def after(self, *events):
        for event in events:
            if event is None:
                continue
            counter, value = event
            if self.reached.get(counter, 0) < value:
                self.reached[counter] = value
                self.steps.append(lambda e, c=counter, v=value: e.wait_ge(c.handle, v))
        return self

    def run(self, step, counter=None, by=1):
        if counter is None:
            self.steps.append(step)
            return None
        counter.value += by
        self.steps.append(lambda e: step(e).then_inc(counter.handle, by))
        return counter.now()

    def play(self, engine):
        for step in self.steps:
            step(engine)


def gnn_kernel(nc, x, src, dst, W0, attn_l, attn_r, Wres, W1, a_src1, a_dst1, b1, g1, be1, Wr1, br1,
               W2, a_src2, a_dst2, b2, g2, be2, Wr2, br2, out):
    N, D = x.shape
    E = src.shape[0]
    C0 = W0.shape[0]
    H0 = D // C0
    H1, C1 = a_src1.shape
    HC = H1 * C1
    NT = (N + P - 1) // P
    KT = D // P
    KH = HC // P
    EP = 125
    ET = E // EP
    assert EP * ET == E and ET % 2 == 0 and 2 * C0 == P and HC == 2 * BANK
    rows = [min(P, N - i * P) for i in range(NT)]
    pieces = [(c, min(BANK, N - c)) for c in range(0, N, BANK)]
    units = [range(0, 4), range(4, 7), range(7, 10)]
    RING = 8
    GT = 5
    GROUPS = ET // GT
    WIN = 64
    assert GROUPS * GT == ET and GROUPS % 2 == 0 and NT % 2 == 0 and (NT // 2) * WIN <= BANK

    x1_dram = nc.dram_tensor("x1_spill", (N, D), F32, kind="Internal").ap()
    base_dram = nc.dram_tensor("base_spill", (N, D), F32, kind="Internal").ap()

    with ExitStack() as ctx:
        def sbuf(name, free, dt=F32, parts=P):
            return ctx.enter_context(nc.sbuf_tensor(name, [parts] + list(free), dt))

        def counter(name):
            return Counter(ctx.enter_context(nc.semaphore(name)))

        LC = sbuf("LC", [NT, N])
        LC2 = LC[:, :, :].rearrange("p a b -> p (a b)")
        R1 = sbuf("R1", [10240])
        R2 = sbuf("R2", [10240])
        R3 = sbuf("R3", [2 * NT * D])
        rowbuf = sbuf("rowbuf", [2, N])
        colbuf = sbuf("colbuf", [3, BANK])
        ident = sbuf("ident", [P])
        off_diag = sbuf("off_diag", [P])
        att = sbuf("att", [NT, 2 * H0])
        diag_count = sbuf("diag_count", [NT])
        diag_ln = sbuf("diag_ln", [NT])
        row_max = sbuf("row_max", [RING])
        stats = sbuf("stats", [2, 12])
        moments = sbuf("moments", [NT, 2])
        rstd = sbuf("rstd", [NT])
        minus_half = sbuf("minus_half", [1])
        tiny = sbuf("tiny", [1])
        recip = sbuf("recip", [8])

        psum = ctx.enter_context(nc.psum_tensor("psum", [P, 8, BANK], F32))
        banks = [psum[:, b, :] for b in range(8)]
        turn_banks, misc_banks, acc_banks = banks[0:2], banks[2:4], banks[4:8]

        def view(region, start, shape, dt=F32, parts=P):
            n = 1
            for s in shape:
                n *= s
            words = n if dt == F32 or dt == I32 else n // 2
            ap = region[0:parts, start:start + words]
            if dt != F32:
                ap = ap.bitcast(dt)
            if len(shape) == 2:
                ap = ap.rearrange("p (a b) -> p a b", a=shape[0])
            if len(shape) == 3:
                ap = ap.rearrange("p (a b c) -> p a b c", a=shape[0], b=shape[1])
            return ap

        CT = view(R1, 0, [NT, N], U16)
        at = NT * N // 2
        turned = [view(R1, at + b * NT * P, [NT, P]) for b in range(2)]
        iota_h = view(R1, at, [N], F16)
        at += N // 2
        hot_full = [view(R1, at + b * (N // 2), [N], BF16, EP) for b in range(2)]
        at += N
        hot_part = [view(R1, at + b * P, [2 * P], BF16, EP) for b in range(2)]
        at += 2 * P
        zeros = view(R1, at, [BANK], BF16, EP)
        at += BANK // 2
        src_f, dst_f, dst_rel = (view(R1, at + k * ET, [ET], F32, EP) for k in range(3))
        at += 3 * ET
        base_all = view(R1, at, [GROUPS], F32, EP)
        base_i = view(R1, at + GROUPS, [GROUPS + 1], I32, 1)
        at += 2 * GROUPS + 1
        base_row = view(R1, at, [2 * GROUPS], F32, 1)
        at += 2 * GROUPS
        group_ends = view(R1, at, [2], F32, GROUPS)
        assert at + 2 <= RING * N and 2 * NT * P + NT * N // 2 <= RING * N
        edge_rows = [(0, P), (P, ET - P)]
        edges_i = [view(LC2, k * EP, [EP], I32) for k in range(4)]
        edges_f = [view(LC2, (4 + k) * EP, [EP], F32) for k in range(4)]
        groups_i = view(LC2, 8 * EP, [GT * EP], I32, GROUPS)
        groups_f = view(LC2, (8 + GT) * EP, [GT * EP], F32, GROUPS)
        iota_i = view(LC2, (8 + 2 * GT) * EP, [N], I32)
        x_in = view(R2, 0, [NT, D])
        xT = view(R3, 0, [KT, N])
        ft = view(R2, 0, [NT, H0, C0 + 1])
        acc0 = view(R3, NT * D, [NT, D])
        W0_twice = view(R2, NT * D, [2, C0], F32, C0)
        Wres_twice = view(R2, NT * D + P, [2, C0], F32, C0)
        attn_in = view(R2, NT * D + 2 * P, [C0], F32, 2 * H0)
        attnT = view(R2, NT * D + 3 * P, [2 * H0], F32, C0)
        ring = view(R1, 0, [RING, N])
        x0 = view(R3, 0, [NT, D])
        aggT = [view(R3, b * BANK, [BANK], F32, C0 + 1) for b in range(2)]

        q = {n: Queue() for n in ("sync", "pe", "act", "dve", "pool")}
        sync, pe, act, dve, pool = (q[n] for n in ("sync", "pe", "act", "dve", "pool"))

        def load(name, dst_ap, src_ap, *waits):
            c = counter("dma_" + name)
            sync.after(*waits)
            return sync.run(lambda e: e.dma_start(dst_ap, src_ap), c, 16)

        def rows_in(name, tile_ap, dram, *waits):
            full = (NT - 1) * P
            a = load(name + "_full", tile_ap[:, 0:NT - 1, :],
                     dram[0:full, :].rearrange("(t p) d -> p t d", p=P), *waits)
            b = load(name + "_last", tile_ap[0:rows[-1], NT - 1, :], dram[full:N, :])
            return a, b

        def spread(vec, parts=P):
            return vec.partition_broadcast(parts)

        ev_edges = []
        for k, ids in enumerate((dst, src)):
            for r, (t0, n) in enumerate(edge_rows):
                ev_edges.append(load(f"edges_{k}_{r}", edges_i[2 * k + r][0:n, :],
                                     ids[t0 * EP:(t0 + n) * EP].rearrange("(t p) -> t p", p=EP)))
        ev_groups = load("dst_groups", groups_i, dst.rearrange("(g e) -> g e", g=GROUPS))
        ev_w = [load("w0a", W0_twice[:, 0, :], W0), load("w0b", W0_twice[:, 1, :], W0),
                load("wra", Wres_twice[:, 0, :], Wres), load("wrb", Wres_twice[:, 1, :], Wres),
                load("al", attn_in[0:H0, :], attn_l[0]), load("ar", attn_in[H0:2 * H0, :], attn_r[0])]
        ev_x = rows_in("x", x_in, x)

        c_const = counter("const")
        c_pool = counter("pool_done")
        pool.run(lambda e: e.iota(iota_i, [[1, N]], base=0, channel_multiplier=0), c_const)
        pool.run(lambda e: e.memset(ident[:, :], 0.0), c_const)
        pool.run(lambda e: e.memset(off_diag[:, :], 1.0), c_const)
        ev = pool.run(lambda e: e.memset(zeros, 0.0), c_const)
        pool.after(ev)
        pool.run(lambda e: e.affine_select(out=ident[:, :], in_=ident[:, :], compare_op=ALU.not_equal, fill=1.0,
                                           base=0, pattern=[[-1, P]], channel_multiplier=1), c_const)
        pool.run(lambda e: e.affine_select(out=off_diag[:, :], in_=off_diag[:, :], compare_op=ALU.not_equal,
                                           fill=0.0, base=0, pattern=[[-1, P]], channel_multiplier=1), c_const)
        pool.run(lambda e: e.memset(minus_half[:, :], -0.5), c_const)
        pool.run(lambda e: e.memset(att[:, :, :], 0.0), c_const)
        pool.run(lambda e: e.memset(row_max[:, :], 0.0), c_const)
        ev_CT0 = pool.run(lambda e: e.memset(R1[:, 0:NT * N // 2], 0.0), counter("counts_zero"))
        ev_const = pool.run(lambda e: e.memset(tiny[:, :], LN_TINY), c_const)

        c_dve = counter("dve_done")
        c_act = counter("act_done")
        c_pe = counter("pe_done")
        dve.after(ev_const, *ev_edges, ev_groups)
        dve.run(lambda e: e.tensor_copy(groups_f, groups_i), c_dve)
        for k in range(4):
            n = edge_rows[k % 2][1]
            ev = dve.run(lambda e, k=k, n=n: e.tensor_copy(edges_f[k][0:n, :], edges_i[k][0:n, :]), c_dve)
        ev_edges_f = ev
        dve.after(ev)
        dve.run(lambda e: e.tensor_copy(iota_h, iota_i), c_dve)
        dve.run(lambda e: e.tensor_reduce(group_ends[:, 0:1], groups_f, AX, ALU.min), c_dve)
        ev = dve.run(lambda e: e.tensor_reduce(group_ends[:, 1:2], groups_f, AX, ALU.max), c_dve)
        dve.after(ev)
        ev = dve.run(lambda e: e.tensor_scalar(group_ends[:, 0:1], group_ends[:, 0:1], float(N - WIN), None, ALU.min),
                     c_dve)
        dve.after(ev)
        ev_ends = dve.run(lambda e: e.tensor_tensor(group_ends[:, 1:2], group_ends[:, 1:2], group_ends[:, 0:1],
                                                    ALU.subtract), c_dve)
        pe.after(ev_const, ev_edges_f)
        for k in range(2):
            for r, (t0, n) in enumerate(edge_rows):
                pe.run(lambda e, k=k, r=r, t0=t0, n=n: e.transpose(
                    banks[k][0:EP, t0:t0 + n], edges_f[2 * k + r][0:n, :], ident[0:n, 0:n]))
        pe.after(ev_ends)
        pe.run(lambda e: e.transpose(banks[2][0:1, 0:GROUPS], group_ends[:, 0:1], ident[0:GROUPS, 0:GROUPS]))
        pe.run(lambda e: e.transpose(banks[2][0:1, P:P + GROUPS], group_ends[:, 1:2], ident[0:GROUPS, 0:GROUPS]))
        ev = pe.run(lambda e: e.matmul(banks[4][0:EP, 0:GROUPS], group_ends[:, 0:1].to_broadcast([GROUPS, EP]),
                                       ident[0:GROUPS, 0:GROUPS], start=True, stop=True), c_pe)
        dve.after(ev)
        dve.run(lambda e: e.tensor_copy(base_i[:, 0:GROUPS], banks[2][0:1, 0:GROUPS]), c_dve)
        ev = dve.run(lambda e: e.tensor_reduce(base_row[:, 0:1], banks[2][0:1, P:P + GROUPS], AX, ALU.max), c_dve)
        dve.after(ev)
        ev_span = dve.run(lambda e: e.tensor_copy(base_i[:, GROUPS:GROUPS + 1], base_row[:, 0:1]), c_dve)
        dve.run(lambda e: e.tensor_copy(dst_f, banks[0][0:EP, 0:ET]), c_dve)
        dve.run(lambda e: e.tensor_copy(src_f, banks[1][0:EP, 0:ET]), c_dve)
        ev = dve.run(lambda e: e.tensor_copy(base_all, banks[4][0:EP, 0:GROUPS]), c_dve)
        dve.after(ev)
        ev_rel = dve.run(lambda e: e.tensor_tensor(
            dst_rel.rearrange("p (g t) -> p g t", t=GT), dst_f.rearrange("p (g t) -> p g t", t=GT),
            base_all.unsqueeze(2).to_broadcast([EP, GROUPS, GT]), ALU.subtract), c_dve)

        c_win_hot, c_win_free = counter("win_hot_ready"), counter("win_hot_free")
        c_win_sum, c_win_added = counter("win_sum_ready"), counter("win_sum_added")
        c_all_hot, c_all_free = counter("all_hot_ready"), counter("all_hot_free")
        c_all_sum, c_all_kept = counter("all_sum_ready"), counter("all_sum_kept")
        c_counted = counter("edges_counted")
        win_sum = [psum[:, 4 * b:4 * b + 2, 0:(NT // 2) * WIN] for b in range(2)]
        all_sum = [[banks[0], banks[1], banks[2]], [banks[4], banks[5], banks[6]]]
        span = {}

        def load_span(e):
            e.wait_ge(c_dve.handle, ev_span[1])
            span[e.engine] = e.value_load(base_i[0:1, GROUPS:GROUPS + 1], min_val=0, max_val=N)

        def windows_dve(e):
            with e.Fori(0, GROUPS // 2) as r:
                for half in range(2):
                    for j in range(GT):
                        t = r * (2 * GT) + (half * GT + j)
                        buf = (half * GT + j) % 2
                        e.wait_ge(c_win_free.handle, t + 1)
                        e.tensor_scalar(hot_full[buf], iota_h[0:EP, :], src_f[:, bass.ds(t, 1)], None, ALU.is_equal)
                        e.tensor_scalar(hot_part[buf][:, 0:WIN], iota_h[0:EP, 0:WIN], dst_rel[:, bass.ds(t, 1)],
                                        None, ALU.is_equal).then_inc(c_win_hot.handle, 1)
                    g = r * 2 + half
                    e.wait_ge(c_win_sum.handle, g + 1)
                    base = e.value_load(base_i[0:1, bass.ds(g, 1)], min_val=0, max_val=N - WIN)
                    window = CT[:, :, bass.ds(base, WIN)].rearrange("p (b i) w -> p b i w", b=2)
                    e.wait_ge(c_win_added.handle, g + 2)
                    e.tensor_tensor(window, window, psum_window(half), ALU.add).then_inc(c_win_added.handle, 1)

        def psum_window(half):
            return psum[:, 4 * half:4 * half + 2, 0:(NT // 2) * WIN].rearrange("p b (i w) -> p b i w", w=WIN)

        def all_dve(e):
            for g in range(NT // 2):
                with e.Fori(0, ET // 2) as r:
                    for buf in range(2):
                        e.wait_ge(c_all_free.handle, r * 2 + (g * ET + buf + 1))
                        t = r * 2 + buf
                        e.tensor_scalar(hot_full[buf], iota_h[0:EP, :], dst_f[:, bass.ds(t, 1)], None, ALU.is_equal)
                        e.tensor_scalar(hot_part[buf], iota_h[0:EP, 0:2 * P], src_f[:, bass.ds(t, 1)],
                                        None, ALU.is_equal).then_inc(c_all_hot.handle, 1)
                e.wait_ge(c_all_sum.handle, g + 1)
                for a in range(2):
                    k = 2 * g + a
                    for (c, w), bank in zip(pieces, all_sum[a]):
                        last = e.tensor_copy(CT[0:rows[k], k, c:c + w], bank[0:rows[k], 0:w])
                last.then_inc(c_all_kept.handle, 1)
                e.wait_ge(c_all_hot.handle, (g + 1) * ET)
                e.tensor_scalar(src_f, src_f, float(-2 * P), None, ALU.add).then_inc(c_all_kept.handle, 1)
                e.wait_ge(c_all_kept.handle, 2 * g + 2)

        def dve_counts(e):
            load_span(e)
            with e.If(span[e.engine] < WIN):
                windows_dve(e)
            with e.Else():
                all_dve(e)

        dve.after(ev_rel, ev_CT0)
        dve.steps.append(dve_counts)
        dve.steps.append(lambda e: e.drain().then_inc(c_counted.handle, 1))
        c_counted.value = 1
        ev_counted = c_counted.now()

        def windows_pe(e, g):
            b = g % 2
            halves_ = [psum[:, 4 * b + k, 0:(NT // 2) * WIN] for k in range(2)]
            e.wait_ge(c_win_added.handle, g + 1)
            for half in halves_:
                e.matmul(half, zeros[:, 0:P], zeros[:, 0:(NT // 2) * WIN], start=True, stop=False)
            for j in range(GT):
                t = g * GT + j
                e.wait_ge(c_win_hot.handle, t + 1)
                for i in range(NT):
                    at = (i % (NT // 2)) * WIN
                    last = e.matmul(halves_[i // (NT // 2)][0:rows[i], at:at + WIN],
                                    hot_full[t % 2][:, i * P:i * P + rows[i]], hot_part[t % 2][:, 0:WIN],
                                    start=False, stop=False, skip_group_check=True)
                last.then_inc(c_win_free.handle, 1)
            for half in halves_:
                last = e.matmul(half, zeros[:, 0:P], zeros[:, 0:(NT // 2) * WIN], start=False, stop=True)
            last.then_inc(c_win_sum.handle, 1)

        def all_pe(e):
            def product(buf, g, start, stop):
                last = None
                for a in range(2):
                    k = 2 * g + a
                    for (c, w), bank in zip(pieces, all_sum[a]):
                        if buf is None:
                            last = e.matmul(bank[0:rows[k], 0:w], zeros[:, 0:rows[k]], zeros[:, 0:w],
                                            start=start, stop=stop)
                        else:
                            last = e.matmul(bank[0:rows[k], 0:w], hot_part[buf][:, a * P:a * P + rows[k]],
                                            hot_full[buf][:, c:c + w], start=False, stop=False)
                return last

            for g in range(NT // 2):
                if g:
                    e.wait_ge(c_all_kept.handle, 2 * g)
                product(None, g, True, False)
                with e.Fori(0, ET // 2) as r:
                    for buf in range(2):
                        e.wait_ge(c_all_hot.handle, r * 2 + (g * ET + buf + 1))
                        product(buf, g, False, False).then_inc(c_all_free.handle, 1)
                product(None, g, False, True).then_inc(c_all_sum.handle, 1)

        def pe_begin(e):
            load_span(e)
            for c in (c_win_free, c_win_added, c_all_free):
                e.sem_inc(c.handle, 2)

        def pe_segment(e, n):
            with e.If(span[e.engine] < WIN):
                windows_pe(e, 2 * n)
                windows_pe(e, 2 * n + 1)
            if n == GROUPS // 2 - 1:
                with e.Else():
                    all_pe(e)

        pe.after(ev_rel)
        pe.steps.append(pe_begin)
        segments = [0]

        def count_segment():
            n = segments[0]
            if n < GROUPS // 2:
                segments[0] += 1
                pe.steps.append(lambda e: pe_segment(e, n))

        for _ in range(3):
            count_segment()

        side_free = {3: None, 7: None}
        side = [0]

        def side_bank():
            side[0] ^= 1
            return (3, 7)[side[0]]

        rhs = view(rowbuf[:, :, :].rearrange("p a b -> p (a b)"), 0, [KT, 2 * P + 4])
        pe.after(ev_const, *ev_w)
        b_w = side_bank()
        pe.run(lambda e: e.transpose(banks[b_w][0:C0, 0:2 * H0], attn_in, ident[0:2 * H0, 0:2 * H0]))
        pe.run(lambda e: e.transpose(banks[b_w][:, P:P + C0], W0_twice.rearrange("p a b -> p (a b)"), ident[0:C0, 0:C0]))
        ev = pe.run(lambda e: e.transpose(banks[b_w][:, 2 * P:2 * P + C0], Wres_twice.rearrange("p a b -> p (a b)"),
                                          ident[0:C0, 0:C0]), c_pe)
        c_rhs0 = counter("rhs0_zero")
        ev_zero = pool.run(lambda e: e.memset(rhs[:, :, :], 0.0), c_rhs0)
        act.after(ev, ev_zero)
        ev_at = act.run(lambda e: e.copy(attnT, banks[b_w][0:C0, 0:2 * H0]), c_act)
        for k in range(KT):
            for half in range(2):
                ps = slice(half * C0, half * C0 + C0)
                act.run(lambda e, k=k, ps=ps: e.copy(rhs[ps, k, ps.start:ps.stop], banks[b_w][ps, P:P + C0]))
                last = act.run(lambda e, k=k, ps=ps: e.copy(rhs[ps, k, P + ps.start:P + ps.stop],
                                                            banks[b_w][ps, 2 * P:2 * P + C0]), c_act)
        side_free[b_w] = last
        b2_ = side_bank()
        pe.after(ev_at)
        ev = pe.run(lambda e: e.matmul(banks[b2_][:, 0:2 * H0], W0_twice.rearrange("p a b -> p (a b)"), attnT,
                                       start=True, stop=True), c_pe)
        act.after(ev)
        for half in range(2):
            ps = slice(half * C0, half * C0 + C0)
            for side_ in range(2):
                ev_rhs = act.run(lambda e, half=half, ps=ps, s=side_: e.copy(
                    rhs[ps, :, 2 * P + 2 * s + half],
                    banks[b2_][ps, s * H0 + half:(s + 1) * H0:2]), c_act)
        side_free[b2_] = ev_rhs
        pe.after(*ev_x)
        for k in range(KT):
            for c, w in pieces:
                b = side_bank()
                if c == 0:
                    count_segment()
                pe.after(side_free[b])
                for i in range(c // P, (c + w + P - 1) // P):
                    ev = pe.run(lambda e, b=b, c=c, i=i, k=k: e.transpose(
                        banks[b][:, i * P - c:i * P - c + rows[i]], x_in[0:rows[i], i, k * P:(k + 1) * P],
                        ident[0:rows[i], 0:rows[i]]), c_pe)
                act.after(ev)
                ev_xT = side_free[b] = act.run(lambda e, b=b, c=c, w=w, k=k: e.copy(xT[:, k, c:c + w],
                                                                                    banks[b][:, 0:w]), c_act)
        pool.after(ev_xT)
        ev_ones = pool.run(lambda e: e.memset(ft, 1.0), counter("ft_ones"))
        pe.after(ev_xT, ev_rhs)
        for i in range(NT):
            m = rows[i]
            count_segment()
            for k in range(KT):
                b = side_bank()
                pe.after(side_free[b])
                ev = pe.run(lambda e, b=b, m=m, i=i, k=k: e.matmul(
                    banks[b][0:m, 0:2 * P + 4], xT[:, k, i * P:i * P + m], rhs[:, k, :], start=True, stop=True), c_pe)
                act.after(ev, ev_ones, ev_const)
                act.run(lambda e, b=b, m=m, i=i, k=k: e.copy(
                    ft[0:m, i, 2 * k:2 * k + 2, 0:C0],
                    banks[b][0:m, 0:P].rearrange("p (a b) -> p a b", a=2)))
                act.run(lambda e, b=b, m=m, i=i, k=k: e.copy(acc0[0:m, i, k * P:(k + 1) * P], banks[b][0:m, P:2 * P]))
                ev_ft = side_free[b] = act.run(lambda e, b=b, m=m, i=i, k=k: e.copy(
                    att[0:m, i, :].rearrange("p (s h) -> p s h", s=2)[:, :, 2 * k:2 * k + 2],
                    banks[b][0:m, 2 * P:2 * P + 4].rearrange("p (s h) -> p s h", s=2)), c_act)

        while segments[0] < GROUPS // 2:
            count_segment()

        c_turn = counter("counts_wide")
        turned_free = [None, None]
        count_free = [ev_counted, ev_counted]
        LC_ready = []
        for k in range(NT):
            m = rows[k]
            b = k % 2
            pool.after(ev_counted, turned_free[b])
            for lo, hi, n in ((0, NT - 1, P), (NT - 1, NT, rows[-1])):
                ev = pool.run(lambda e, b=b, k=k, m=m, lo=lo, hi=hi, n=n: e.tensor_copy(
                    turned[b][0:n, lo:hi, 0:m], CT[0:n, lo:hi, k * P:k * P + m]), c_turn)
            pe.after(ev, count_free[b])
            for i in range(NT):
                ev = pe.run(lambda e, b=b, i=i, m=m: e.transpose(
                    banks[4 * b + i // 4][0:m, (i % 4) * P:(i % 4) * P + rows[i]], turned[b][0:rows[i], i, 0:m],
                    ident[0:rows[i], 0:rows[i]]), c_pe)
            turned_free[b] = ev
            act.after(ev)
            count_free[b] = act.run(lambda e, b=b, k=k, m=m: e.activation(
                LC[0:m, k, :], psum[0:m, 4 * b:4 * b + 3, :].rearrange("p a b -> p (a b)")[:, 0:N], ACT.Ln,
                bias=tiny[0:m, :], scale=2.0), c_act)
            dve.after(ev_counted, count_free[b])
            LC_ready.append(dve.run(lambda e, k=k, m=m: e.scalar_tensor_tensor(
                out=LC[0:m, k, :], in0=LC[0:m, k, :], scalar=NO_EDGE_FACTOR, in1=LC[0:m, k, :], op0=ALU.mult,
                op1=ALU.min), c_dve))
            if k:
                dve.after(ev_diag)
            ev_diag = dve.run(lambda e, k=k, m=m: e.tensor_tensor_reduce(
                colbuf[0:m, 0, 0:m], CT[0:m, k, k * P:k * P + m], ident[0:m, 0:m], 1.0, 0.0, ALU.mult, ALU.add,
                diag_count[0:m, k:k + 1]), c_dve)
        ev_counting_over = count_free[0]
        ev_LC = ev_diag
        dve.after(ev_diag)

        ring_free = [None] * RING
        ring_at = [0]
        turn_at = [0]
        turn_free = [count_free[0]] * 2
        col_at = [0]
        acc_free = [count_free[1]] * 4
        misc_at = [0]
        misc_free = [count_free[0], count_free[1]]

        def row_of(col, buf, piece, free_evs):
            c, w = pieces[piece]
            b = misc_at[0] % 2
            misc_at[0] += 1
            pe.after(misc_free[b], *row_ready)
            for i in range(c // P, (c + w + P - 1) // P):
                m = rows[i]
                ev = pe.run(lambda e, i=i, m=m: e.matmul(
                    misc_banks[b][:, i * P - c:i * P - c + m], att[0:m, i, col:col + 1].to_broadcast([m, P]),
                    ident[0:m, 0:m], start=True, stop=True), c_pe)
            dve.after(ev, *free_evs)
            misc_free[b] = dve.run(lambda e: e.tensor_copy(rowbuf[:, buf, c:c + w], misc_banks[b][:, 0:w]), c_dve)
            return misc_free[b]

        def edge_maximum(i, row_buf, row_ev, slot, junk):
            m = rows[i]
            dve.after(row_ev, junk_written[0])
            junk_written[0] = dve.run(lambda e: e.tensor_tensor_reduce(
                junk[0:m, :], rowbuf[0:m, row_buf, :], LC[0:m, i, :], 1.0, MAX_FLOOR, ALU.add, ALU.max,
                row_max[0:m, slot:slot + 1]), c_dve)

        def unit_maxima(tiles, slot, dst_col, net):
            t = row_max[:, slot:slot + len(tiles)]
            a = att[:, tiles[0]:tiles[-1] + 1, dst_col]
            dve.after(junk_written[0])
            ev = dve.run(lambda e: e.tensor_tensor(t, t, a, ALU.add), c_dve)
            dve.after(ev)
            ev = dve.run(lambda e: e.scalar_tensor_tensor(out=t, in0=t, scalar=SLOPE, in1=t, op0=ALU.mult,
                                                          op1=ALU.max), c_dve)
            dve.after(ev)
            return dve.run(lambda e: e.tensor_tensor(t, t, net.att_slope[:, tiles[0]:tiles[-1] + 1, dst_col],
                                                     ALU.subtract), c_dve)

        def scores(i, row_buf, row_ev, dst_col, slot, max_slot, max_ev, net):
            m = rows[i]
            act.after(row_ev, ring_free[slot])
            ev_r = act.run(lambda e: e.activation(ring[0:m, slot, :], rowbuf[0:m, row_buf, :], ACT.Relu,
                                                  bias=net.att_rest[0:m, i, dst_col:dst_col + 1],
                                                  scale=1.0 - SLOPE), c_act)
            dve.after(ev_r, max_ev)
            ev = dve.run(lambda e: e.scalar_tensor_tensor(
                out=ring[0:m, slot, :], in0=ring[0:m, slot, :], scalar=row_max[0:m, max_slot:max_slot + 1],
                in1=LC[0:m, i, :], op0=ALU.subtract, op1=ALU.add), c_dve)
            return ev_r, ev

        def columns(s, tiles, slots, col_ap, col_free, bias):
            m = rows[s]
            b = turn_at[0] % 2
            turn_at[0] += 1
            pe.after(turn_free[b])
            w = 0
            for (slot, ev_s), i in zip(slots, tiles):
                pe.after(ev_s)
                n = rows[i]
                ev = pe.run(lambda e, slot=slot, n=n, w=w: e.transpose(
                    turn_banks[b][0:m, w:w + n], ring[0:n, slot, s * P:s * P + m], ident[0:n, 0:n]), c_pe)
                w += n
            if s == NT - 1:
                for slot, _ in slots:
                    ring_free[slot] = ev
            act.after(ev, col_free)
            turn_free[b] = act.run(lambda e: e.activation(col_ap[0:m, 0:w], turn_banks[b][0:m, 0:w], ACT.Exp,
                                                          bias=bias), c_act)
            return turn_free[b], w

        class Net:

            def __init__(self, att_slope, att_rest, junk, ring_slots, ready):
                self.att_slope, self.att_rest, self.junk, self.ring_slots = att_slope, att_rest, junk, ring_slots
                self.n = att_slope.shape[2]
                dve.after(*ready)
                self.scaled = None
                self.junk_ready = ready

            def scale_terms(self, ev):
                dve.after(ev)
                dve.run(lambda e: e.tensor_scalar(self.att_slope, att[:, :, 0:self.n], SLOPE, None, ALU.mult), c_dve)
                return dve.run(lambda e: e.tensor_scalar(self.att_rest, att[:, :, 0:self.n], 1.0 - SLOPE, None,
                                                         ALU.mult), c_dve)

        junk_written = [None]
        row_ready = []
        max_free = [None, None]

        def attention(net, heads, row_col, dst_col, begin_head, column, use, finish):
            todo = [(h, u) for h in heads for u in range(len(units))]
            made = {}
            row_evs = {}
            row_readers = {}

            def make_row(h, piece):
                row_readers.setdefault(h, [])
                row_evs[h] = row_of(row_col(h), h % 2, piece, row_readers.get(h - 2, []))

            def beside(old, s):
                h, u = old
                if h + 1 not in heads:
                    return
                if u == 0:
                    begin_head(h + 1, s)
                if u == 1 and s in (1, 4, 7):
                    make_row(h + 1, s // 3)

            for n in range(len(todo) + 1):
                new = todo[n] if n < len(todo) else None
                old = todo[n - 1] if n else None
                plan = []
                if new:
                    h, u = new
                    if h not in row_evs:
                        for i in range(NT):
                            begin_head(h, i)
                        for piece in range(len(pieces)):
                            make_row(h, piece)
                    made[new] = []
                    tiles = units[u]
                    half = 4 * (n % 2)
                    state = {}

                    def maximum(j, h=h, tiles=tiles, half=half):
                        if j == 0:
                            dve.after(max_free[half // 4])
                        edge_maximum(tiles[j], h % 2, row_evs[h], half + j, net.junk)
                        row_readers[h].append(junk_written[0])

                    def all_maxima(h=h, tiles=tiles, half=half, state=state):
                        state["ev"] = unit_maxima(tiles, half, dst_col(h), net)

                    def score(j, h=h, tiles=tiles, half=half, state=state, new=new):
                        slot = ring_at[0] % net.ring_slots
                        ring_at[0] += 1
                        ev_r, ev = scores(tiles[j], h % 2, row_evs[h], dst_col(h), slot, half + j, state["ev"], net)
                        made[new].append((slot, ev))
                        row_readers[h].append(ev_r)
                        max_free[half // 4] = ev

                    plan = [lambda j=j: maximum(j) for j in range(len(tiles))] + [all_maxima]
                    plan += [lambda j=j: score(j) for j in range(len(tiles))]
                if not old:
                    for step in plan:
                        step()
                    column(new, 0, units[new[1]], made[new])
                    continue
                for s in range(NT):
                    if s < len(plan):
                        plan[s]()
                    beside(old, s)
                    if s + 1 < NT:
                        column(old, s + 1, units[old[1]], made[old])
                    elif new:
                        column(new, 0, units[new[1]], made[new])
                    use(old, s, units[old[1]])
                finish(old, units[old[1]])

        c_fin = counter("network0_units")
        col_free = [None] * 3
        agg_free = [None] * 2
        recip_read = [None]
        acc_of = {}

        def ring_ready(ev):
            for s in range(RING):
                ring_free[s] = ev

        ring_ready(turned_free[1])
        act.after(ev_LC)
        col_free_after = ev_LC
        dve_last0 = {}

        col_slot = {}

        def column0(unit, s, tiles, slots):
            h, u = unit
            c = col_at[0] % 3
            col_at[0] += 1
            col_slot[unit, s] = c, columns(s, tiles, slots, colbuf[:, c, :], col_free[c],
                                           net0.att_slope[0:rows[s], s, h:h + 1])

        def use0(unit, s, tiles):
            h, u = unit
            if s == 3 and late0:
                late0.pop()()
            c, (ev, w) = col_slot[unit, s]
            if s == 0:
                acc_of[unit] = len(acc_of) % 2
                pe.after(acc_free[acc_of[unit]])
            b = acc_of[unit]
            m = rows[s]
            pe.after(ev)
            col_free[c] = pe.run(lambda e: e.matmul(acc_banks[b][0:C0 + 1, 0:w], ft[0:m, s, h, :],
                                                    colbuf[0:m, c, 0:w], start=(s == 0), stop=(s == NT - 1)), c_pe)

        late0 = []

        def finish0(unit, tiles):
            h, u = unit
            b = acc_of[unit]
            w = sum(rows[i] for i in tiles)
            dve.after(c_pe.now(), agg_free[b])
            ev = dve.run(lambda e: e.tensor_copy(aggT[b][:, 0:w], acc_banks[b][0:C0 + 1, 0:w]), c_dve)
            acc_free[b] = ev
            late0.append(lambda: normalise0(h, b, tiles, ev))

        def normalise0(h, b, tiles, ev):
            ob = acc_banks[2 + b]
            pe.after(ev, acc_free[2 + b])
            at = 0
            for j, i in enumerate(tiles):
                n = rows[i]
                ev = pe.run(lambda e, j=j, n=n, at=at: e.transpose(
                    ob[0:n, j * (C0 + 1):(j + 1) * (C0 + 1)], aggT[b][:, at:at + n], ident[0:C0 + 1, 0:C0 + 1]), c_pe)
                at += n
            agg_free[b] = ev
            dve.after(ev)
            k = len(tiles)
            full = k if rows[tiles[-1]] == P else k - 1
            sums = ob[:, C0:C0 + (k - 1) * (C0 + 1) + 1:C0 + 1]
            dve.after(recip_read[0])
            groups = [(0, full, P)] + ([(full, k, rows[tiles[-1]])] if full < k else [])
            for lo, hi, m in groups:
                ev = dve.run(lambda e, lo=lo, hi=hi, m=m: e.tensor_scalar(recip[0:m, lo:hi], sums[0:m, lo:hi],
                                                                          1e-16, None, ALU.max), c_dve)
            dve.after(ev)
            for lo, hi, m in groups:
                ev = dve.run(lambda e, lo=lo, hi=hi, m=m: e.reciprocal(recip[0:m, lo:hi], recip[0:m, lo:hi]), c_dve)
            dve.after(ev)
            for j, i in enumerate(tiles):
                n = rows[i]
                dst_ap = acc0[0:n, i, h * C0:(h + 1) * C0]
                ev = dve.run(lambda e, j=j, n=n, dst_ap=dst_ap: e.scalar_tensor_tensor(
                    out=dst_ap, in0=ob[0:n, j * (C0 + 1):j * (C0 + 1) + C0], scalar=recip[0:n, j:j + 1],
                    in1=dst_ap, op0=ALU.mult, op1=ALU.add), c_dve)
            acc_free[2 + b] = recip_read[0] = ev

        def begin0(h, i):
            pass

        net0 = Net(view(R3, 2 * BANK, [NT, 2 * H0]), view(R1, RING * N, [NT, 2 * H0]),
                   view(R3, 4 * BANK, [N], BF16), RING, [ev_ft])
        act.after(net0.scale_terms(ev_LC))
        row_ready.append(ev_ft)
        attention(net0, range(H0), lambda h: h, lambda h: H0 + h, begin0, column0, use0, finish0)
        late0.pop()()
        ev_attn0 = c_dve.now()

        ev_x0 = rows_in("x0", x0, x, ev_attn0, c_pe.now())
        dve.after(*ev_x0)
        ev = act.run(lambda e: e.activation(diag_ln[:, 0:NT - 1], diag_count[:, 0:NT - 1], ACT.Ln, bias=2.0, scale=2.0), c_act)
        ev = act.run(lambda e: e.activation(diag_ln[0:rows[-1], NT - 1:NT], diag_count[0:rows[-1], NT - 1:NT],
                                            ACT.Ln, bias=2.0, scale=2.0), c_act)
        for i in range(NT):
            m = rows[i]
            dve.run(lambda e, m=m, i=i: e.scalar_tensor_tensor(
                out=acc0[0:m, i, :], in0=acc0[0:m, i, :], scalar=0.0, in1=x0[0:m, i, :], op0=ALU.max, op1=ALU.add),
                c_dve)
        ev_sum = c_dve.now()
        dve.after(ev)
        for i in range(NT):
            m = rows[i]
            block = LC[0:m, i, i * P:i * P + m]
            ev = dve.run(lambda e, m=m, b=block: e.tensor_tensor(b, b, off_diag[0:m, 0:m], ALU.mult), c_dve)
            dve.after(ev)
            ev_LC1 = dve.run(lambda e, m=m, i=i, b=block: e.scalar_tensor_tensor(
                out=b, in0=ident[0:m, 0:m], scalar=diag_ln[0:m, i:i + 1], in1=b, op0=ALU.mult, op1=ALU.add), c_dve)

        c_pool_rstd = counter("rstd")

        def norm_stats(i, ap, width, waits=()):
            m = rows[i]
            half = width // 2
            dve.after(*waits)
            dve.run(lambda e: e.bn_stats(stats[0:m, 0, 0:6], ap[:, 0:half]))
            ev = dve.run(lambda e: e.bn_stats(stats[0:m, 0, 6:12], ap[:, half:width]), c_dve)
            dve.after(ev)
            ev = dve.run(lambda e: e.bn_aggr(moments[0:m, i, :], stats[0:m, 0, :]), c_dve)
            dve.after(ev)
            ev = dve.run(lambda e: e.tensor_scalar(rstd[0:m, i:i + 1], moments[0:m, i, 1:2], LN_EPS, None, ALU.add),
                         c_dve)
            pool.after(ev)
            return pool.run(lambda e: e.tensor_tensor(rstd[0:m, i:i + 1], rstd[0:m, i:i + 1], minus_half[0:m, :],
                                                      ALU.pow), c_pool_rstd)

        x1T = view(R3, 0, [KT, N])
        dve.after(ev_sum)
        evs = [norm_stats(i, acc0[0:rows[i], i, :], D) for i in range(NT)]
        ev_x1 = []
        for i in range(NT):
            m = rows[i]
            dve.after(evs[i])
            ev_x1.append(dve.run(lambda e, m=m, i=i: e.tensor_scalar(
                acc0[0:m, i, :], acc0[0:m, i, :], moments[0:m, i, 0:1], rstd[0:m, i:i + 1],
                ALU.subtract, ALU.mult), c_dve))
        full = (NT - 1) * P
        ev_spill = [load("x1_out_full", x1_dram[0:full, :].rearrange("(t p) d -> p t d", p=P), acc0[:, 0:NT - 1, :],
                         ev_x1[-1]),
                    load("x1_out_last", x1_dram[full:N, :], acc0[0:rows[-1], NT - 1, :])]

        def transpose_rows(src_ap, dst_ap, n_k, tile_evs, free_ev):
            last = None
            for c, w in pieces:
                for k in range(n_k):
                    b = turn_at[0] % 2
                    turn_at[0] += 1
                    pe.after(turn_free[b])
                    for i in range(c // P, (c + w + P - 1) // P):
                        pe.after(tile_evs[i])
                        ev = pe.run(lambda e, b=b, c=c, i=i, k=k: e.transpose(
                            turn_banks[b][:, i * P - c:i * P - c + rows[i]],
                            src_ap[0:rows[i], i, k * P:(k + 1) * P], ident[0:rows[i], 0:rows[i]]), c_pe)
                    act.after(ev, free_ev)
                    last = turn_free[b] = act.run(lambda e, b=b, c=c, w=w, k=k: e.copy(
                        dst_ap[:, k, c:c + w], turn_banks[b][:, 0:w]), c_act)
            return last

        ev_x1T = transpose_rows(acc0, x1T, KT, ev_x1, ev_sum)

        XL = NT * (C1 + 1)
        base = NT * D
        xl = [view(R3, base + b * XL, [NT, C1 + 1]) for b in range(2)]
        W1h = view(R3, base + 2 * XL, [KT, C1])
        h_buf = view(R2, 0, [NT, HC])
        vec_at = base + 2 * XL + KT * C1
        a1_b = [view(R3, vec_at + s * C1, [C1]) for s in range(2)]
        b1_b = view(R3, vec_at + 2 * C1, [C1])
        assert vec_at + 3 * C1 + NT * 2 * H1 <= 2 * NT * D
        ring_junk = view(R1, (RING - 1) * N, [N])
        pool.after(*ev_spill, ev_x1T)
        ev_ones1 = pool.run(lambda e: e.memset(view(R3, base, [2 * XL]), 1.0), counter("xl_ones"))
        lin_free = [None, None]
        w1_free = [None]
        xl_free = [None] * 4
        vec_free = [None]
        b1_free = [None]
        ev_b1 = {}
        unit_last = {}

        w1_ev = {}

        def begin1(h, i):
            if i == 0:
                w1_ev[h] = [
                    load(f"w1_{h}", W1h, W1[:, h * C1:(h + 1) * C1].rearrange("(k p) c -> p k c", p=P),
                         ev_ones1, *ev_spill, ev_x1T, w1_free[0]),
                    load(f"a1s_{h}", a1_b[0], spread(a_src1[h]), ev_ones1, ev_x1T, *ev_spill, vec_free[0]),
                    load(f"a1d_{h}", a1_b[1], spread(a_dst1[h]))]
            k = h % 2
            m = rows[i]
            b = misc_at[0] % 2
            misc_at[0] += 1
            pe.after(ev_x1T, *w1_ev[h], misc_free[b])
            for kk in range(KT):
                ev = pe.run(lambda e, kk=kk: e.matmul(
                    misc_banks[b][0:m, 0:C1], x1T[:, kk, i * P:i * P + m], W1h[:, kk, :],
                    start=(kk == 0), stop=(kk == KT - 1)), c_pe)
            dve.after(ev, xl_free[h - 2] if h >= 2 else None, ev_ones1)
            ev = dve.run(lambda e: e.tensor_copy(xl[k][0:m, i, 0:C1], misc_banks[b][0:m, 0:C1]), c_dve)
            dve.after(ev, *w1_ev[h])
            for s in range(2):
                dve.after(ev)
                ev = dve.run(lambda e, s=s: e.tensor_tensor_reduce(
                    misc_banks[b][0:m, C1:2 * C1], xl[k][0:m, i, 0:C1], a1_b[s][0:m, :], 1.0, 0.0, ALU.mult,
                    ALU.add, att[0:m, i, 2 * h + s:2 * h + s + 1]), c_dve)
            misc_free[b] = ev
            if i < NT - 1:
                return
            w1_free[0] = c_pe.now()
            vec_free[0] = ev
            dve.after(ev)
            for part, factor in ((net1.att_slope, SLOPE), (net1.att_rest, 1.0 - SLOPE)):
                ev = dve.run(lambda e, p=part, f=factor: e.tensor_scalar(
                    p[:, :, 2 * h:2 * h + 2], att[:, :, 2 * h:2 * h + 2], f, None, ALU.mult), c_dve)
            act.after(ev)
            row_ready[:] = [ev]

        def column1(unit, s, tiles, slots):
            h, u = unit
            c = col_at[0] % 3
            col_at[0] += 1
            col_slot[unit, s] = c, columns(s, tiles, slots, colbuf[:, c, :], col_free[c],
                                           net1.att_slope[0:rows[s], s, 2 * h:2 * h + 1])

        def use1(unit, s, tiles):
            h, u = unit
            c, (ev, w) = col_slot[unit, s]
            m = rows[s]
            at = 0
            for j, i in enumerate(tiles):
                if s == 0:
                    pe.after(acc_free[j])
                pe.after(ev)
                n = rows[i]
                col_free[c] = pe.run(lambda e, j=j, n=n, at=at: e.matmul(
                    acc_banks[j][0:n, 0:C1 + 1], colbuf[0:m, c, at:at + n], xl[h % 2][0:m, s, :],
                    start=(s == 0), stop=(s == NT - 1)), c_pe)
                at += n
            if s == NT - 1:
                xl_free[h] = col_free[c]

        def finish1(unit, tiles):
            h, u = unit
            if u == 0:
                ev_b1[h] = load(f"b1_{h}", b1_b, spread(b1[h * C1:(h + 1) * C1]), b1_free[0])
            dve.after(c_pe.now(), ev_b1[h], recip_read[0])
            for j, i in enumerate(tiles):
                n = rows[i]
                ev = dve.run(lambda e, j=j, n=n: e.tensor_scalar(recip[0:n, j:j + 1], acc_banks[j][0:n, C1:C1 + 1],
                                                                 1e-16, None, ALU.add), c_dve)
            dve.after(ev)
            for j, i in enumerate(tiles):
                n = rows[i]
                ev = dve.run(lambda e, j=j, n=n: e.reciprocal(recip[0:n, j:j + 1], recip[0:n, j:j + 1]), c_dve)
            dve.after(ev)
            for j, i in enumerate(tiles):
                n = rows[i]
                acc_free[j] = dve.run(lambda e, j=j, n=n, i=i: e.scalar_tensor_tensor(
                    out=h_buf[0:n, i, h * C1:(h + 1) * C1], in0=acc_banks[j][0:n, 0:C1], scalar=recip[0:n, j:j + 1],
                    in1=b1_b[0:n, :], op0=ALU.mult, op1=ALU.add), c_dve)
            b1_free[0] = recip_read[0] = acc_free[len(tiles) - 1]

        dve.after(ev_LC1)
        ring_ready(None)
        net1 = Net(view(R3, vec_at + 3 * C1, [NT, 2 * H1]), view(R1, RING * N, [NT, 2 * H1]),
                   ring_junk, RING - 1, [])
        attention(net1, range(H1), lambda h: 2 * h, lambda h: 2 * h + 1, begin1, column1, use1, finish1)
        ev_attn1 = c_dve.now()
        ev_attn1_pe = c_pe.now()

        Wr1_sb = view(R1, 0, [KT, HC])
        vecs1 = view(R3, base, [4, HC])
        ev_wr1 = load("wr1", Wr1_sb, Wr1.rearrange("(k p) c -> p k c", p=P), ev_attn1_pe, ev_attn1)
        ev_v = [load(f"vec1_{n}", vecs1[:, n, :], spread(v)) for n, v in enumerate((g1, be1, br1))]
        ones_row = view(R3, base + 4 * HC, [P])
        ev_or = pool.after(ev_attn1_pe).run(lambda e: e.memset(ones_row, 1.0), counter("ones_row"))
        evs = [norm_stats(i, h_buf[0:rows[i], i, :], HC) for i in range(NT)]
        ev_h1 = []
        for i in range(NT):
            m = rows[i]
            pair = (i % 2) * 2
            pe.after(ev_wr1, ev_v[2], ev_or, acc_free[pair], acc_free[pair + 1])
            for half in range(2):
                cols = slice(half * BANK, (half + 1) * BANK)
                for k in range(KT):
                    pe.run(lambda e, k=k, m=m, i=i, cols=cols, b=pair + half: e.matmul(
                        acc_banks[b][0:m, :], x1T[:, k, i * P:i * P + m], Wr1_sb[:, k, cols],
                        start=(k == 0), stop=False))
                ev = pe.run(lambda e, m=m, cols=cols, b=pair + half: e.matmul(
                    acc_banks[b][0:m, :], ones_row[0:1, 0:m], vecs1[0:1, 2, cols], start=False, stop=True), c_pe)
            hi = h_buf[0:m, i, :]
            dve.after(evs[i], *ev_v)
            e1 = dve.run(lambda e, m=m, i=i, hi=hi: e.scalar_tensor_tensor(
                out=hi, in0=hi, scalar=moments[0:m, i, 0:1], in1=vecs1[0:m, 0, :], op0=ALU.subtract, op1=ALU.mult),
                c_dve)
            dve.after(e1)
            e1 = dve.run(lambda e, m=m, i=i, hi=hi: e.scalar_tensor_tensor(
                out=hi, in0=hi, scalar=rstd[0:m, i:i + 1], in1=vecs1[0:m, 1, :], op0=ALU.mult, op1=ALU.add), c_dve)
            dve.after(e1, ev)
            for half in range(2):
                cols = slice(half * BANK, (half + 1) * BANK)
                e1 = dve.run(lambda e, m=m, hi=hi, cols=cols, b=pair + half: e.scalar_tensor_tensor(
                    out=hi[:, cols], in0=hi[:, cols], scalar=0.0, in1=acc_banks[b][0:m, :], op0=ALU.max,
                    op1=ALU.add), c_dve)
            acc_free[pair] = acc_free[pair + 1] = e1
            ev_h1.append(e1)
        ev_wr1_done = c_pe.now()

        h1T = view(R3, 0, [KH, N])
        tail = KH * N
        a2_b = [view(R3, tail + s * D, [D]) for s in range(2)]
        stage = [view(R3, tail + (2 + s) * D, [D]) for s in range(2)]
        x1_back = [view(R3, tail + (4 + s) * D, [D]) for s in range(2)]
        br2_row = rowbuf[:, 0, 0:D]
        W2_sb = view(R1, 0, [KH, D])
        xl2 = view(R2, 0, [NT, D + 1])
        ev_w2 = load("w2", W2_sb, W2.rearrange("(k p) c -> p k c", p=P), ev_wr1_done)
        ev_a2 = [load("a2s", a2_b[0], spread(a_src2[0]), ev_h1[-1], ev_wr1_done),
                 load("a2d", a2_b[1], spread(a_dst2[0])), load("br2", br2_row, spread(br2))]
        ev_h1T = transpose_rows(h_buf, h1T, KH, ev_h1, ev_h1[-1])
        assert tail + 6 * D <= 2 * NT * D
        ones2 = rowbuf[:, 0, D:D + P]
        ev_or2 = pool.after(ev_h1[-1], ev_wr1_done).run(lambda e: e.memset(ones2, 1.0), counter("ones_row2"))
        ev_ones2 = pool.after(ev_h1T).run(lambda e: e.memset(xl2, 1.0), counter("xl2_ones"))
        halves = [(0, BANK), (BANK, D - BANK)]
        ev_att2 = None
        for i in range(NT):
            m = rows[i]
            pair = (i % 2) * 2
            pe.after(ev_w2, ev_h1T, acc_free[pair], acc_free[pair + 1])
            for half, (c, w) in enumerate(halves):
                for k in range(KH):
                    ev = pe.run(lambda e, k=k, m=m, i=i, c=c, w=w, b=pair + half: e.matmul(
                        acc_banks[b][0:m, 0:w], h1T[:, k, i * P:i * P + m], W2_sb[:, k, c:c + w],
                        start=(k == 0), stop=(k == KH - 1)), c_pe)
            act.after(ev, ev_ones2)
            for half, (c, w) in enumerate(halves):
                ev = act.run(lambda e, m=m, i=i, c=c, w=w, b=pair + half: e.copy(
                    xl2[0:m, i, c:c + w], acc_banks[b][0:m, 0:w]), c_act)
            acc_free[pair] = acc_free[pair + 1] = ev
            dve.after(ev, *ev_a2)
            for s in range(2):
                dve.after(ev_att2)
                ev_att2 = dve.run(lambda e, i=i, m=m, s=s: e.tensor_tensor_reduce(
                    rowbuf[0:m, 1, 0:D], xl2[0:m, i, 0:D], a2_b[s][0:m, :], 1.0, 0.0, ALU.mult, ALU.add,
                    att[0:m, i, s:s + 1]), c_dve)
        ev_w2_done = c_pe.now()
        Wr2_sb = view(R1, 0, [KH, D])
        ev_wr2 = load("wr2", Wr2_sb, Wr2.rearrange("(k p) c -> p k c", p=P), ev_w2_done)
        x1b_free = [None, None]
        stage_free = [None, None]
        ev_base = []
        for i in range(NT):
            m = rows[i]
            pair = (i % 2) * 2
            s = i % 2
            ev_xb = load(f"x1b_{i}", x1_back[s][0:m, :], x1_dram[i * P:i * P + m, :], *ev_spill, x1b_free[s],
                         ev_h1[-1])
            pe.after(ev_wr2, *ev_a2, ev_or2, acc_free[pair], acc_free[pair + 1])
            for half, (c, w) in enumerate(halves):
                for k in range(KH):
                    pe.run(lambda e, k=k, m=m, i=i, c=c, w=w, b=pair + half: e.matmul(
                        acc_banks[b][0:m, 0:w], h1T[:, k, i * P:i * P + m], Wr2_sb[:, k, c:c + w],
                        start=(k == 0), stop=False))
                ev = pe.run(lambda e, m=m, c=c, w=w, b=pair + half: e.matmul(
                    acc_banks[b][0:m, 0:w], ones2[0:1, 0:m], br2_row[0:1, c:c + w], start=False, stop=True), c_pe)
            dve.after(ev, ev_xb, stage_free[s])
            for half, (c, w) in enumerate(halves):
                ev = dve.run(lambda e, m=m, s=s, c=c, w=w, b=pair + half: e.tensor_tensor(
                    stage[s][0:m, c:c + w], acc_banks[b][0:m, 0:w], x1_back[s][0:m, c:c + w], ALU.add), c_dve)
            acc_free[pair] = acc_free[pair + 1] = ev
            x1b_free[s] = ev
            stage_free[s] = load(f"base_{i}", base_dram[i * P:i * P + m, :], stage[s][0:m, :], ev)
            ev_base.append(stage_free[s])
        ev_wr2_done = c_pe.now()

        cols2 = view(R3, NT * D + 2 * NT, [NT + 1, BANK])
        base_sb = view(R3, 0, [NT, D])
        ev_bl = rows_in("base", base_sb, base_dram, *ev_base, ev_wr2_done)
        vec2_at = NT * (D + 1)
        vecs2 = view(R2, vec2_at, [3, D])
        assert vec2_at + 3 * D <= 10240
        ev_v2 = [load(f"vec2_{n}", vecs2[:, n, :], spread(v), ev_h1T) for n, v in enumerate((b2, g2, be2))]
        for b in range(RING):
            ring_free[b] = ev_wr2_done
        ring_at[0] = 0
        y_bufs = [view_ap for view_ap in (colbuf[:, :, :].rearrange("p a b -> p (a b)")[:, 0:D],
                                          colbuf[:, :, :].rearrange("p a b -> p (a b)")[:, D:2 * D])]
        cols2_free = [None] * (NT + 1)
        col2_at = [0]
        y_free = [col_free[2], col_free[2]]
        c_out = []

        def column2(unit, s, tiles, slots):
            c = col2_at[0] % (NT + 1)
            col2_at[0] += 1
            ev, w = columns(s, tiles, slots, cols2[:, c, :], cols2_free[c], net2.att_slope[0:rows[s], s, 0:1])
            col_ready[unit, s] = c, ev

        def use2(unit, s, tiles):
            pass

        col_ready = {}
        out_n = [0]

        def finish2(unit, tiles):
            at = 0
            for j, i in enumerate(tiles):
                n = rows[i]
                pair = (out_n[0] % 2) * 2
                yb = out_n[0] % 2
                out_n[0] += 1
                pe.after(acc_free[pair], acc_free[pair + 1])
                for s in range(NT):
                    m = rows[s]
                    place, ready = col_ready[unit, s]
                    pe.after(ready)
                    for half, (c, w) in enumerate([(0, BANK), (BANK, D + 1 - BANK)]):
                        ev = pe.run(lambda e, s=s, m=m, n=n, at=at, c=c, w=w, b=pair + half, place=place: e.matmul(
                            acc_banks[b][0:n, 0:w], cols2[0:m, place, at:at + n], xl2[0:m, s, c:c + w],
                            start=(s == 0), stop=(s == NT - 1)), c_pe)
                    cols2_free[place] = ev
                at += n
                y = y_bufs[yb][0:n, :]
                dve.after(ev, y_free[yb], *ev_v2, *ev_bl)
                r = recip[0:n, yb:yb + 1]
                ev = dve.run(lambda e, n=n, r=r, b=pair + 1: e.tensor_scalar(
                    r, acc_banks[b][0:n, D - BANK:D - BANK + 1], 1e-16, None, ALU.add), c_dve)
                dve.after(ev)
                ev = dve.run(lambda e, r=r: e.reciprocal(r, r), c_dve)
                dve.after(ev)
                for half, (c, w) in enumerate(halves):
                    ev = dve.run(lambda e, n=n, r=r, y=y, c=c, w=w, b=pair + half: e.scalar_tensor_tensor(
                        out=y[:, c:c + w], in0=acc_banks[b][0:n, 0:w], scalar=r, in1=vecs2[0:n, 0, c:c + w],
                        op0=ALU.mult, op1=ALU.add), c_dve)
                acc_free[pair] = acc_free[pair + 1] = ev
                ev = norm_stats(i, y, D, [ev])
                dve.after(ev)
                ev = dve.run(lambda e, n=n, i=i, y=y: e.scalar_tensor_tensor(
                    out=y, in0=y, scalar=moments[0:n, i, 0:1], in1=vecs2[0:n, 1, :], op0=ALU.subtract,
                    op1=ALU.mult), c_dve)
                dve.after(ev)
                ev = dve.run(lambda e, n=n, i=i, y=y: e.scalar_tensor_tensor(
                    out=y, in0=y, scalar=rstd[0:n, i:i + 1], in1=vecs2[0:n, 2, :], op0=ALU.mult, op1=ALU.add), c_dve)
                dve.after(ev)
                ev = dve.run(lambda e, n=n, i=i, y=y: e.tensor_tensor(y, y, base_sb[0:n, i, :], ALU.add), c_dve)
                ev = norm_stats(i, y, D, [ev])
                dve.after(ev)
                ev = dve.run(lambda e, n=n, i=i, y=y: e.tensor_scalar(
                    y, y, moments[0:n, i, 0:1], rstd[0:n, i:i + 1], ALU.subtract, ALU.mult), c_dve)
                y_free[yb] = load(f"out_{i}", out[i * P:i * P + n, :], y, ev)
                c_out.append(y_free[yb])

        net2 = Net(view(R3, NT * D, [NT, 2]), view(R1, RING * N, [NT, 2]), ring_junk, RING - 1, [ev_att2])
        dve.after(ev_wr2_done, *ev_base)
        act.after(*ev_base)
        act.after(net2.scale_terms(ev_att2))
        row_ready[:] = [ev_att2]
        attention(net2, [0], lambda h: 0, lambda h: 1, begin0, column2, use2, finish2)
        sync.after(*c_out)

        block = ctx.enter_context(nc.Block())

        @block.sync
        def _(e):
            sync.play(e)

        @block.tensor
        def _(e):
            pe.play(e)

        @block.scalar
        def _(e):
            act.play(e)

        @block.vector
        def _(e):
            dve.play(e)

        @block.gpsimd
        def _(e):
            pool.play(e)


_INS = ['x', 'src', 'dst', 'L0_gnn_W', 'L0_gnn_attn_l', 'L0_gnn_attn_r', 'L0_gnn_W_res', 'L1_gnn_W1',
        'L1_gnn_a_src1', 'L1_gnn_a_dst1', 'L1_gnn_b1', 'L1_gnn_g1', 'L1_gnn_be1', 'L1_gnn_Wr1', 'L1_gnn_br1',
        'L1_gnn_W2', 'L1_gnn_a_src2', 'L1_gnn_a_dst2', 'L1_gnn_b2', 'L1_gnn_g2', 'L1_gnn_be2', 'L1_gnn_Wr2',
        'L1_gnn_br2']


def kernel(**inputs):
    import numpy as _np
    import concourse.bacc as _bacc
    from concourse import mybir as _mybir
    from concourse.bass_utils import run_bass_kernel_spmd as _run

    nc = _bacc.Bacc("TRN2", target_bir_lowering=False, num_devices=1)
    arrays, args = {}, []
    for name in _INS:
        a = _np.ascontiguousarray(inputs[name])
        arrays[f"in_{name}_dram"] = a
        args.append(nc.dram_tensor(f"in_{name}_dram", a.shape, _mybir.dt.from_np(a.dtype), kind="ExternalInput").ap())
    out = nc.dram_tensor("out_dram", inputs['x'].shape, _mybir.dt.float32, kind="ExternalOutput").ap()
    gnn_kernel(nc, *args, out)
    r = _run(nc, [arrays], core_ids=[0])
    return r.results[0]["out_dram"]
```

```python
from contextlib import ExitStack

import concourse.bass as bass
from concourse import mybir

F32 = mybir.dt.float32
F32R = mybir.dt.float32r
BF16 = mybir.dt.bfloat16
F16 = mybir.dt.float16
I32 = mybir.dt.int32
U16 = mybir.dt.uint16
ALU = mybir.AluOpType
ACT = mybir.ActivationFunctionType
AX = mybir.AxisListType.X

P = 128
BANK = 512
NO_EDGE_FACTOR = 1.0e29
MAX_FLOOR = -1.0e29
SLOPE = 0.2
LN_EPS = 1e-5
LN_TINY = 2.0 ** -60


class Counter:

    def __init__(self, handle):
        self.handle = handle
        self.value = 0

    def now(self):
        return self, self.value


class Queue:

    def __init__(self):
        self.steps = []
        self.reached = {}

    def after(self, *events):
        for event in events:
            if event is None:
                continue
            counter, value = event
            if self.reached.get(counter, 0) < value:
                self.reached[counter] = value
                self.steps.append(lambda e, c=counter, v=value: e.wait_ge(c.handle, v))
        return self

    def run(self, step, counter=None, by=1):
        if counter is None:
            self.steps.append(step)
            return None
        counter.value += by
        self.steps.append(lambda e: step(e).then_inc(counter.handle, by))
        return counter.now()

    def play(self, engine):
        for step in self.steps:
            step(engine)


def gnn_kernel(nc, x, src, dst, W0, attn_l, attn_r, Wres, W1, a_src1, a_dst1, b1, g1, be1, Wr1, br1,
               W2, a_src2, a_dst2, b2, g2, be2, Wr2, br2, out):
    N, D = x.shape
    E = src.shape[0]
    C0 = W0.shape[0]
    H0 = D // C0
    H1, C1 = a_src1.shape
    HC = H1 * C1
    NT = (N + P - 1) // P
    KT = D // P
    KH = HC // P
    EP = 125
    ET = E // EP
    assert EP * ET == E and ET % 2 == 0 and 2 * C0 == P and HC == 2 * BANK
    rows = [min(P, N - i * P) for i in range(NT)]
    pieces = [(c, min(BANK, N - c)) for c in range(0, N, BANK)]
    pair_units = [range(i, i + 2) for i in range(0, NT, 2)]
    RING = 8
    GT = 5
    GROUPS = ET // GT
    WIN = 64
    assert GROUPS * GT == ET and GROUPS % 2 == 0 and NT % 2 == 0 and (NT // 2) * WIN <= BANK

    x1_dram = nc.dram_tensor("x1_spill", (N, D), F32, kind="Internal").ap()
    base_dram = nc.dram_tensor("base_spill", (N, D), F32, kind="Internal").ap()

    with ExitStack() as ctx:
        def sbuf(name, free, dt=F32, parts=P):
            return ctx.enter_context(nc.sbuf_tensor(name, [parts] + list(free), dt))

        def counter(name):
            return Counter(ctx.enter_context(nc.semaphore(name)))

        LC = sbuf("LC", [NT, N])
        LC2 = LC[:, :, :].rearrange("p a b -> p (a b)")
        rowbuf = sbuf("rowbuf", [2, N])
        ident = sbuf("ident", [P])
        off_diag = sbuf("off_diag", [P])
        att = sbuf("att", [NT, 2 * H0])
        diag_count = sbuf("diag_count", [NT])
        diag_ln = sbuf("diag_ln", [NT])
        row_max = sbuf("row_max", [RING])
        stats = sbuf("stats", [2, 6 * H1])
        moments = sbuf("moments", [NT, 2])
        rstd = sbuf("rstd", [NT])
        minus_half = sbuf("minus_half", [1])
        tiny = sbuf("tiny", [1])
        ones_col = sbuf("ones_col", [1])
        recip = sbuf("recip", [8])
        psum = ctx.enter_context(nc.psum_tensor("psum", [P, 8, BANK], F32))
        regions = ctx.enter_context(ExitStack())
        region_at = {}

        def region(name, words):
            words = (words + 7) // 8 * 8
            region_at[name] = sum(region_words)
            region_words.append(words)
            return regions.enter_context(nc.sbuf_tensor(name, [P, words], F32))

        region_words = []
        colbuf = region("colbuf", 3 * BANK)
        R1 = region("R1", RING * N + NT * 2 * H0)
        R2 = region("R2", NT * HC + 2 * NT)
        R3 = region("R3", 2 * NT * D)

        def overlay(stack, *places):
            made, at = [], 0
            for n, (name, reg, start, shape) in enumerate(places):
                start += region_at[reg]
                assert start % 8 == 0 and start >= at
                if start > at:
                    stack.enter_context(nc.sbuf_tensor(f"{name}_before", [P, start - at], F32))
                words = (shape[0] * shape[1] + 7) // 8 * 8
                t = stack.enter_context(nc.sbuf_tensor(name, [P, words], F32R))
                made.append(t[:, 0:shape[0] * shape[1]].rearrange("p (a b) -> p a b", a=shape[0]))
                at = start + words
            return made

        banks = [psum[:, b, :] for b in range(8)]
        turn_banks, misc_banks, acc_banks = banks[0:2], banks[2:4], banks[4:8]

        def view(region, start, shape, dt=F32, parts=P):
            n = 1
            for s in shape:
                n *= s
            words = n if dt in (F32, F32R, I32) else n // 2
            ap = region[0:parts, start:start + words]
            if dt != F32:
                ap = ap.bitcast(dt)
            if len(shape) == 2:
                ap = ap.rearrange("p (a b) -> p a b", a=shape[0])
            if len(shape) == 3:
                ap = ap.rearrange("p (a b c) -> p a b c", a=shape[0], b=shape[1])
            return ap

        CT = view(R1, 0, [NT, N], U16)
        turned = [view(R1, NT * N // 2 + b * NT * P, [NT, P]) for b in range(2)]
        assert NT * N // 2 + 2 * NT * P <= R1.shape[1]
        edge_at = [0]

        def edge_view(shape, dt=F32, parts=P):
            ap = view(LC2, edge_at[0], shape, dt, parts)
            n = 1
            for size in shape:
                n *= size
            edge_at[0] += n if dt in (F32, I32) else (n + 1) // 2
            assert edge_at[0] <= NT * N
            return ap

        HOT = GT
        edge_rows = [(0, P), (P, ET - P)]
        iota_h = edge_view([N], F16)
        hot_full = [edge_view([N], BF16, EP) for _ in range(HOT)]
        hot_part = [edge_view([2 * P], BF16, EP) for _ in range(2)]
        hot_win = [edge_view([GT, WIN], BF16, EP) for _ in range(2)]
        zeros = edge_view([BANK], BF16, EP)
        src_f, dst_f, dst_rel = (edge_view([ET], F32, EP) for _ in range(3))
        base_all = edge_view([GROUPS], F32, EP)
        base_i = edge_view([GROUPS + 1], I32, 1)
        widest = edge_view([1], F32, 1)
        group_ends = edge_view([2], F32, GROUPS)
        iota_i = edge_view([N], I32)
        edges_i = [edge_view([EP], I32) for _ in range(4)]
        edges_f = [edge_view([EP]) for _ in range(4)]
        groups_i = edge_view([GT * EP], I32, GROUPS)
        groups_f = edge_view([GT * EP], F32, GROUPS)
        x_in = view(R2, 0, [NT, D])
        xT = view(R3, 0, [KT, N])
        ft = view(R2, 0, [NT, H0, C0])
        acc0 = view(R3, NT * D, [NT, D])
        W0_twice = view(R2, NT * D, [2, C0], F32, C0)
        Wres_twice = view(R2, NT * D + P, [2, C0], F32, C0)
        attn_in = view(R2, NT * D + 2 * P, [C0], F32, 2 * H0)
        attnT = view(R2, NT * D + 3 * P, [2 * H0], F32, C0)
        ring = view(R1, 0, [RING, N])
        COLS0 = 4
        cols0 = view(R3, 0, [COLS0, BANK])
        col_sum = view(R3, COLS0 * BANK, [2, BANK])
        aggT = view(R3, (COLS0 + 2) * BANK, [2, 2 * P])
        at0 = (COLS0 + 3) * BANK
        att_slope0 = view(R3, at0, [NT, 2 * H0])
        junk0 = view(R3, at0 + NT * 2 * H0, [N], BF16)
        more_rows = view(R3, at0 + NT * 2 * H0 + N // 2 + 1, [2, N])
        assert at0 + NT * 2 * H0 + N // 2 + 1 + 2 * N <= NT * D
        X0 = 3
        x0 = view(R2, NT * D, [X0, D])
        assert (NT + X0) * D <= R2.shape[1]

        q = {n: Queue() for n in ("sync", "pe", "act", "dve", "pool")}
        sync, pe, act, dve, pool = (q[n] for n in ("sync", "pe", "act", "dve", "pool"))

        def load(name, dst_ap, src_ap, *waits):
            c = counter("dma_" + name)
            sync.after(*waits)
            return sync.run(lambda e: e.dma_start(dst_ap, src_ap), c, 16)

        def rows_in(name, tile_ap, dram, *waits):
            full = (NT - 1) * P
            a = load(name + "_full", tile_ap[:, 0:NT - 1, :],
                     dram[0:full, :].rearrange("(t p) d -> p t d", p=P), *waits)
            b = load(name + "_last", tile_ap[0:rows[-1], NT - 1, :], dram[full:N, :])
            return a, b

        def spread(vec, parts=P):
            return vec.partition_broadcast(parts)

        ev_edges = []
        for k, ids in enumerate((dst, src)):
            for r, (t0, n) in enumerate(edge_rows):
                ev_edges.append(load(f"edges_{k}_{r}", edges_i[2 * k + r][0:n, :],
                                     ids[t0 * EP:(t0 + n) * EP].rearrange("(t p) -> t p", p=EP)))
        ev_groups = load("dst_groups", groups_i, dst.rearrange("(g e) -> g e", g=GROUPS))
        ev_w = [load("w0a", W0_twice[:, 0, :], W0), load("w0b", W0_twice[:, 1, :], W0),
                load("wra", Wres_twice[:, 0, :], Wres), load("wrb", Wres_twice[:, 1, :], Wres),
                load("al", attn_in[0:H0, :], attn_l[0]), load("ar", attn_in[H0:2 * H0, :], attn_r[0])]
        ev_x = rows_in("x", x_in, x)

        c_const = counter("const")
        pool.run(lambda e: e.iota(iota_i, [[1, N]], base=0, channel_multiplier=0), c_const)
        pool.run(lambda e: e.memset(ident[:, :], 0.0), c_const)
        pool.run(lambda e: e.memset(off_diag[:, :], 1.0), c_const)
        ev = pool.run(lambda e: e.memset(zeros, 0.0), c_const)
        pool.after(ev)
        pool.run(lambda e: e.affine_select(out=ident[:, :], in_=ident[:, :], compare_op=ALU.not_equal, fill=1.0,
                                           base=0, pattern=[[-1, P]], channel_multiplier=1), c_const)
        pool.run(lambda e: e.affine_select(out=off_diag[:, :], in_=off_diag[:, :], compare_op=ALU.not_equal,
                                           fill=0.0, base=0, pattern=[[-1, P]], channel_multiplier=1), c_const)
        pool.run(lambda e: e.memset(minus_half[:, :], -0.5), c_const)
        pool.run(lambda e: e.memset(ones_col[:, :], 1.0), c_const)
        pool.run(lambda e: e.memset(att[:, :, :], 0.0), c_const)
        pool.run(lambda e: e.memset(row_max[:, :], 0.0), c_const)
        ev_const = pool.run(lambda e: e.memset(tiny[:, :], LN_TINY), c_const)
        ev_CT0 = pool.run(lambda e: e.memset(R1[:, 0:NT * N // 2], 0.0), counter("counts_zero"))

        c_dve = counter("dve_done")
        c_act = counter("act_done")
        c_pe = counter("pe_done")
        dve.after(ev_const, *ev_edges, ev_groups)
        dve.run(lambda e: e.tensor_copy(groups_f, groups_i), c_dve)
        for k in range(4):
            n = edge_rows[k % 2][1]
            ev = dve.run(lambda e, k=k, n=n: e.tensor_copy(edges_f[k][0:n, :], edges_i[k][0:n, :]), c_dve)
        ev_edges_f = ev
        dve.after(ev)
        dve.run(lambda e: e.tensor_copy(iota_h, iota_i), c_dve)
        dve.run(lambda e: e.tensor_reduce(group_ends[:, 0:1], groups_f, AX, ALU.min), c_dve)
        ev = dve.run(lambda e: e.tensor_reduce(group_ends[:, 1:2], groups_f, AX, ALU.max), c_dve)
        dve.after(ev)
        ev = dve.run(lambda e: e.tensor_scalar(group_ends[:, 0:1], group_ends[:, 0:1], float(N - WIN), None, ALU.min),
                     c_dve)
        dve.after(ev)
        ev_ends = dve.run(lambda e: e.tensor_tensor(group_ends[:, 1:2], group_ends[:, 1:2], group_ends[:, 0:1],
                                                    ALU.subtract), c_dve)
        pe.after(ev_const, ev_edges_f)
        for k in range(2):
            for r, (t0, n) in enumerate(edge_rows):
                pe.run(lambda e, k=k, r=r, t0=t0, n=n: e.transpose(
                    banks[k][0:EP, t0:t0 + n], edges_f[2 * k + r][0:n, :], ident[0:n, 0:n]))
        pe.after(ev_ends)
        pe.run(lambda e: e.transpose(banks[2][0:1, 0:GROUPS], group_ends[:, 0:1], ident[0:GROUPS, 0:GROUPS]))
        pe.run(lambda e: e.transpose(banks[2][0:1, P:P + GROUPS], group_ends[:, 1:2], ident[0:GROUPS, 0:GROUPS]))
        ev = pe.run(lambda e: e.matmul(banks[4][0:EP, 0:GROUPS], group_ends[:, 0:1].to_broadcast([GROUPS, EP]),
                                       ident[0:GROUPS, 0:GROUPS], start=True, stop=True), c_pe)
        dve.after(ev)
        dve.run(lambda e: e.tensor_copy(base_i[:, 0:GROUPS], banks[2][0:1, 0:GROUPS]), c_dve)
        ev = dve.run(lambda e: e.tensor_reduce(widest, banks[2][0:1, P:P + GROUPS], AX, ALU.max), c_dve)
        dve.after(ev)
        ev_span = dve.run(lambda e: e.tensor_copy(base_i[:, GROUPS:GROUPS + 1], widest), c_dve)
        dve.run(lambda e: e.tensor_copy(dst_f, banks[0][0:EP, 0:ET]), c_dve)
        dve.run(lambda e: e.tensor_copy(src_f, banks[1][0:EP, 0:ET]), c_dve)
        ev = dve.run(lambda e: e.tensor_copy(base_all, banks[4][0:EP, 0:GROUPS]), c_dve)
        dve.after(ev)
        ev_rel = dve.run(lambda e: e.tensor_tensor(
            dst_rel.rearrange("p (g t) -> p g t", t=GT), dst_f.rearrange("p (g t) -> p g t", t=GT),
            base_all.unsqueeze(2).to_broadcast([EP, GROUPS, GT]), ALU.subtract), c_dve)

        c_win_hot, c_win_free = counter("win_hot_ready"), counter("win_hot_free")
        c_win_dst = counter("win_dst_ready")
        c_win_sum, c_win_added = counter("win_sum_ready"), counter("win_sum_added")
        c_all_hot, c_all_free = counter("all_hot_ready"), counter("all_hot_free")
        c_all_sum, c_all_kept = counter("all_sum_ready"), counter("all_sum_kept")
        c_counted = counter("edges_counted")
        all_sum = [[banks[0], banks[1], banks[2]], [banks[4], banks[5], banks[6]]]
        span = {}

        def load_span(e):
            e.wait_ge(c_dve.handle, ev_span[1])
            span[e.engine] = e.value_load(base_i[0:1, GROUPS:GROUPS + 1], min_val=0, max_val=N)

        def windows_dve(e):
            def window(g, half):
                e.tensor_tensor(hot_win[half], iota_h[0:EP, 0:WIN].unsqueeze(1).to_broadcast([EP, GT, WIN]),
                                dst_rel[:, bass.ds(g * GT, GT)].unsqueeze(2).to_broadcast([EP, GT, WIN]),
                                ALU.is_equal).then_inc(c_win_dst.handle, 1)

            def tile(t, j, again):
                if again:
                    e.wait_ge(c_win_free.handle, t + (1 - HOT))
                e.tensor_scalar(hot_full[j], iota_h[0:EP, :], src_f[:, bass.ds(t, 1)], None,
                                ALU.is_equal).then_inc(c_win_hot.handle, 1)

            def add(g, half):
                e.wait_ge(c_win_sum.handle, g + 1)
                base = e.value_load(base_i[0:1, bass.ds(g, 1)], min_val=0, max_val=N - WIN)
                window = CT[:, :, bass.ds(base, WIN)].rearrange("p (b i) w -> p b i w", b=2)
                e.wait_ge(c_win_added.handle, g)
                e.tensor_tensor(window, window, psum_window(half), ALU.add).then_inc(c_win_added.handle, 1)

            def group(g, half):
                window(g, half)
                for j in range(GT):
                    tile(g * GT + j, j, True)
                    if j == GT // 2:
                        add(g + (-1), 1 - half)

            window(0, 0)
            for j in range(GT):
                tile(j, j, False)
            group(1, 1)
            with e.Fori(1, GROUPS // 2) as r:
                for half in range(2):
                    group(r * 2 + half, half)
            add(GROUPS - 1, 1)

        def psum_window(half):
            return psum[:, 4 * half:4 * half + 2, 0:(NT // 2) * WIN].rearrange("p b (i w) -> p b i w", w=WIN)

        def all_dve(e):
            for g in range(NT // 2):
                with e.Fori(0, ET // 2) as r:
                    for buf in range(2):
                        e.wait_ge(c_all_free.handle, r * 2 + (g * ET + buf + 1))
                        t = r * 2 + buf
                        e.tensor_scalar(hot_full[buf], iota_h[0:EP, :], dst_f[:, bass.ds(t, 1)], None, ALU.is_equal)
                        e.tensor_scalar(hot_part[buf], iota_h[0:EP, 0:2 * P], src_f[:, bass.ds(t, 1)],
                                        None, ALU.is_equal).then_inc(c_all_hot.handle, 1)
                e.wait_ge(c_all_sum.handle, g + 1)
                for a in range(2):
                    k = 2 * g + a
                    for (c, w), bank in zip(pieces, all_sum[a]):
                        last = e.tensor_copy(CT[0:rows[k], k, c:c + w], bank[0:rows[k], 0:w])
                last.then_inc(c_all_kept.handle, 1)
                e.wait_ge(c_all_hot.handle, (g + 1) * ET)
                e.tensor_scalar(src_f, src_f, float(-2 * P), None, ALU.add).then_inc(c_all_kept.handle, 1)
                e.wait_ge(c_all_kept.handle, 2 * g + 2)

        def dve_counts(e):
            load_span(e)
            with e.If(span[e.engine] < WIN):
                windows_dve(e)
            with e.Else():
                all_dve(e)

        dve.after(ev_rel, ev_CT0)
        dve.steps.append(dve_counts)
        dve.steps.append(lambda e: e.drain().then_inc(c_counted.handle, 1))
        c_counted.value = 1
        ev_counted = c_counted.now()

        def windows_pe(e, g):
            b = g % 2
            halves_ = [psum[:, 4 * b + k, 0:(NT // 2) * WIN] for k in range(2)]
            if g >= 2:
                e.wait_ge(c_win_added.handle, g - 1)
            for half in halves_:
                e.matmul(half, zeros[:, 0:P], zeros[:, 0:(NT // 2) * WIN], start=True, stop=False)
            e.wait_ge(c_win_dst.handle, g + 1)
            for j in range(GT):
                t = g * GT + j
                e.wait_ge(c_win_hot.handle, t + 1)
                for i in range(NT):
                    at = (i % (NT // 2)) * WIN
                    last = e.matmul(halves_[i // (NT // 2)][0:rows[i], at:at + WIN],
                                    hot_full[j][:, i * P:i * P + rows[i]], hot_win[b][:, j, :],
                                    start=False, stop=False, skip_group_check=True)
                last.then_inc(c_win_free.handle, 1)
            for half in halves_:
                last = e.matmul(half, zeros[:, 0:P], zeros[:, 0:(NT // 2) * WIN], start=False, stop=True)
            last.then_inc(c_win_sum.handle, 1)

        def all_pe(e):
            def product(buf, g, start, stop):
                last = None
                for a in range(2):
                    k = 2 * g + a
                    for (c, w), bank in zip(pieces, all_sum[a]):
                        if buf is None:
                            last = e.matmul(bank[0:rows[k], 0:w], zeros[:, 0:rows[k]], zeros[:, 0:w],
                                            start=start, stop=stop)
                        else:
                            last = e.matmul(bank[0:rows[k], 0:w], hot_part[buf][:, a * P:a * P + rows[k]],
                                            hot_full[buf][:, c:c + w], start=False, stop=False)
                return last

            for g in range(NT // 2):
                if g:
                    e.wait_ge(c_all_kept.handle, 2 * g)
                product(None, g, True, False)
                with e.Fori(0, ET // 2) as r:
                    for buf in range(2):
                        e.wait_ge(c_all_hot.handle, r * 2 + (g * ET + buf + 1))
                        product(buf, g, False, False).then_inc(c_all_free.handle, 1)
                product(None, g, False, True).then_inc(c_all_sum.handle, 1)

        def pe_begin(e):
            load_span(e)
            e.sem_inc(c_all_free.handle, 2)

        def pe_segment(e, n):
            with e.If(span[e.engine] < WIN):
                windows_pe(e, 2 * n)
                windows_pe(e, 2 * n + 1)
            if n == GROUPS // 2 - 1:
                with e.Else():
                    all_pe(e)

        pe.after(ev_rel)
        pe.steps.append(pe_begin)
        segments = [0]

        def count_segment():
            n = segments[0]
            if n < GROUPS // 2:
                segments[0] += 1
                pe.steps.append(lambda e: pe_segment(e, n))

        for _ in range(3):
            count_segment()

        side_free = {3: None, 7: None}
        side = [0]

        def side_bank():
            side[0] ^= 1
            return (3, 7)[side[0]]

        rhs = view(rowbuf[:, :, :].rearrange("p a b -> p (a b)"), 0, [KT, 2 * P + 4])
        pe.after(ev_const, *ev_w)
        b_w = side_bank()
        pe.run(lambda e: e.transpose(banks[b_w][0:C0, 0:2 * H0], attn_in, ident[0:2 * H0, 0:2 * H0]))
        pe.run(lambda e: e.transpose(banks[b_w][:, P:P + C0], W0_twice.rearrange("p a b -> p (a b)"),
                                     ident[0:C0, 0:C0]))
        ev = pe.run(lambda e: e.transpose(banks[b_w][:, 2 * P:2 * P + C0], Wres_twice.rearrange("p a b -> p (a b)"),
                                          ident[0:C0, 0:C0]), c_pe)
        c_rhs0 = counter("rhs0_zero")
        ev_zero = pool.run(lambda e: e.memset(rhs[:, :, :], 0.0), c_rhs0)
        act.after(ev, ev_zero)
        ev_at = act.run(lambda e: e.copy(attnT, banks[b_w][0:C0, 0:2 * H0]), c_act)
        for k in range(KT):
            for half in range(2):
                ps = slice(half * C0, half * C0 + C0)
                act.run(lambda e, k=k, ps=ps: e.copy(rhs[ps, k, ps.start:ps.stop], banks[b_w][ps, P:P + C0]))
                last = act.run(lambda e, k=k, ps=ps: e.copy(rhs[ps, k, P + ps.start:P + ps.stop],
                                                            banks[b_w][ps, 2 * P:2 * P + C0]), c_act)
        side_free[b_w] = last
        b2_ = side_bank()
        pe.after(ev_at)
        ev = pe.run(lambda e: e.matmul(banks[b2_][:, 0:2 * H0], W0_twice.rearrange("p a b -> p (a b)"), attnT,
                                       start=True, stop=True), c_pe)
        act.after(ev)
        for half in range(2):
            ps = slice(half * C0, half * C0 + C0)
            for side_ in range(2):
                ev_rhs = act.run(lambda e, half=half, ps=ps, s=side_: e.copy(
                    rhs[ps, :, 2 * P + 2 * s + half],
                    banks[b2_][ps, s * H0 + half:(s + 1) * H0:2]), c_act)
        side_free[b2_] = ev_rhs
        pe.after(*ev_x)
        for k in range(KT):
            for c, w in pieces:
                b = side_bank()
                if c == 0:
                    count_segment()
                pe.after(side_free[b])
                for i in range(c // P, (c + w + P - 1) // P):
                    ev = pe.run(lambda e, b=b, c=c, i=i, k=k: e.transpose(
                        banks[b][:, i * P - c:i * P - c + rows[i]], x_in[0:rows[i], i, k * P:(k + 1) * P],
                        ident[0:rows[i], 0:rows[i]]), c_pe)
                act.after(ev)
                ev_xT = side_free[b] = act.run(lambda e, b=b, c=c, w=w, k=k: e.copy(xT[:, k, c:c + w],
                                                                                    banks[b][:, 0:w]), c_act)
        pe.after(ev_xT, ev_rhs)
        for i in range(NT):
            m = rows[i]
            count_segment()
            for k in range(KT):
                b = side_bank()
                pe.after(side_free[b])
                ev = pe.run(lambda e, b=b, m=m, i=i, k=k: e.matmul(
                    banks[b][0:m, 0:2 * P + 4], xT[:, k, i * P:i * P + m], rhs[:, k, :], start=True, stop=True), c_pe)
                act.after(ev, ev_const)
                act.run(lambda e, b=b, m=m, i=i, k=k: e.copy(
                    ft[0:m, i, 2 * k:2 * k + 2, 0:C0],
                    banks[b][0:m, 0:P].rearrange("p (a b) -> p a b", a=2)))
                act.run(lambda e, b=b, m=m, i=i, k=k: e.copy(acc0[0:m, i, k * P:(k + 1) * P], banks[b][0:m, P:2 * P]))
                ev_ft = side_free[b] = act.run(lambda e, b=b, m=m, i=i, k=k: e.copy(
                    att[0:m, i, :].rearrange("p (s h) -> p s h", s=2)[:, :, 2 * k:2 * k + 2],
                    banks[b][0:m, 2 * P:2 * P + 4].rearrange("p (s h) -> p s h", s=2)), c_act)

        while segments[0] < GROUPS // 2:
            count_segment()

        c_turn_dve, c_turn_act = counter("counts_turned_dve"), counter("counts_turned_act")
        turned_free = [None, None]
        count_free = [ev_counted, ev_counted]
        ev_diag = None
        half_tiles = NT // 2

        def mask_tile(k, ev_ln):
            m = rows[k]
            dve.after(ev_ln)
            dve.run(lambda e: e.scalar_tensor_tensor(
                out=LC[0:m, k, :], in0=LC[0:m, k, :], scalar=NO_EDGE_FACTOR, in1=LC[0:m, k, :], op0=ALU.mult,
                op1=ALU.min), c_dve)
            dve.after(ev_diag)
            return dve.run(lambda e: e.tensor_tensor_reduce(
                colbuf[0:m, 0:m], CT[0:m, k, k * P:k * P + m], ident[0:m, 0:m], 1.0, 0.0, ALU.mult, ALU.add,
                diag_count[0:m, k:k + 1]), c_dve)

        def widen(k):
            m = rows[k]
            b = k % 2
            dve.after(turned_free[b])
            act.after(ev_counted, turned_free[b])
            ev_d = dve.run(lambda e: e.tensor_copy(
                turned[b][:, 0:half_tiles, 0:m], CT[:, 0:half_tiles, k * P:k * P + m]), c_turn_dve)
            for lo, hi, n in ((half_tiles, NT - 1, P), (NT - 1, NT, rows[-1])):
                ev_a = act.run(lambda e, lo=lo, hi=hi, n=n: e.copy(
                    turned[b][0:n, lo:hi, 0:m], CT[0:n, lo:hi, k * P:k * P + m]), c_turn_act)
            return ev_d, ev_a

        wide = widen(0)
        for k in range(NT):
            m = rows[k]
            b = k % 2
            pe.after(*wide, count_free[b])
            for i in range(NT):
                ev = pe.run(lambda e, b=b, i=i, m=m: e.transpose(
                    banks[4 * b + i // 4][0:m, (i % 4) * P:(i % 4) * P + rows[i]], turned[b][0:rows[i], i, 0:m],
                    ident[0:rows[i], 0:rows[i]]), c_pe)
            turned_free[b] = ev
            if k + 1 < NT:
                wide = widen(k + 1)
            if k:
                ev_diag = mask_tile(k - 1, count_free[1 - b])
            act.after(ev)
            count_free[b] = act.run(lambda e, b=b, k=k, m=m: e.activation(
                LC[0:m, k, :], psum[0:m, 4 * b:4 * b + 3, :].rearrange("p a b -> p (a b)")[:, 0:N], ACT.Ln,
                bias=tiny[0:m, :], scale=2.0), c_act)
        ev_diag = mask_tile(NT - 1, count_free[(NT - 1) % 2])
        ev_LC = ev_diag
        dve.after(ev_diag)

        ring_free = [None] * RING
        ring_at = [0]
        turn_at = [0]
        turn_free = [count_free[0]] * 2
        col_at = [0]
        acc_free = [count_free[1]] * 4
        misc_at = [0]
        misc_free = [count_free[0], count_free[1]]

        def row_of(col, row_ap, piece, free_evs):
            c, w = pieces[piece]
            b = misc_at[0] % 2
            misc_at[0] += 1
            pe.after(misc_free[b], *row_ready)
            for i in range(c // P, (c + w + P - 1) // P):
                m = rows[i]
                ev = pe.run(lambda e, i=i, m=m: e.transpose(
                    misc_banks[b][:, i * P - c:i * P - c + m], att[0:m, i, col:col + 1].to_broadcast([m, P]),
                    ident[0:m, 0:m]), c_pe)
            act.after(ev, *free_evs)
            misc_free[b] = act.run(lambda e: e.copy(row_ap[:, c:c + w], misc_banks[b][:, 0:w]), c_act)
            return misc_free[b]

        def edge_maximum(i, row_ap, row_ev, slot, junk):
            m = rows[i]
            dve.after(row_ev, junk_written[0])
            junk_written[0] = dve.run(lambda e: e.tensor_tensor_reduce(
                junk[0:m, :], row_ap[0:m, :], LC[0:m, i, :], 1.0, MAX_FLOOR, ALU.add, ALU.max,
                row_max[0:m, slot:slot + 1]), c_dve)

        def unit_maxima(tiles, slot, dst_col, net):
            n = len(tiles)
            t = row_max[:, slot:slot + net.together * n].rearrange("p (h t) -> p h t", t=n)

            def terms(ap):
                return ap[:, tiles[0]:tiles[-1] + 1, dst_col:dst_col + net.together].rearrange("p t h -> p h t")

            dve.after(junk_written[0])
            ev = dve.run(lambda e: e.tensor_tensor(t, t, terms(att), ALU.add), c_dve)
            dve.after(ev)
            ev = dve.run(lambda e: e.scalar_tensor_tensor(out=t, in0=t, scalar=SLOPE, in1=t, op0=ALU.mult,
                                                          op1=ALU.max), c_dve)
            dve.after(ev)
            return dve.run(lambda e: e.tensor_tensor(t, t, terms(net.att_slope), ALU.subtract), c_dve)

        def relu_row(i, row_ap, row_ev, dst_col, slot, net):
            m = rows[i]
            act.after(row_ev, ring_free[slot])
            return act.run(lambda e: e.activation(ring[0:m, slot, :], row_ap[0:m, :], ACT.Relu,
                                                  bias=net.att_rest[0:m, i, dst_col:dst_col + 1],
                                                  scale=1.0 - SLOPE), c_act)

        def score_row(i, slot, relu_ev, max_slot, max_ev):
            m = rows[i]
            dve.after(relu_ev, max_ev)
            return dve.run(lambda e: e.scalar_tensor_tensor(
                out=ring[0:m, slot, :], in0=ring[0:m, slot, :], scalar=row_max[0:m, max_slot:max_slot + 1],
                in1=LC[0:m, i, :], op0=ALU.subtract, op1=ALU.add), c_dve)

        def columns(s, unit_rows, slots, col_aps, free_evs, bias_of):
            m = rows[s]
            b = turn_at[0] % 2
            turn_at[0] += 1
            pe.after(turn_free[b])
            w = 0
            stretch = {}
            for (slot, ev_s), (h, i) in zip(slots, unit_rows):
                pe.after(ev_s)
                n = rows[i]
                ev = pe.run(lambda e, slot=slot, n=n, w=w: e.transpose(
                    turn_banks[b][0:m, w:w + n], ring[0:n, slot, s * P:s * P + m], ident[0:n, 0:n]), c_pe)
                stretch[h] = stretch.get(h, (w, w))[0], w + n
                w += n
            if s == NT - 1:
                for slot, _ in slots:
                    ring_free[slot] = ev
            act.after(ev, *free_evs)
            for col_ap in col_aps:
                for h, (lo, hi) in stretch.items():
                    turn_free[b] = act.run(lambda e, h=h, lo=lo, hi=hi, col_ap=col_ap: e.activation(
                        col_ap[0:m, lo:hi], turn_banks[b][0:m, lo:hi], ACT.Exp, bias=bias_of(h)), c_act)
            return turn_free[b], stretch

        class Net:

            def __init__(self, together, units, att_slope, att_rest, src_col, dst_col, row_bufs, junk, ring_slots,
                         two_first=False, ahead=1):
                self.together, self.units = together, units
                self.att_slope, self.att_rest, self.src_col, self.dst_col = att_slope, att_rest, src_col, dst_col
                self.row_bufs, self.junk = row_bufs, junk
                self.ring_slots = ring_slots
                self.ahead = ahead
                self.two_first = two_first

            def scale_terms(self, *evs):
                dve.after(*evs)
                n = self.att_slope.shape[2]
                dve.run(lambda e: e.tensor_scalar(self.att_slope, att[:, :, 0:n], SLOPE, None, ALU.mult), c_dve)
                return dve.run(lambda e: e.tensor_scalar(self.att_rest, att[:, :, 0:n], 1.0 - SLOPE, None,
                                                         ALU.mult), c_dve)

        junk_written = [None]
        row_ready = []
        max_free = [None, None]

        def attention(net, n_heads, begin_head, column, use, finish):
            G, U = net.together, len(net.units)
            todo = [(g, u) for g in range(n_heads // G) for u in range(U)]
            made = {}
            row_evs = {}
            row_readers = {}
            begun = {}

            def row_buf(h):
                return net.row_bufs[h % len(net.row_bufs)]

            def make_row(h, piece):
                row_readers.setdefault(h, [])
                row_evs[h] = row_of(net.src_col(h), row_buf(h), piece, row_readers.get(h - len(net.row_bufs), []))

            def beside(old, s):
                g, u = old
                if (g + 1) * G >= n_heads:
                    return
                i = begun.get(g + 1, 0)
                if (u * NT + s) % 3 == 0 and i < NT:
                    begun[g + 1] = i + 1
                    begin_head(g + 1, i)
                k = u - (U - 1 - G)
                if 0 <= k < G and s in (1, 4, 7):
                    make_row((g + 1) * G + k, s // 3)

            def rows_of(unit):
                g, u = unit
                return [(h, i) for h in range(g * G, (g + 1) * G) for i in net.units[u]]

            for n in range(len(todo) + 1):
                new = todo[n] if n < len(todo) else None
                old = todo[n - 1] if n else None
                plan = {}
                if new:
                    g, u = new
                    if not old:
                        for i in range(NT):
                            begin_head(0, i)
                        for h in range(G):
                            for piece in range(len(pieces)):
                                make_row(h, piece)
                    made[new] = []
                    half = 4 * (n % 2)
                    state = {}

                    def maximum(j, h, i, half=half):
                        if j == 0:
                            dve.after(max_free[half // 4])
                        edge_maximum(i, row_buf(h), row_evs[h], half + j, net.junk)
                        row_readers[h].append(junk_written[0])

                    def all_maxima(g=g, u=u, half=half, state=state):
                        state["ev"] = unit_maxima(net.units[u], half, net.dst_col(g * G), net)

                    def relu(j, h, i, state=state):
                        slot = ring_at[0] % net.ring_slots
                        ring_at[0] += 1
                        state[j] = slot, relu_row(i, row_buf(h), row_evs[h], net.dst_col(h), slot, net)
                        row_readers[h].append(state[j][1])

                    def score(j, i, half=half, state=state, new=new):
                        slot, relu_ev = state[j]
                        made[new].append((slot, score_row(i, slot, relu_ev, half + j, state["ev"])))
                        max_free[half // 4] = made[new][-1][1]

                    new_rows = list(enumerate(rows_of(new)))
                    R = len(new_rows)
                    plan = {}
                    for j, (h, i) in new_rows:
                        plan.setdefault(j, []).append(lambda j=j, h=h, i=i: maximum(j, h, i))
                    plan[R - 1].append(all_maxima)
                    for j, (h, i) in new_rows:
                        plan.setdefault(8 // R * j - 0.5, []).append(lambda j=j, h=h, i=i: relu(j, h, i))
                        plan.setdefault(max(R + j, 8 // R * j + 1), []).append(lambda j=j, i=i: score(j, i))
                if not old:
                    for n_at, at in enumerate(sorted(plan)):
                        for step in plan[at]:
                            step()
                        if net.two_first and n_at < NT:
                            begin_head(1, n_at)
                            begun[1] = n_at + 1
                    for t in range(net.ahead):
                        column(new, t, rows_of(new), made[new])
                    continue
                for s in range(NT):
                    for at in (s - 0.5, s):
                        for step in plan.get(at, []):
                            step()
                    beside(old, s)
                    t = s + net.ahead
                    if t < NT:
                        column(old, t, rows_of(old), made[old])
                    elif new:
                        column(new, t - NT, rows_of(new), made[new])
                    use(old, s, net.units[old[1]])
                finish(old, net.units[old[1]])

        col_free0 = [()] * COLS0
        col_slot = {}
        agg_free = [None] * 2
        sum_free = [None] * 2
        sum_done = {}
        recip_read = [None]
        c_sum = counter("col_sums")
        for slot in range(RING):
            ring_free[slot] = turned_free[1]
        act.after(ev_LC)

        def unit_number0(unit):
            return unit[0] * len(pair_units) + unit[1]

        def column0(unit, s, unit_rows, slots):
            c = (unit_number0(unit) * NT + s) % COLS0
            col_slot[unit, s] = columns(s, unit_rows, slots, [cols0[:, c, :]], col_free0[c],
                                        lambda h: att_slope0[0:rows[s], s, h:h + 1])

        def use0(unit, s, tiles):
            g, u = unit
            if s in late0:
                for step in late0.pop(s):
                    step()
            c = (unit_number0(unit) * NT + s) % COLS0
            ev, stretch = col_slot[unit, s]
            b = unit_number0(unit) % 2
            m = rows[s]
            if s == 0:
                pe.after(acc_free[b])
            pe.after(ev)
            for h, (lo, hi) in stretch.items():
                k = (h % 2) * C0
                ev_pe = pe.run(lambda e, h=h, lo=lo, hi=hi, k=k: e.matmul(
                    acc_banks[b][k:k + C0, 0:hi - lo], ft[0:m, s, h, :], cols0[0:m, c, lo:hi],
                    start=(s == 0), stop=(s == NT - 1)), c_pe)
            col_free0[c] = (ev_pe,)
            if s == 0:
                return
            w = hi
            before = (c - 1) % COLS0
            pool.after(ev, sum_free[b] if s == 1 else sum_done[unit])
            first = cols0[:, before, :] if s == 1 else col_sum[:, b, :]
            sum_done[unit] = pool.run(lambda e: e.tensor_tensor(
                col_sum[0:m, b, 0:w], first[0:m, 0:w], cols0[0:m, c, 0:w], ALU.add), c_sum)
            col_free0[c] += (sum_done[unit],)
            if s == 1:
                col_free0[before] += (sum_done[unit],)

        late0 = {}

        def finish0(unit, tiles):
            b = unit_number0(unit) % 2
            w = sum(rows[i] for i in tiles)
            dve.after(c_pe.now(), agg_free[b])
            ev = dve.run(lambda e: e.tensor_copy(aggT[:, b, 0:w], acc_banks[b][:, 0:w]), c_dve)
            acc_free[b] = ev
            late0[3] = [lambda: normalise0(unit, b, tiles, ev)]
            if unit[0] == H0 // 2 - 1:
                for j, i in enumerate(tiles):
                    late0[4 + j] = [lambda i=i: first_sum(i)]
                    late0[6 + 2 * j] = [lambda i=i: first_norm(i)]
            if unit == (H0 // 2 - 1, len(pair_units) - 2):
                load_first_weights()

        def normalise0(unit, b, tiles, ev):
            g, u = unit
            ob = acc_banks[2 + b]
            pe.after(ev, sum_done[unit], acc_free[2 + b])
            w = sum(rows[i] for i in tiles)
            at = 0
            sums_at = 2 * P
            for j, i in enumerate(tiles):
                n = rows[i]
                agg_free[b] = pe.run(lambda e, j=j, n=n, at=at: e.transpose(
                    ob[0:n, j * P:(j + 1) * P], aggT[:, b, at:at + n], ident[:, :]), c_pe)
                for k in range(2):
                    sum_at = sums_at + 2 * j + k
                    ev = pe.run(lambda e, n=n, at=k * w + at, sum_at=sum_at: e.matmul(
                        ob[0:n, sum_at:sum_at + 1], col_sum[:, b, at:at + n], ones_col[:, :], start=True,
                        stop=True), c_pe)
                at += n
            sum_free[b] = ev
            dve.after(ev, recip_read[0])
            last = rows[tiles[-1]]
            groups = [(0, 4, P)] if last == P else [(0, 2, P), (2, 4, last)]
            for lo, hi, m in groups:
                ev = dve.run(lambda e, lo=lo, hi=hi, m=m: e.tensor_scalar(
                    recip[0:m, lo:hi], ob[0:m, sums_at + lo:sums_at + hi], 1e-16, None, ALU.max), c_dve)
            dve.after(ev)
            for lo, hi, m in groups:
                ev = dve.run(lambda e, lo=lo, hi=hi, m=m: e.reciprocal(recip[0:m, lo:hi], recip[0:m, lo:hi]), c_dve)
            dve.after(ev)
            for j, i in enumerate(tiles):
                for k in range(2):
                    n = rows[i]
                    dst_ap = acc0[0:n, i, (2 * g + k) * C0:(2 * g + k + 1) * C0]
                    ev = dve.run(lambda e, j=j, k=k, n=n, dst_ap=dst_ap: e.scalar_tensor_tensor(
                        out=dst_ap, in0=ob[0:n, j * P + k * C0:j * P + (k + 1) * C0],
                        scalar=recip[0:n, 2 * j + k:2 * j + k + 1], in1=dst_ap, op0=ALU.mult, op1=ALU.add), c_dve)
            acc_free[2 + b] = recip_read[0] = ev
            acc0_done[0] = ev

        c_pool_rstd = counter("rstd")
        ev_x0, x0_read, ev_x1, ev_spill = {}, {}, [], []
        stats_read = [None, None]

        def halves_of(ap):
            return [ap[:, 0:D // 2], ap[:, D // 2:D]]

        def norm_stats(i, parts, waits=(), power_now=True):
            m = rows[i]
            b = i % 2
            dve.after(*waits, stats_read[b])
            for n, part in enumerate(parts):
                ev = dve.run(lambda e, n=n, part=part: e.bn_stats(stats[0:m, b, 6 * n:6 * n + 6], part), c_dve)
            dve.after(ev)
            ev = stats_read[b] = dve.run(lambda e: e.bn_aggr(moments[0:m, i, :], stats[0:m, b, 0:6 * len(parts)]),
                                         c_dve)
            dve.after(ev)
            ev = dve.run(lambda e: e.tensor_scalar(rstd[0:m, i:i + 1], moments[0:m, i, 1:2], LN_EPS, None, ALU.add),
                         c_dve)
            return norm_power(i, ev) if power_now else ev

        def norm_power(i, ev):
            m = rows[i]
            pool.after(ev)
            return pool.run(lambda e: e.tensor_tensor(rstd[0:m, i:i + 1], rstd[0:m, i:i + 1], minus_half[0:m, :],
                                                      ALU.pow), c_pool_rstd)

        norm_ready = {}
        acc0_done = [None]

        def load_x0(i):
            if i < NT:
                ev_x0[i] = load(f"x0_{i}", x0[0:rows[i], i % X0, :], x[i * P:i * P + rows[i], :], x0_read.get(i - X0),
                                ev_rhs)

        def first_sum(i):
            m = rows[i]
            tile = acc0[0:m, i, :]
            dve.after(acc0_done[0], ev_x0[i])
            ev = x0_read[i] = dve.run(lambda e: e.scalar_tensor_tensor(
                out=tile, in0=tile, scalar=0.0, in1=x0[0:m, i % X0, :], op0=ALU.max, op1=ALU.add), c_dve)
            load_x0(i + X0)
            norm_ready[i] = norm_stats(i, halves_of(tile), [ev])

        def first_norm(i):
            m = rows[i]
            tile = acc0[0:m, i, :]
            dve.after(norm_ready[i])
            ev_x1.append(dve.run(lambda e: e.tensor_scalar(
                tile, tile, moments[0:m, i, 0:1], rstd[0:m, i:i + 1], ALU.subtract, ALU.mult), c_dve))
            ev_spill.append(load(f"x1_out_{i}", x1_dram[i * P:i * P + m, :], tile, ev_x1[-1]))

        W1_first = view(R1, 0, [KT, C1])
        a1_first = [view(R1, KT * C1 + s * C1, [C1]) for s in range(2)]
        w1_ev = {}

        def load_first_weights():
            free = [ring_free[s] for s in range(2)]
            w1_ev[0] = [load("w1_0", W1_first, W1[:, 0:C1].rearrange("(k p) c -> p k c", p=P), *free),
                        load("a1s_0", a1_first[0], spread(a_src1[0])),
                        load("a1d_0", a1_first[1], spread(a_dst1[0]))]

        def begin0(g, i):
            pass

        net0 = Net(2, pair_units, att_slope0, view(R1, RING * N, [NT, 2 * H0]), lambda h: h, lambda h: H0 + h,
                   [rowbuf[:, 0, :], rowbuf[:, 1, :], more_rows[:, 0, :], more_rows[:, 1, :]], junk0, RING)
        act.after(net0.scale_terms(ev_ft, ev_LC))
        row_ready.append(ev_ft)
        for i in range(X0):
            load_x0(i)
        attention(net0, H0, begin0, column0, use0, finish0)
        for step in late0.pop(3):
            step()
        ev_attn0_dve = c_dve.now()
        for s in sorted(late0):
            for step in late0[s]:
                step()
        ev_attn0_pe = c_pe.now()

        x1T = view(R3, 0, [KT, N])

        def transpose_rows(src_of, dst_ap, n_k, tile_evs, free_evs, shared):
            for c, w in pieces:
                for k in range(n_k):
                    b = turn_at[0] % 2
                    turn_at[0] += 1
                    pe.after(turn_free[b])
                    for i in range(c // P, (c + w + P - 1) // P):
                        pe.after(tile_evs[i])
                        ev = pe.run(lambda e, b=b, c=c, i=i, k=k: e.transpose(
                            turn_banks[b][:, i * P - c:i * P - c + rows[i]],
                            src_of(i, k), ident[0:rows[i], 0:rows[i]]), c_pe)
                    if b and shared:
                        dve.after(ev, *free_evs)
                        turn_free[b] = dve.run(lambda e, b=b, c=c, w=w, k=k: e.tensor_copy(
                            dst_ap[:, k, c:c + w], turn_banks[b][:, 0:w]), c_dve)
                    else:
                        act.after(ev, *free_evs)
                        turn_free[b] = act.run(lambda e, b=b, c=c, w=w, k=k: e.copy(
                            dst_ap[:, k, c:c + w], turn_banks[b][:, 0:w]), c_act)
            return list(turn_free)

        ev_x1T = transpose_rows(lambda i, k: acc0[0:rows[i], i, k * P:(k + 1) * P], x1T, KT, ev_x1,
                                [ev_attn0_pe, ev_attn0_dve], shared=False)

        act.run(lambda e: e.activation(diag_ln[:, 0:NT - 1], diag_count[:, 0:NT - 1], ACT.Ln, bias=2.0, scale=2.0))
        ev = act.run(lambda e: e.activation(diag_ln[0:rows[-1], NT - 1:NT], diag_count[0:rows[-1], NT - 1:NT],
                                            ACT.Ln, bias=2.0, scale=2.0), c_act)
        dve.after(ev)
        for i in range(NT):
            m = rows[i]
            block = LC[0:m, i, i * P:i * P + m]
            ev = dve.run(lambda e, m=m, b=block: e.tensor_tensor(b, b, off_diag[0:m, 0:m], ALU.mult), c_dve)
            dve.after(ev)
            ev_LC1 = dve.run(lambda e, m=m, i=i, b=block: e.scalar_tensor_tensor(
                out=b, in0=ident[0:m, 0:m], scalar=diag_ln[0:m, i:i + 1], in1=b, op0=ALU.mult, op1=ALU.add), c_dve)

        col_free = [None] * 3
        XL1 = C1 + 2
        XLW = NT * XL1 + 4
        base = NT * D
        W1h = view(R3, base + 2 * XLW, [KT, C1])
        h_buf = view(R2, 0, [H1, NT, C1])
        vec_at = base + 2 * XLW + KT * C1
        a1_b = [view(R3, vec_at + s * C1, [C1]) for s in range(2)]
        b1_b = view(R3, vec_at + 2 * C1, [C1])
        assert vec_at + 3 * C1 + NT * 2 * H1 <= 2 * NT * D and (H1 - 1) * NT * C1 + XLW <= R2.shape[1]
        assert XLW % 8 == 0 and H1 % 2 == 0
        RING1, W2N, COLS1 = 4, len(pair_units[0]) * P, 3
        junk1 = view(R1, RING1 * N, [N], BF16)
        exp1_at = RING1 * N + N // 2 + 7
        exp1 = view(R1, exp1_at, [2, W2N])
        lo_at = exp1_at + 2 * W2N
        assert lo_at % 8 == 0 and lo_at + XLW + HC <= RING * N
        regions.close()
        with ExitStack() as layer1:
            cols1_hi, cols1_lo, xl_lo_odd, xl_lo_even, xl_hi_even, xl_hi_odd = overlay(
                layer1, ("cols1_hi", "colbuf", 0, [COLS1, W2N]), ("cols1_lo", "colbuf", COLS1 * W2N, [COLS1, W2N]),
                ("xl_lo_odd", "R1", lo_at, [NT, XL1]), ("xl_lo_even", "R2", (H1 - 1) * NT * C1, [NT, XL1]),
                ("xl_hi_even", "R3", base, [NT, XL1]), ("xl_hi_odd", "R3", base + XLW, [NT, XL1]))
        xl_hi, xl_lo = [xl_hi_even, xl_hi_odd], [xl_lo_even, xl_lo_odd]
        ones_pairs = ones_col[:, :].unsqueeze(2).to_broadcast([P, NT, 2])
        act.after(*ev_spill, *ev_x1T)
        dve.after(*ev_spill, *ev_x1T)
        for b in range(2):
            act.run(lambda e, b=b: e.copy(xl_hi[b][:, :, C1:XL1], ones_pairs), c_act)
            dve.run(lambda e, b=b: e.tensor_tensor(xl_lo[b][:, :, C1:XL1], ones_pairs, ones_pairs, ALU.subtract),
                    c_dve)
        w1_free = [None]
        xl_free = [None] * H1
        xl_ready = {}
        vec_free = [None]
        b1_free = [None]
        ev_b1 = {}

        def begin1(h, i):
            if i == 0 and h:
                w1_ev[h] = [
                    load(f"w1_{h}", W1h, W1[:, h * C1:(h + 1) * C1].rearrange("(k p) c -> p k c", p=P),
                         *ev_spill, *ev_x1T, w1_free[0]),
                    load(f"a1s_{h}", a1_b[0], spread(a_src1[h]), vec_free[0]),
                    load(f"a1d_{h}", a1_b[1], spread(a_dst1[h]))]
            weights = W1h if h else W1_first
            a1 = a1_b if h else a1_first
            k = h % 2
            m = rows[i]
            b = misc_at[0] % 2
            misc_at[0] += 1
            pe.after(*ev_x1T, *w1_ev[h], misc_free[b])
            for kk in range(KT):
                ev = pe.run(lambda e, kk=kk: e.matmul(
                    misc_banks[b][0:m, 0:C1], x1T[:, kk, i * P:i * P + m], weights[:, kk, :],
                    start=(kk == 0), stop=(kk == KT - 1)), c_pe)
            before = xl_free[h - 2] if h >= 2 else None
            act.after(ev, before)
            ev_hi = act.run(lambda e: e.copy(xl_hi[k][0:m, i, 0:C1], misc_banks[b][0:m, 0:C1]), c_act)
            dve.after(ev_hi, before, *w1_ev[h])
            ev = dve.run(lambda e: e.tensor_tensor(xl_lo[k][0:m, i, 0:C1], misc_banks[b][0:m, 0:C1],
                                                   xl_hi[k][0:m, i, 0:C1].bitcast(F32), ALU.subtract), c_dve)
            xl_ready[h] = ev
            for s in range(2):
                dve.after(ev)
                ev = dve.run(lambda e, s=s: e.tensor_tensor_reduce(
                    misc_banks[b][0:m, C1:2 * C1], misc_banks[b][0:m, 0:C1], a1[s][0:m, :], 1.0, 0.0, ALU.mult,
                    ALU.add, att[0:m, i, 2 * h + s:2 * h + s + 1]), c_dve)
            misc_free[b] = ev
            if i < NT - 1:
                return
            if h:
                w1_free[0] = c_pe.now()
                vec_free[0] = ev
            dve.after(ev)
            for part, factor in ((net1.att_slope, SLOPE), (net1.att_rest, 1.0 - SLOPE)):
                ev = dve.run(lambda e, p=part, f=factor: e.tensor_scalar(
                    p[:, :, 2 * h:2 * h + 2], att[:, :, 2 * h:2 * h + 2], f, None, ALU.mult), c_dve)
            act.after(ev)
            row_ready[:] = [ev]

        exp1_free = [None, None]
        c_rest = counter("exp_rest")

        def column1(unit, s, unit_rows, slots):
            c = col_at[0] % COLS1
            b = col_at[0] % 2
            col_at[0] += 1
            m = rows[s]
            ev, stretch = columns(s, unit_rows, slots, [exp1[:, b, :], cols1_hi[:, c, :]],
                                  [exp1_free[b], col_free[c]],
                                  lambda h: net1.att_slope[0:m, s, 2 * h:2 * h + 1])
            w = max(hi for _, hi in stretch.values())
            pool.after(ev, col_free[c])
            ev_lo = exp1_free[b] = pool.run(lambda e: e.tensor_tensor(
                cols1_lo[0:m, c, 0:w], exp1[0:m, b, 0:w], cols1_hi[0:m, c, 0:w].bitcast(F32), ALU.subtract), c_rest)
            col_slot[unit, s] = c, ev, ev_lo

        def acc1(unit, j):
            return 2 * ((unit[0] * len(pair_units) + unit[1]) % 2) + j

        def use1(unit, s, tiles):
            h, u = unit
            c, *evs = col_slot[unit, s]
            if s == 5:
                h_stats()
            m = rows[s]
            at = 0
            pe.after(*evs, xl_ready[h])
            for j, i in enumerate(tiles):
                a = acc1(unit, j)
                if s == 0:
                    pe.after(acc_free[a])
                n = rows[i]
                for step, (col, xs) in enumerate(((cols1_hi, xl_hi), (cols1_hi, xl_lo), (cols1_lo, xl_hi))):
                    col_free[c] = pe.run(lambda e, a=a, n=n, at=at, step=step, col=col, xs=xs: e.matmul(
                        acc_banks[a][0:n, 0:XL1], col[0:m, c, at:at + n], xs[h % 2][0:m, s, :],
                        start=(s == 0 and step == 0), stop=(s == NT - 1 and step == 2)), c_pe)
                at += n
            if s == NT - 1:
                xl_free[h] = col_free[c]

        late1 = []

        def h_stats():
            for tiles in late1:
                for i in tiles:
                    h_norm[i] = norm_stats(i, [h_buf[0:rows[i], k, i, :] for k in range(H1)], [recip_read[0]],
                                           power_now=False)
            late1.clear()

        def finish1(unit, tiles):
            h, u = unit
            if u == 0:
                ev_b1[h] = load(f"b1_{h}", b1_b, spread(b1[h * C1:(h + 1) * C1]), b1_free[0])
            dve.after(c_pe.now(), ev_b1[h], recip_read[0])
            for j, i in enumerate(tiles):
                n = rows[i]
                sums = acc_banks[acc1(unit, j)][0:n, C1:C1 + 1]
                ev = dve.run(lambda e, j=j, n=n, sums=sums: e.tensor_scalar(recip[0:n, j:j + 1], sums, 1e-16, None,
                                                                            ALU.add), c_dve)
            dve.after(ev)
            for j, i in enumerate(tiles):
                n = rows[i]
                ev = dve.run(lambda e, j=j, n=n: e.reciprocal(recip[0:n, j:j + 1], recip[0:n, j:j + 1]), c_dve)
            dve.after(ev)
            for j, i in enumerate(tiles):
                n = rows[i]
                acc_free[acc1(unit, j)] = dve.run(lambda e, j=j, n=n, i=i: e.scalar_tensor_tensor(
                    out=h_buf[0:n, h, i, :], in0=acc_banks[acc1(unit, j)][0:n, 0:C1], scalar=recip[0:n, j:j + 1],
                    in1=b1_b[0:n, :], op0=ALU.mult, op1=ALU.add), c_dve)
            b1_free[0] = recip_read[0] = acc_free[acc1(unit, len(tiles) - 1)]
            if h == H1 - 1:
                late1.append(tiles)
            if unit == (H1 - 1, len(pair_units) - 2):
                load_residual_weights()

        ring_at[0] = 0
        slots_free = 2
        wr1_at = [0, HC, RING * N - HC]
        wr1_late_at = [slots_free * N + 4, slots_free * N + 4 + HC]
        WR1_EARLY = len(wr1_at) + 1
        Wr1_k = [view(R1, at, [HC]) for at in wr1_at] + [view(R3, base + 2 * XLW, [HC])]
        Wr1_k += [view(R1, at, [HC]) for at in wr1_late_at]
        br1_row = view(R3, base + 2 * XLW + HC, [HC])
        vecs1 = view(R3, base, [2, HC])
        ones_row = view(R3, base + 2 * HC, [P])
        assert len(Wr1_k) == KT and 2 * HC <= slots_free * N and wr1_late_at[-1] + HC <= RING1 * N
        assert 2 * HC + P <= XLW and 2 * HC <= KT * C1 + 2 * C1 and H1 * NT % RING1 == 0
        h_norm, ev_wr1, ev_v, ev_or = {}, [], [], []

        def load_residual_weights():
            free = [ring_free[s] for s in range(slots_free)] + [w1_free[0], vec_free[0]]
            for k in range(WR1_EARLY):
                ev_wr1.append(load(f"wr1_{k}", Wr1_k[k], Wr1[k * P:(k + 1) * P, :], *free))
            ev_v.extend([load("br1", br1_row, spread(br1)),
                         load("g1", vecs1[:, 0, :], spread(g1), xl_free[H1 - 2]),
                         load("be1", vecs1[:, 1, :], spread(be1))])
            pool.after(xl_free[H1 - 2])
            ev_or.append(pool.run(lambda e: e.memset(ones_row, 1.0), counter("ones_row")))

        dve.after(ev_LC1)
        net1 = Net(1, pair_units, view(R3, vec_at + 3 * C1, [NT, 2 * H1]), view(R1, RING * N, [NT, 2 * H1]),
                   lambda h: 2 * h, lambda h: 2 * h + 1, [rowbuf[:, 0, :], rowbuf[:, 1, :]], junk1, RING1,
                   two_first=True, ahead=2)
        attention(net1, H1, begin1, column1, use1, finish1)
        h_stats()
        for i in range(NT):
            h_norm[i] = norm_power(i, h_norm[i])
        ev_attn1 = c_dve.now()
        ev_attn1_pe = c_pe.now()

        ev_wr1 += [load(f"wr1_{k}", Wr1_k[k], Wr1[k * P:(k + 1) * P, :], ev_attn1, ev_attn1_pe)
                   for k in range(WR1_EARLY, KT)]
        W2_EARLY = 5
        w2_at = [RING1 * N + k * D for k in range(W2_EARLY)] + [k * D for k in range(KH - W2_EARLY)]
        W2_k = [view(R1, at, [D]) for at in w2_at]
        assert w2_at[W2_EARLY - 1] + D <= wr1_at[2]
        ev_w2 = [load(f"w2_{k}", W2_k[k], W2[k * P:(k + 1) * P, :], ev_attn1, ev_attn1_pe) for k in range(W2_EARLY)]
        ev_h1 = []
        for i in range(NT):
            m = rows[i]
            pair = (i % 2) * 2
            pe.after(ev_v[0], *ev_or, acc_free[pair], acc_free[pair + 1])
            for half in range(2):
                cols = slice(half * BANK, (half + 1) * BANK)
                for k in range(KT):
                    pe.after(ev_wr1[k])
                    pe.run(lambda e, k=k, m=m, i=i, cols=cols, b=pair + half: e.matmul(
                        acc_banks[b][0:m, :], x1T[:, k, i * P:i * P + m], Wr1_k[k][:, cols],
                        start=(k == 0), stop=False))
                ev = pe.run(lambda e, m=m, cols=cols, b=pair + half: e.matmul(
                    acc_banks[b][0:m, :], ones_row[0:1, 0:m], br1_row[0:1, cols], start=False, stop=True), c_pe)
            hi = h_buf[0:m, :, i, :]
            by_head = [vecs1[0:m, n, :].rearrange("p (h c) -> p h c", h=H1) for n in range(2)]
            dve.after(h_norm[i], *ev_v)
            e1 = dve.run(lambda e, m=m, i=i, hi=hi, by_head=by_head: e.scalar_tensor_tensor(
                out=hi, in0=hi, scalar=moments[0:m, i, 0:1], in1=by_head[0], op0=ALU.subtract, op1=ALU.mult),
                c_dve)
            dve.after(e1)
            e1 = dve.run(lambda e, m=m, i=i, hi=hi, by_head=by_head: e.scalar_tensor_tensor(
                out=hi, in0=hi, scalar=rstd[0:m, i:i + 1], in1=by_head[1], op0=ALU.mult, op1=ALU.add), c_dve)
            dve.after(e1, ev)
            for half in range(2):
                heads = slice(half * H1 // 2, (half + 1) * H1 // 2)
                e1 = dve.run(lambda e, m=m, hi=hi, heads=heads, b=pair + half: e.scalar_tensor_tensor(
                    out=hi[:, heads, :], in0=hi[:, heads, :], scalar=0.0,
                    in1=acc_banks[b][0:m, :].rearrange("p (h c) -> p h c", h=H1 // 2), op0=ALU.max,
                    op1=ALU.add), c_dve)
            acc_free[pair] = acc_free[pair + 1] = e1
            ev_h1.append(e1)
        ev_wr1_done = c_pe.now()

        h1T = view(R3, 0, [KH, N])
        tail = KH * N
        a2_b = [view(R3, tail + s * D, [D]) for s in range(2)]
        x1_back = [view(R3, tail + (2 + s) * D, [D]) for s in range(2)]
        junk2_at = 2 * NT * D - (N // 2 + 1 + 2 * NT)
        junk2 = view(R3, junk2_at, [N], BF16)
        att_slope2 = view(R3, junk2_at + N // 2 + 1, [NT, 2])
        assert tail + 5 * D <= junk2_at
        br2_row = rowbuf[:, 0, 0:D]
        ones2 = rowbuf[:, 0, D:D + P]
        XL2 = D + 2
        xl2 = view(R2, 0, [NT, XL2])
        vec2_at = NT * XL2
        RING2 = 4
        first_slot = RING - 2
        wr2_at = [(KH - W2_EARLY + k) * D for k in range(3)] + [k * D for k in range(KH - W2_EARLY)] + [w2_at[0]]
        Wr2_k = [view(R3, tail + 4 * D, [D])] + [view(R1, at, [D]) for at in wr2_at]
        WR2_EARLY = 4
        assert wr2_at[2] + D <= w2_at[0] and wr2_at[-1] + D <= first_slot * N and len(Wr2_k) == KH
        ev_w2 += [load(f"w2_{k}", W2_k[k], W2[k * P:(k + 1) * P, :], ev_wr1_done) for k in range(W2_EARLY, KH)]
        ev_a2 = [load("a2s", a2_b[0], spread(a_src2[0]), ev_h1[-1], ev_wr1_done),
                 load("a2d", a2_b[1], spread(a_dst2[0])), load("br2", br2_row, spread(br2))]
        ev_wr2 = [load(f"wr2_{k}", Wr2_k[k], Wr2[k * P:(k + 1) * P, :], ev_wr1_done, ev_h1[-1])
                  for k in range(WR2_EARLY)]
        pool.after(ev_h1[-1], ev_wr1_done)
        ev_or2 = pool.run(lambda e: e.memset(ones2, 1.0), counter("ones_row2"))
        ev_h1T = transpose_rows(lambda i, k: h_buf[0:rows[i], k * P // C1, i, k * P % C1:k * P % C1 + P], h1T, KH,
                                ev_h1, [ev_h1[-1]], shared=True)
        pool.after(*ev_h1T)
        ev_ones2 = pool.run(lambda e: e.memset(xl2[:, :, D:XL2], 1.0), counter("xl2_ones"))
        halves = [(0, BANK), (BANK, D - BANK)]
        ev_att2 = None
        for i in range(NT):
            m = rows[i]
            pair = (i % 2) * 2
            pe.after(*ev_h1T, acc_free[pair], acc_free[pair + 1])
            for half, (c, w) in enumerate(halves):
                for k in range(KH):
                    pe.after(ev_w2[k])
                    ev = pe.run(lambda e, k=k, m=m, i=i, c=c, w=w, b=pair + half: e.matmul(
                        acc_banks[b][0:m, 0:w], h1T[:, k, i * P:i * P + m], W2_k[k][:, c:c + w],
                        start=(k == 0), stop=(k == KH - 1)), c_pe)
            act.after(ev, ev_ones2)
            for half, (c, w) in enumerate(halves):
                ev = act.run(lambda e, m=m, i=i, c=c, w=w, b=pair + half: e.copy(
                    xl2[0:m, i, c:c + w], acc_banks[b][0:m, 0:w]), c_act)
            acc_free[pair] = acc_free[pair + 1] = ev
            dve.after(ev, *ev_a2)
            for s in range(2):
                dve.after(ev_att2)
                ev_att2 = dve.run(lambda e, i=i, m=m, s=s: e.tensor_tensor_reduce(
                    rowbuf[0:m, 1, 0:D], xl2[0:m, i, 0:D], a2_b[s][0:m, :], 1.0, 0.0, ALU.mult, ALU.add,
                    att[0:m, i, s:s + 1]), c_dve)
        ev_w2_done = c_pe.now()
        be2_row = view(R2, vec2_at + 2 * D, [D])
        dve.after(*ev_a2, load("be2", be2_row, spread(be2), *ev_h1T))
        ev_br2 = dve.run(lambda e: e.tensor_tensor(br2_row, br2_row, be2_row, ALU.add), c_dve)
        ev_wr2 += [load(f"wr2_{k}", Wr2_k[k], Wr2[k * P:(k + 1) * P, :], ev_w2_done) for k in range(WR2_EARLY, KH)]
        ev_base = []
        x1_back_free = [None, None]

        def base_stage():
            for i in range(NT):
                m = rows[i]
                pair = (i % 2) * 2
                s = i % 2
                ev_xb = load(f"x1b_{i}", x1_back[s][0:m, :], x1_dram[i * P:i * P + m, :], *ev_spill, x1_back_free[s],
                             ev_h1[-1])
                pe.after(ev_br2, ev_or2, acc_free[pair], acc_free[pair + 1])
                for half, (c, w) in enumerate(halves):
                    for k in range(KH):
                        pe.after(ev_wr2[k])
                        pe.run(lambda e, k=k, m=m, i=i, c=c, w=w, b=pair + half: e.matmul(
                            acc_banks[b][0:m, 0:w], h1T[:, k, i * P:i * P + m], Wr2_k[k][:, c:c + w],
                            start=(k == 0), stop=False))
                    ev = pe.run(lambda e, m=m, c=c, w=w, b=pair + half: e.matmul(
                        acc_banks[b][0:m, 0:w], ones2[0:1, 0:m], br2_row[0:1, c:c + w], start=False, stop=True), c_pe)
                dve.after(ev, ev_xb)
                for half, (c, w) in enumerate(halves):
                    ev = dve.run(lambda e, m=m, s=s, c=c, w=w, b=pair + half: e.tensor_tensor(
                        x1_back[s][0:m, c:c + w], acc_banks[b][0:m, 0:w], x1_back[s][0:m, c:c + w], ALU.add), c_dve)
                acc_free[pair] = acc_free[pair + 1] = ev
                x1_back_free[s] = load(f"base_{i}", base_dram[i * P:i * P + m, :], x1_back[s][0:m, :], ev)
                ev_base.append(x1_back_free[s])
            ev_wr2_done = c_pe.now()
            act.after(ev_wr2_done)
            for b in range(RING - RING2, first_slot):
                ring_free[b] = ev_wr2_done
            for i in range(BASE_TILES):
                load_base(i, ev_wr2_done)

        cols_at = (NT * XL2 + 7) // 8 * 8
        xl2_lo, xl2_hi, cols_hi, cols_lo = overlay(
            ctx, ("xl2_lo", "R2", 0, [NT, XL2]), ("xl2_hi", "R3", 0, [NT, XL2]),
            ("cols_hi", "R3", cols_at, [NT + 1, W2N]), ("cols_lo", "R3", cols_at + (NT + 1) * W2N, [NT + 1, W2N]))
        xl2_split = []
        assert cols_at + 2 * (NT + 1) * W2N <= junk2_at
        exp2 = rowbuf[:, 0, 0:2 * W2N].rearrange("p (a b) -> p a b", a=2)
        exp2_free = [None, None]
        BASE_TILES = (RING - RING2) * N // D - 2
        base_sb = view(R1, 0, [BASE_TILES, D])
        ev_bl, base_read = {}, {}

        def load_base(i, *waits):
            if i < NT:
                ev_bl[i] = load(f"base_in_{i}", base_sb[0:rows[i], i % BASE_TILES, :],
                                base_dram[i * P:i * P + rows[i], :], ev_base[i],
                                base_read.get(i - BASE_TILES), *waits)

        vecs2 = view(R2, vec2_at, [2, D])
        assert vec2_at + 3 * D <= NT * HC
        ev_v2 = [load(f"vec2_{n}", vecs2[:, n, :], spread(v), *ev_h1T) for n, v in enumerate((b2, g2))]
        for b in range(first_slot, RING):
            ring_free[b] = ev_w2_done
        ring_at[0] = RING2 - 2
        y_bufs = [view(colbuf, j * D, [D]) for j in range(2)]
        y_bufs += [view(R1, (BASE_TILES + j) * D, [D]) for j in range(2)]
        cols2_free = {}
        col2_at = [0]
        y_free = [col_free[2]] * 4
        c_out = []

        def split_features(i):
            m = rows[i]
            ev = act.run(lambda e: e.copy(xl2_hi[0:m, i, :], xl2[0:m, i, :]), c_act)
            dve.after(ev)
            xl2_split.append(dve.run(lambda e: e.tensor_tensor(
                xl2_lo[0:m, i, :], xl2[0:m, i, :], xl2_hi[0:m, i, :].bitcast(F32), ALU.subtract), c_dve))

        def rows2(u):
            tiles = pair_units[u]
            half = 4 * (u % 2)
            dve.after(max_free[half // 4])
            for j, i in enumerate(tiles):
                edge_maximum(i, rowbuf[:, 1, :], row2[-1], half + j, junk2)
            ev_max = unit_maxima(tiles, half, 1, net2)
            made2[u] = []
            relus = []
            for j, i in enumerate(tiles):
                slot = RING - RING2 + ring_at[0] % RING2
                ring_at[0] += 1
                relus.append((i, slot, relu_row(i, rowbuf[:, 1, :], row2[-1], 1, slot, net2)))
            for j, (i, slot, ev) in enumerate(relus):
                made2[u].append((slot, score_row(i, slot, ev, half + j, ev_max)))
            max_free[half // 4] = made2[u][-1][1]

        def column2(u, s):
            unit_rows, slots = [(0, i) for i in pair_units[u]], made2[u]
            c = col2_at[0] % (NT + 1)
            col2_at[0] += 1
            m = rows[s]
            b = s % 2
            free = [cols2_free[c]] if c in cols2_free else ev_base
            ev, stretch = columns(s, unit_rows, slots, [exp2[:, b, :], cols_hi[:, c, :]], [exp2_free[b], *free],
                                  lambda h: att_slope2[0:m, s, 0:1])
            w = stretch[0][1]
            pool.after(ev, *free)
            ev_lo = exp2_free[b] = pool.run(lambda e: e.tensor_tensor(
                cols_lo[0:m, c, 0:w], exp2[0:m, b, 0:w], cols_hi[0:m, c, 0:w].bitcast(F32), ALU.subtract), c_rest)
            col_ready[u, s] = c, ev, ev_lo

        col_ready = {}
        halves2 = [(0, BANK), (BANK, XL2 - BANK)]

        def product2(u, s, j, at):
            n, m = rows[pair_units[u][j]], rows[s]
            pair = 2 * j
            place, *evs = col_ready[u, s]
            pe.after(*evs, xl2_split[s])
            if s == 0:
                pe.after(acc_free[pair], acc_free[pair + 1])
            for step, (col, xs) in enumerate(((cols_hi, xl2_hi), (cols_hi, xl2_lo), (cols_lo, xl2_hi))):
                for half, (c, w) in enumerate(halves2):
                    ev = pe.run(lambda e, c=c, w=w, b=pair + half, col=col, xs=xs, step=step: e.matmul(
                        acc_banks[b][0:n, 0:w], col[0:m, place, at:at + n], xs[0:m, s, c:c + w],
                        start=(s == 0 and step == 0), stop=(s == NT - 1 and step == 2)), c_pe)
            cols2_free[place] = ev
            return ev

        def divide2(u, j, ev):
            i = pair_units[u][j]
            n = rows[i]
            pair = 2 * j
            k = 2 * (u % 2) + j
            y = y_bufs[k][0:n, :]
            dve.after(ev, y_free[k], *ev_v2)
            r = recip[0:n, j:j + 1]
            ev = dve.run(lambda e: e.tensor_scalar(
                r, acc_banks[pair + 1][0:n, D - BANK:D - BANK + 1], 1e-16, None, ALU.add), c_dve)
            dve.after(ev)
            ev = dve.run(lambda e: e.reciprocal(r, r), c_dve)
            dve.after(ev)
            for half, (c, w) in enumerate(halves):
                ev = dve.run(lambda e, c=c, w=w, b=pair + half: e.scalar_tensor_tensor(
                    out=y[:, c:c + w], in0=acc_banks[b][0:n, 0:w], scalar=r, in1=vecs2[0:n, 0, c:c + w],
                    op0=ALU.mult, op1=ALU.add), c_dve)
            acc_free[pair] = acc_free[pair + 1] = ev
            return i, n, y, norm_stats(i, halves_of(y), [ev]), k

        def finish2(ready):
            evs = []
            for i, n, y, ev, _ in ready:
                dve.after(ev)
                evs.append(dve.run(lambda e, n=n, i=i, y=y: e.scalar_tensor_tensor(
                    out=y, in0=y, scalar=moments[0:n, i, 0:1], in1=vecs2[0:n, 1, :], op0=ALU.subtract,
                    op1=ALU.mult), c_dve))
            for k, (i, n, y, _, place) in enumerate(ready):
                dve.after(evs[k], ev_bl[i])
                evs[k] = base_read[i] = dve.run(lambda e, n=n, i=i, y=y: e.scalar_tensor_tensor(
                    out=y, in0=y, scalar=rstd[0:n, i:i + 1], in1=base_sb[0:n, i % BASE_TILES, :], op0=ALU.mult,
                    op1=ALU.add), c_dve)
                load_base(i + BASE_TILES)
            for k, (i, n, y, _, place) in enumerate(ready):
                evs[k] = norm_stats(i, halves_of(y), [evs[k]])
            for k, (i, n, y, _, place) in enumerate(ready):
                dve.after(evs[k])
                ev = dve.run(lambda e, n=n, i=i, y=y: e.tensor_scalar(
                    y, y, moments[0:n, i, 0:1], rstd[0:n, i:i + 1], ALU.subtract, ALU.mult), c_dve)
                y_free[place] = load(f"out_{i}", out[i * P:i * P + n, :], y, ev)
                c_out.append(y_free[place])

        net2 = Net(1, pair_units, att_slope2, view(R1, RING * N, [NT, 2]), None, None, None, junk2, RING2)
        act.after(net2.scale_terms(ev_att2))
        row_ready[:] = [ev_att2]
        made2, units_n = {}, len(pair_units)
        row2 = [row_of(0, rowbuf[:, 1, :], piece, []) for piece in range(len(pieces))]
        rows2(0)
        base_stage()
        for s in range(NT):
            column2(0, s)
            split_features(s)
        rows2(1)
        for u in range(units_n):
            for s in range(NT):
                ev = product2(u, s, 0, 0)
            first_done = ev
            for s in range(NT):
                ev = product2(u, s, 1, rows[pair_units[u][0]])
                if u + 1 < units_n:
                    column2(u + 1, s)
            ready = [divide2(u, 0, first_done), divide2(u, 1, ev)]
            if u + 2 < units_n:
                rows2(u + 2)
            finish2(ready)
        sync.after(*c_out)

        block = ctx.enter_context(nc.Block())

        @block.sync
        def _(e):
            sync.play(e)

        @block.tensor
        def _(e):
            pe.play(e)

        @block.scalar
        def _(e):
            act.play(e)

        @block.vector
        def _(e):
            dve.play(e)

        @block.gpsimd
        def _(e):
            pool.play(e)


_INS = ['x', 'src', 'dst', 'L0_gnn_W', 'L0_gnn_attn_l', 'L0_gnn_attn_r', 'L0_gnn_W_res', 'L1_gnn_W1',
        'L1_gnn_a_src1', 'L1_gnn_a_dst1', 'L1_gnn_b1', 'L1_gnn_g1', 'L1_gnn_be1', 'L1_gnn_Wr1', 'L1_gnn_br1',
        'L1_gnn_W2', 'L1_gnn_a_src2', 'L1_gnn_a_dst2', 'L1_gnn_b2', 'L1_gnn_g2', 'L1_gnn_be2', 'L1_gnn_Wr2',
        'L1_gnn_br2']


def kernel(**inputs):
    import numpy as _np
    import concourse.bacc as _bacc
    from concourse import mybir as _mybir
    from concourse.bass_utils import run_bass_kernel_spmd as _run

    nc = _bacc.Bacc("TRN2", target_bir_lowering=False, num_devices=1)
    arrays, args = {}, []
    for name in _INS:
        a = _np.ascontiguousarray(inputs[name])
        arrays[f"in_{name}_dram"] = a
        args.append(nc.dram_tensor(f"in_{name}_dram", a.shape, _mybir.dt.from_np(a.dtype), kind="ExternalInput").ap())
    out = nc.dram_tensor("out_dram", inputs['x'].shape, _mybir.dt.float32, kind="ExternalOutput").ap()
    gnn_kernel(nc, *args, out)
    r = _run(nc, [arrays], core_ids=[0])
    return r.results[0]["out_dram"]
```
